# Optimizing a Trainium2 kernel written in Bass

```python
import numpy as np
import jax
import jax.numpy as jnp

def _softmax(x, axis=-1):
    return jax.nn.softmax(x, axis=axis)

def _gelu(x):
    return jax.nn.gelu(x, approximate=True)

def _silu(x):
    return jax.nn.silu(x)

def _sigmoid(x):
    return jax.nn.sigmoid(x)

def _layernorm(x, axis=-1, eps=1e-05):
    m = jnp.mean(x, axis=axis, keepdims=True)
    v = jnp.var(x, axis=axis, keepdims=True)
    return (x - m) / jnp.sqrt(v + eps)

def _scatter_add(tgt, idx, src, axis=0):
    return tgt.at[idx].add(src)

def _segment_sum(src, seg, n):
    return jax.ops.segment_sum(src, seg, n)
kernel_name = 'mk_hybrid_d1_jaxref_r4_0bd250'

def setup_inputs(seed: int=0):
    np.random.seed(seed)
    _w = jnp.asarray

    def _L0_attn_a_setup():
        import jax, jax.numpy as jnp
        import numpy as np
        H = 512
        NH = 16
        KD = H // 2
        VD = H // 2
        DK = KD // NH
        DV = VD // NH
        RLOW = 64
        GLOW = 64
        EPS = 1e-05
        B, T = (2, 256)
        key = jax.random.key(seed)
        ks = jax.random.split(key, 18)

        def rn(k, shape, scale=0.02):
            return (jax.random.normal(k, shape) * scale).astype(jnp.float32)
        return {'x': jax.random.normal(ks[0], (B, T, H), dtype=jnp.float32), 'mu_x': rn(ks[1], (H,), 0.5), 'Wx1': rn(ks[2], (H, 5 * RLOW)), 'Wx2': rn(ks[3], (H, 5, RLOW)), 'x_bias': rn(ks[4], (5, H)), 'Wr': rn(ks[5], (H, KD)), 'Wk': rn(ks[6], (H, KD)), 'Wv': rn(ks[7], (H, VD)), 'Ww_a': rn(ks[8], (H, GLOW)), 'Ww_b': rn(ks[9], (GLOW, KD)), 'bw': rn(ks[10], (KD,)), 'Wg_a': rn(ks[11], (H, GLOW)), 'Wg_b': rn(ks[12], (GLOW, VD)), 'bg': rn(ks[13], (VD,)), 'bonus': rn(ks[14], (NH, DK), 0.5), 'ln_w': jnp.ones((DV,), jnp.float32), 'ln_b': jnp.zeros((DV,), jnp.float32), 'Wo': rn(ks[15], (VD, H))}
    _L0_attn_a_in = _L0_attn_a_setup()

    def _L0_attn_b_setup():
        import jax, jax.numpy as jnp
        import numpy as np
        HIDDEN = 512
        HEAD_DIM = 64
        N_HEADS = HIDDEN // HEAD_DIM
        ROT_DIM = HEAD_DIM // 2
        THETA = 10000.0
        SCALE_BASE = 512.0
        EPS = 1e-05
        B, S = (1, 512)

        def _rotate_half(t):
            x1 = t[..., 0::2]
            x2 = t[..., 1::2]
            return jnp.stack([-x2, x1], axis=-1).reshape(t.shape)

        def _xpos_rotary(q, k, seqlen):
            dim = ROT_DIM
            inv_freq = 1.0 / THETA ** (jnp.arange(0, dim, 2, dtype=jnp.float32) / dim)
            t = jnp.arange(seqlen, dtype=jnp.float32)
            freqs = t[:, None] * inv_freq[None, :]
            freqs = jnp.repeat(freqs, 2, axis=-1)
            base_scale = (jnp.arange(0, dim, 2, dtype=jnp.float32) + 0.4 * dim) / (1.4 * dim)
            power = (t - seqlen // 2) / SCALE_BASE
            scale = base_scale[None, :] ** power[:, None]
            scale = jnp.concatenate([scale, scale], axis=-1)
            cos, sin = (jnp.cos(freqs), jnp.sin(freqs))

            def apply(x, sc):
                xr, xp = (x[..., :dim], x[..., dim:])
                xr = xr * cos * sc + _rotate_half(xr) * sin * sc
                return jnp.concatenate([xr, xp], axis=-1)
            return (apply(q, scale), apply(k, 1.0 / scale))

        def _msr_forward(x, wqkv, wg, wo, gn_weight, gn_bias):
            b, s, _ = x.shape
            qkv = x @ wqkv.T
            qkv = qkv.reshape(b, s, N_HEADS, 3 * HEAD_DIM).transpose(0, 2, 1, 3)
            q, k, v = jnp.split(qkv, 3, axis=-1)
            q, k = _xpos_rotary(q, k, s)
            gamma = 1.0 - 2.0 ** (-5.0 - jnp.arange(N_HEADS, dtype=jnp.float32))
            idx = jnp.arange(s)
            nm = idx[:, None] - idx[None, :]
            decay = jnp.where(nm >= 0, gamma[:, None, None] ** jnp.maximum(nm, 0).astype(jnp.float32), 0.0)
            scores = jnp.einsum('bhid,bhjd->bhij', q, k) * decay
            ret = jnp.einsum('bhij,bhjd->bhid', scores, v)
            mean = ret.mean(axis=(2, 3), keepdims=True)
            var = ret.var(axis=(2, 3), keepdims=True)
            ret = (ret - mean) / jnp.sqrt(var + EPS)
            ret = ret * gn_weight[None, :, None, None] + gn_bias[None, :, None, None]
            y = ret.transpose(0, 2, 1, 3).reshape(b, s, HIDDEN)
            g = x @ wg.T
            mish = g * jnp.tanh(jax.nn.softplus(g))
            return mish * y @ wo.T
        key = jax.random.key(seed)
        ks = jax.random.split(key, 4)
        std = HIDDEN ** (-0.5)
        x = jax.random.normal(ks[0], (B, S, HIDDEN), jnp.float32)
        wqkv = jax.random.normal(ks[1], (3 * HIDDEN, HIDDEN), jnp.float32) * std
        wg = jax.random.normal(ks[2], (HIDDEN, HIDDEN), jnp.float32) * std
        wo = jax.random.normal(ks[3], (HIDDEN, HIDDEN), jnp.float32) * std
        gn_weight = jnp.ones((N_HEADS,), jnp.float32)
        gn_bias = jnp.zeros((N_HEADS,), jnp.float32)
        return {'x': x, 'wqkv': wqkv, 'wg': wg, 'wo': wo, 'gn_weight': gn_weight, 'gn_bias': gn_bias}
    _L0_attn_b_in = _L0_attn_b_setup()

    def _L0_ffn_setup():
        import jax, jax.numpy as jnp
        import numpy as np
        LN_EPS = 1e-05
        Q_EPS = 1e-05

        def ternary_quantize(w):
            scale = jnp.mean(jnp.abs(w))
            return jnp.clip(jnp.round(w / (scale + Q_EPS)), -1.0, 1.0)

        def layernorm(x, gamma, beta):
            mu = jnp.mean(x, axis=-1, keepdims=True)
            var = jnp.mean(jnp.square(x - mu), axis=-1, keepdims=True)
            return (x - mu) * jax.lax.rsqrt(var + LN_EPS) * gamma + beta
        key = jax.random.key(seed)
        k_x, k_w = jax.random.split(key)
        B, S, D_IN, D_OUT = (4, 512, 512, 512)
        x = jax.random.normal(k_x, (B, S, D_IN), dtype=jnp.float32)
        std = np.sqrt(2.0 / D_OUT).astype(np.float32)
        weight = jax.random.normal(k_w, (D_OUT, D_IN), dtype=jnp.float32) * std
        bias = jnp.zeros((D_OUT,), dtype=jnp.float32)
        ln_gamma = jnp.ones((D_IN,), dtype=jnp.float32)
        ln_beta = jnp.zeros((D_IN,), dtype=jnp.float32)
        return {'x': x, 'weight': weight, 'bias': bias, 'ln_gamma': ln_gamma, 'ln_beta': ln_beta}
    _L0_ffn_in = _L0_ffn_setup()
    _d = {'L0_attn_a_x': _L0_attn_a_in['x'], 'L0_attn_a_mu_x': _L0_attn_a_in['mu_x'], 'L0_attn_a_Wx1': _L0_attn_a_in['Wx1'], 'L0_attn_a_Wx2': _L0_attn_a_in['Wx2'], 'L0_attn_a_x_bias': _L0_attn_a_in['x_bias'], 'L0_attn_a_Wr': _L0_attn_a_in['Wr'], 'L0_attn_a_Wk': _L0_attn_a_in['Wk'], 'L0_attn_a_Wv': _L0_attn_a_in['Wv'], 'L0_attn_a_Ww_a': _L0_attn_a_in['Ww_a'], 'L0_attn_a_Ww_b': _L0_attn_a_in['Ww_b'], 'L0_attn_a_bw': _L0_attn_a_in['bw'], 'L0_attn_a_Wg_a': _L0_attn_a_in['Wg_a'], 'L0_attn_a_Wg_b': _L0_attn_a_in['Wg_b'], 'L0_attn_a_bg': _L0_attn_a_in['bg'], 'L0_attn_a_bonus': _L0_attn_a_in['bonus'], 'L0_attn_a_ln_w': _L0_attn_a_in['ln_w'], 'L0_attn_a_ln_b': _L0_attn_a_in['ln_b'], 'L0_attn_a_Wo': _L0_attn_a_in['Wo'], 'L0_attn_b_wqkv': _L0_attn_b_in['wqkv'], 'L0_attn_b_wg': _L0_attn_b_in['wg'], 'L0_attn_b_wo': _L0_attn_b_in['wo'], 'L0_attn_b_gn_weight': _L0_attn_b_in['gn_weight'], 'L0_attn_b_gn_bias': _L0_attn_b_in['gn_bias'], 'L0_ffn_weight': _L0_ffn_in['weight'], 'L0_ffn_bias': _L0_ffn_in['bias'], 'L0_ffn_ln_gamma': _L0_ffn_in['ln_gamma'], 'L0_ffn_ln_beta': _L0_ffn_in['ln_beta']}
    _x0 = _d['L0_attn_a_x']
    _d['L0_attn_a_x'] = jax.random.normal(jax.random.fold_in(jax.random.key(seed), 1), (4, 512, 512), dtype=_x0.dtype)
    del _x0
    return _d

def reference(L0_attn_a_x, L0_attn_a_mu_x, L0_attn_a_Wx1, L0_attn_a_Wx2, L0_attn_a_x_bias, L0_attn_a_Wr, L0_attn_a_Wk, L0_attn_a_Wv, L0_attn_a_Ww_a, L0_attn_a_Ww_b, L0_attn_a_bw, L0_attn_a_Wg_a, L0_attn_a_Wg_b, L0_attn_a_bg, L0_attn_a_bonus, L0_attn_a_ln_w, L0_attn_a_ln_b, L0_attn_a_Wo, L0_attn_b_wqkv, L0_attn_b_wg, L0_attn_b_wo, L0_attn_b_gn_weight, L0_attn_b_gn_bias, L0_ffn_weight, L0_ffn_bias, L0_ffn_ln_gamma, L0_ffn_ln_beta):

    def _L0_attn_a_ref(x, mu_x, Wx1, Wx2, x_bias, Wr, Wk, Wv, Ww_a, Ww_b, bw, Wg_a, Wg_b, bg, bonus, ln_w, ln_b, Wo):
        import jax, jax.numpy as jnp
        import numpy as np
        H = 512
        NH = 16
        KD = H // 2
        VD = H // 2
        DK = KD // NH
        DV = VD // NH
        RLOW = 64
        GLOW = 64
        EPS = 1e-05
        B, T = (2, 256)
        b, t, _ = x.shape
        shifted = jnp.pad(x, ((0, 0), (1, 0), (0, 0)))[:, :t]
        delta = shifted - x
        lr = jnp.tanh(((x + delta * mu_x) @ Wx1).reshape(b, t, 5, RLOW))
        mus = jnp.einsum('btnr,hnr->btnh', lr, Wx2) + x_bias
        mr, mw, mk, mv, mg = (mus[:, :, i] for i in range(5))
        r = (x + delta * mr) @ Wr
        w = jnp.tanh((x + delta * mw) @ Ww_a) @ Ww_b + bw
        k = (x + delta * mk) @ Wk
        v = (x + delta * mv) @ Wv
        g = jnp.tanh((x + delta * mg) @ Wg_a) @ Wg_b + bg
        r = r.reshape(b, t, NH, DK)
        k = k.reshape(b, t, NH, DK)
        v = v.reshape(b, t, NH, DV)
        decay = jnp.exp(-jnp.exp(w.reshape(b, t, NH, DK)))
        xs = (jnp.moveaxis(r, 1, 0), jnp.moveaxis(k, 1, 0), jnp.moveaxis(v, 1, 0), jnp.moveaxis(decay, 1, 0))
        S0 = jnp.zeros((b, NH, DK, DV), x.dtype)

        def step(S, inp):
            rt, kt, vt, dt = inp
            kv = kt[..., :, None] * vt[..., None, :]
            ot = jnp.einsum('bhk,bhkv->bhv', rt, S + bonus[None, :, :, None] * kv)
            S = dt[..., None] * S + kv
            return (S, ot)
        _, o = jax.lax.scan(step, S0, xs)
        o = jnp.moveaxis(o, 0, 1)
        g = g.reshape(b, t, NH, DV)
        mean = o.mean(-1, keepdims=True)
        var = o.var(-1, keepdims=True)
        on = (o - mean) * jax.lax.rsqrt(var + EPS) * ln_w + ln_b
        o = on * g * jax.nn.sigmoid(g)
        return o.reshape(b, t, VD) @ Wo

    def _L0_attn_b_ref(x, wqkv, wg, wo, gn_weight, gn_bias):
        import jax, jax.numpy as jnp
        import numpy as np
        HIDDEN = 512
        HEAD_DIM = 64
        N_HEADS = HIDDEN // HEAD_DIM
        ROT_DIM = HEAD_DIM // 2
        THETA = 10000.0
        SCALE_BASE = 512.0
        EPS = 1e-05
        B, S = (1, 512)

        def _rotate_half(t):
            x1 = t[..., 0::2]
            x2 = t[..., 1::2]
            return jnp.stack([-x2, x1], axis=-1).reshape(t.shape)

        def _xpos_rotary(q, k, seqlen):
            dim = ROT_DIM
            inv_freq = 1.0 / THETA ** (jnp.arange(0, dim, 2, dtype=jnp.float32) / dim)
            t = jnp.arange(seqlen, dtype=jnp.float32)
            freqs = t[:, None] * inv_freq[None, :]
            freqs = jnp.repeat(freqs, 2, axis=-1)
            base_scale = (jnp.arange(0, dim, 2, dtype=jnp.float32) + 0.4 * dim) / (1.4 * dim)
            power = (t - seqlen // 2) / SCALE_BASE
            scale = base_scale[None, :] ** power[:, None]
            scale = jnp.concatenate([scale, scale], axis=-1)
            cos, sin = (jnp.cos(freqs), jnp.sin(freqs))

            def apply(x, sc):
                xr, xp = (x[..., :dim], x[..., dim:])
                xr = xr * cos * sc + _rotate_half(xr) * sin * sc
                return jnp.concatenate([xr, xp], axis=-1)
            return (apply(q, scale), apply(k, 1.0 / scale))

        def _msr_forward(x, wqkv, wg, wo, gn_weight, gn_bias):
            b, s, _ = x.shape
            qkv = x @ wqkv.T
            qkv = qkv.reshape(b, s, N_HEADS, 3 * HEAD_DIM).transpose(0, 2, 1, 3)
            q, k, v = jnp.split(qkv, 3, axis=-1)
            q, k = _xpos_rotary(q, k, s)
            gamma = 1.0 - 2.0 ** (-5.0 - jnp.arange(N_HEADS, dtype=jnp.float32))
            idx = jnp.arange(s)
            nm = idx[:, None] - idx[None, :]
            decay = jnp.where(nm >= 0, gamma[:, None, None] ** jnp.maximum(nm, 0).astype(jnp.float32), 0.0)
            scores = jnp.einsum('bhid,bhjd->bhij', q, k) * decay
            ret = jnp.einsum('bhij,bhjd->bhid', scores, v)
            mean = ret.mean(axis=(2, 3), keepdims=True)
            var = ret.var(axis=(2, 3), keepdims=True)
            ret = (ret - mean) / jnp.sqrt(var + EPS)
            ret = ret * gn_weight[None, :, None, None] + gn_bias[None, :, None, None]
            y = ret.transpose(0, 2, 1, 3).reshape(b, s, HIDDEN)
            g = x @ wg.T
            mish = g * jnp.tanh(jax.nn.softplus(g))
            return mish * y @ wo.T
        return _msr_forward(x, wqkv, wg, wo, gn_weight, gn_bias)

    def _L0_ffn_ref(x, weight, bias, ln_gamma, ln_beta):
        import jax, jax.numpy as jnp
        import numpy as np
        LN_EPS = 1e-05
        Q_EPS = 1e-05

        def ternary_quantize(w):
            scale = jnp.mean(jnp.abs(w))
            return jnp.clip(jnp.round(w / (scale + Q_EPS)), -1.0, 1.0)

        def layernorm(x, gamma, beta):
            mu = jnp.mean(x, axis=-1, keepdims=True)
            var = jnp.mean(jnp.square(x - mu), axis=-1, keepdims=True)
            return (x - mu) * jax.lax.rsqrt(var + LN_EPS) * gamma + beta
        xn = layernorm(x, ln_gamma, ln_beta)
        w_q = ternary_quantize(weight)
        return jnp.einsum('bsi,oi->bso', xn, w_q) + bias
    x = L0_attn_a_x
    x = x + _L0_attn_a_ref(_layernorm(x, axis=-1), L0_attn_a_mu_x, L0_attn_a_Wx1, L0_attn_a_Wx2, L0_attn_a_x_bias, L0_attn_a_Wr, L0_attn_a_Wk, L0_attn_a_Wv, L0_attn_a_Ww_a, L0_attn_a_Ww_b, L0_attn_a_bw, L0_attn_a_Wg_a, L0_attn_a_Wg_b, L0_attn_a_bg, L0_attn_a_bonus, L0_attn_a_ln_w, L0_attn_a_ln_b, L0_attn_a_Wo)
    x = x + _L0_ffn_ref(_layernorm(x, axis=-1), L0_ffn_weight, L0_ffn_bias, L0_ffn_ln_gamma, L0_ffn_ln_beta)
    x = x + _L0_attn_b_ref(_layernorm(x, axis=-1), L0_attn_b_wqkv, L0_attn_b_wg, L0_attn_b_wo, L0_attn_b_gn_weight, L0_attn_b_gn_bias)
    x = x + _L0_ffn_ref(_layernorm(x, axis=-1), L0_ffn_weight, L0_ffn_bias, L0_ffn_ln_gamma, L0_ffn_ln_beta)
    return x

_drawn_inputs = setup_inputs


def setup_inputs(seed=0):
    import zlib

    import numpy as np

    out = dict(_drawn_inputs(seed))
    spreads = {'L0_attn_a_ln_w': (1.0, 0.6),
     'L0_attn_a_ln_b': (0.0, 0.8),
     'L0_attn_b_gn_weight': (1.0, 0.6),
     'L0_attn_b_gn_bias': (0.0, 0.8),
     'L0_ffn_bias': (0.0, 0.8),
     'L0_ffn_ln_gamma': (1.0, 0.2),
     'L0_ffn_ln_beta': (0.0, 0.1)}
    factors = {'L0_attn_a_mu_x': 8.0,
     'L0_attn_a_Wx1': 8.0,
     'L0_attn_a_Wx2': 8.0,
     'L0_attn_a_x_bias': 8.0,
     'L0_attn_a_Wr': 5.218,
     'L0_attn_a_Wk': 5.205,
     'L0_attn_a_Wv': 5.221,
     'L0_attn_a_Ww_a': 8.0,
     'L0_attn_a_Ww_b': 8.0,
     'L0_attn_a_bw': 8.0,
     'L0_attn_a_Wg_a': 5.442,
     'L0_attn_a_Wg_b': 5.411,
     'L0_attn_a_bg': 8.0,
     'L0_attn_a_bonus': 8.0,
     'L0_attn_a_Wo': 5.196}
    for name, (base, spread) in spreads.items():
        noise = np.random.default_rng([zlib.crc32(name.encode()), seed]).standard_normal(out[name].shape)
        drawn = base * np.exp(spread * noise) if base else spread * noise
        out[name] = jnp.asarray(drawn.astype(out[name].dtype))
    for name, factor in factors.items():
        out[name] = (out[name] * factor).astype(out[name].dtype)
    return out
```

```python
from contextlib import ExitStack

import concourse.bass as bass
from concourse import mybir

ALU = mybir.AluOpType
ACT = mybir.ActivationFunctionType
F32 = mybir.dt.float32

P = 128
B, T, H = 4, 512, 512
TT = T // P
CC = H // P
NH, DK, DV = 16, 16, 16
KD = NH * DK
HF = KD // P
HH = NH // HF
R = 64
MR, MW, MK, MV, MG = range(5)
ORDER = (MK, MV, MW, MR, MG)
NHB, HD = 8, 64
QUADS = NHB // 4
ROT = 32
EPS = 1e-5
BANKS = 7
XM = 2
RING = 4


class Signal:

    def __init__(self, ctx, nc, name, per):
        self.sem = ctx.enter_context(nc.semaphore(name))
        self.per = per

    def at(self, i, k):
        assert 1 <= k <= self.per, (self.per, k)
        return i * self.per + k


def hybrid_block(nc, x_in, weights, vectors, ffn_bias, consts, out, layout):
    with ExitStack() as ctx:
        def sb(name, shape, dt=F32):
            return ctx.enter_context(nc.sbuf_tensor(name, shape, dt))

        def signal(name, per):
            return Signal(ctx, nc, name, per)

        psum = [ctx.enter_context(nc.psum_tensor(f"bank{n}", [P, 512], F32)) for n in range(8)]
        scan_sum = psum[BANKS]

        W = {n: sb("w_" + n, [P, *s]) for n, s in layout["weights"].items()}
        V = {n: sb("v_" + n, [P, s]) for n, s in layout["vectors"].items()}
        C = {n: sb("c_" + n, [P, *s]) for n, s in layout["consts"].items()}
        bias_bc = sb("bias_bc", [P, H])
        eps_t = sb("eps_t", [P, 1])
        mhalf = sb("mhalf", [P, TT])
        one_t = sb("one_t", [P, 1])
        scratch = sb("scratch", [P, 1])
        eps4 = sb("eps4", [P, TT])
        wabs = sb("wabs", [P, 1])
        thr = sb("thr", [P, 2])

        x = sb("x", [P, TT, H])
        stats = sb("stats", [P, TT, 6])
        mv = sb("mv", [P, TT, 2])
        sc = sb("sc", [P, 3, TT])
        xnT = sb("xnT", [P, CC, T + 1])
        REGION = 19584
        region = sb("region", [P, REGION])
        used = [0]

        def part(*shape):
            n = 1
            for s in shape:
                n *= s
            a = region[:, used[0]:used[0] + n]
            used[0] += n
            assert used[0] <= REGION, used
            return a.rearrange("p (a b) -> p a b", a=shape[0]) if len(shape) == 2 else a

        xh = part(TT, H)
        used[0] = 0
        kv = part(RING, T)
        low = kv[:, 0, :]
        St = part(RING, T + 2)
        delta = region[:, RING * T:RING * T + CC * T].rearrange("p (c t) -> p c t", c=CC)
        rS = part(RING, T)
        xm = [part(CC, T) for _ in range(XM)]
        lrT = part(3, T)
        kT, vT, rT, dT, gT, sg = (part(HF, T) for _ in range(6))
        bv, oT = xm[0][:, 0:2, :], xm[0][:, 2:4, :]
        oc, sq = xm[1][:, 0:2, :], xm[1][:, 2:4, :]
        rk = lrT[:, 0:2, :]

        used[0] = 0
        retT, gB, mish = (part(CC, T) for _ in range(3))
        qR, kR, qP, kP = (part(QUADS, T) for _ in range(4))
        vB = part(TT, H)
        t1, t2 = part(2, T), part(2, T)
        AT_AT = [0, 4 * P, 7 * P, 9 * P]
        AT = [part(10 * P) for _ in range(4)]
        gst = sb("gst", [P, CC, 6])
        gmv = sb("gmv", [P, CC, 2])
        ge = sb("ge", [P, 2, CC])
        gs = sb("gs", [P, 2, CC])
        gc = sb("gc", [P, 6, CC])

        loaded = ctx.enter_context(nc.semaphore("weights_loaded"))
        consts_set = ctx.enter_context(nc.semaphore("consts_set"))
        abs_summed = ctx.enter_context(nc.semaphore("abs_summed"))
        abs_total = ctx.enter_context(nc.semaphore("abs_total"))
        thr_ready = ctx.enter_context(nc.semaphore("thr_ready"))
        wq_step = ctx.enter_context(nc.semaphore("wq_step"))
        mhalf_set = ctx.enter_context(nc.semaphore("mhalf_set"))
        x_loaded = signal("x_loaded", 16)
        x_stored = signal("x_stored", 16)
        stats_step = signal("stats_step", 4 * TT)
        mv_ready = signal("mv_ready", 4 * TT)
        ln_step = signal("ln_step", 14)
        ln_scale = signal("ln_scale", 4)
        xh_ready = signal("xh_ready", 4 * TT)
        xT_psum = signal("xT_psum", 4 * CC)
        xT_ready = signal("xT_ready", 4 * CC)
        delta_ready = signal("delta_ready", CC)
        xx_ready = signal("xx_ready", CC)
        lr_psum = signal("lr_psum", 3)
        lr_ready = signal("lr_ready", 3)
        mus_psum = signal("mus_psum", 5 * CC)
        dm_ready = signal("dm_ready", 5 * CC)
        xm_ready = signal("xm_ready", 5 * CC)
        proj_psum = signal("proj_psum", 8)
        proj_ready = signal("proj_ready", 8)
        lowb_psum = signal("lowb_psum", 4)
        lowb_out = signal("lowb_out", 4)
        decay_ready = signal("decay_ready", HF)
        th_ready = signal("th_ready", HF)
        sg_ready = signal("sg_ready", HF)
        st_zero = signal("st_zero", 1)
        vb_psum = signal("vb_psum", HF * DV)
        kv_ready = signal("kv_ready", HF * DV)
        state_ready = signal("state_ready", HF * DV)
        rs_ready = signal("rs_ready", HF * DV)
        o_psum = signal("o_psum", HF * DV)
        rk_ready = signal("rk_ready", HF)
        bonus_psum = signal("bonus_psum", HF)
        bv_ready = signal("bv_ready", HF)
        o_ready = signal("o_ready", HF)
        mean_psum = signal("mean_psum", HF)
        oc_ready = signal("oc_ready", HF)
        sq_ready = signal("sq_ready", HF)
        var_psum = signal("var_psum", HF)
        rstd_step = signal("rstd_step", HF)
        rstd_ready = signal("rstd_ready", HF)
        on_step = signal("on_step", 2 * HF)
        og_ready = signal("og_ready", HF)
        out_psum = signal("out_psum", 4 * TT)
        x_added = signal("x_added", 4 * TT)
        biased = signal("biased", 2 * TT)
        rot_psum = signal("rot_psum", 4)
        rot_parts = signal("rot_parts", 8)
        rot_step = signal("rot_step", 4)
        rot_ready = signal("rot_ready", 4)
        pas_psum = signal("pas_psum", 4)
        pas_ready = signal("pas_ready", 4)
        v_psum = signal("v_psum", TT)
        v_ready = signal("v_ready", TT)
        g_psum = signal("g_psum", CC)
        g_ready = signal("g_ready", CC)
        g_cut = signal("g_cut", 1)
        mish_step = signal("mish_step", 3)
        mish_ready = signal("mish_ready", 1)
        sc_psum = signal("sc_psum", QUADS * TT * 4)
        at_copied = signal("at_copied", QUADS * TT * 4)
        at_masked = signal("at_masked", QUADS * TT * 4)
        ret_psum = signal("ret_psum", CC)
        ret_ready = signal("ret_ready", CC)
        gst_step = signal("gst_step", 2 * CC + 2)
        gn_in = signal("gn_in", 1)
        gn_psum = signal("gn_psum", 1)
        gn_out = signal("gn_out", 1)
        gn_step = signal("gn_step", 6)
        gn_coef = signal("gn_coef", 1)
        y_norm = signal("y_norm", CC)
        y_ready = signal("y_ready", CC)

        groups = {}
        order = []

        def group(key, reader, k):
            groups[key] = len(order)
            order.append((reader, k))

        def ln_groups(l):
            for c in range(CC):
                group(("xT", l, c), xT_ready, l * CC + c + 1)

        ln_groups(0)
        for m in range(3):
            group(("lr", m), lr_ready, m + 1)
        proj_no = {}
        steps = [("mus", 0), ("mus", 1), ("proj", 0), ("mus", 2), ("proj", 1), ("mus", 3), ("proj", 2),
                 ("mus", 4), ("proj", 3), ("proj", 4)]
        for kind, s in steps:
            n = ORDER[s]
            if kind == "mus":
                for c in range(CC):
                    group(("mus", s, c), dm_ready, s * CC + c + 1)
            else:
                for hf in range(1 if n in (MW, MG) else HF):
                    proj_no[n, hf] = len(proj_no) + 1
                    group(("proj", n, hf), proj_ready, proj_no[n, hf])
        for j in range(2):
            for hf in range(HF):
                group(("lowb", j, hf), lowb_out, j * HF + hf + 1)
        for hf in range(HF):
            for n in range(DV):
                group(("vb", hf, n), kv_ready, hf * DV + n + 1)
            group(("bonus", hf), bv_ready, hf + 1)
            group(("mean", hf), oc_ready, hf + 1)
            group(("var", hf), rstd_step, hf + 1)
        for tt in range(TT):
            group(("out", 0, tt), x_added, tt + 1)
        ln_groups(1)
        for tt in range(TT):
            group(("out", 1, tt), x_added, TT + tt + 1)
        ln_groups(2)
        for j in range(2):
            for q in range(QUADS):
                group(("rot", j, q), rot_parts, 2 * (j * QUADS + q) + 2)
        for j in range(2):
            for q in range(QUADS):
                group(("pas", j, q), pas_ready, j * QUADS + q + 1)
        for tt in range(TT):
            group(("v", tt), v_ready, tt + 1)
        for c in range(CC):
            group(("g", c), g_ready, c + 1)
        for q in range(QUADS):
            for jt in range(TT):
                for h in range(4):
                    group(("sc", q, jt, h), at_copied, (q * TT + jt) * 4 + h + 1)
            for c in range(2):
                group(("ret", 2 * q + c), ret_ready, 2 * q + c + 1)
        group("gn", gn_out, 1)
        for tt in range(TT):
            group(("out", 2, tt), x_added, 2 * TT + tt + 1)
        ln_groups(3)
        for tt in range(TT):
            group(("out", 3, tt), x_added, 3 * TT + tt + 1)

        def bank(key):
            return psum[groups[key] % BANKS]

        wmean = region[:, 4096:4096 + P]
        wlow = region[:, 0:CC * H].rearrange("p (c o) -> p c o", c=CC)
        def wait_apart(sem, value):
            nc.vector.wait_ge(sem, value)
            nc.vector.memset(scratch[:], 0.0)

        wmean = region[:, 4096:4096 + P]
        wlow = region[:, 0:CC * H].rearrange("p (c o) -> p c o", c=CC)
        def wait_alone(eng, sem, value):
            value = eng.snap(value)
            eng.wait_ge(loaded, 16 * n_loads)
            eng.wait_ge(sem, value)

        n_loads = len(W) + len(V) + len(C) + 1
        block = ctx.enter_context(nc.Block())

        @block.sync
        def _(sp):
            for n in W:
                sp.dma_start(W[n][:], weights[n]).then_inc(loaded, 16)
            for n in V:
                sp.dma_start(V[n][:], vectors[n]).then_inc(loaded, 16)
            for n in C:
                sp.dma_start(C[n][:], consts[n]).then_inc(loaded, 16)
            sp.dma_start(bias_bc[:], ffn_bias.rearrange("(a n) -> a n", a=1).to_broadcast([P, H])).then_inc(loaded, 16)

            def load(i):
                sp.dma_start(x[:], x_in[bass.ds(i, 1)].rearrange("b (t p) h -> p (b t) h", p=P)).then_inc(x_loaded.sem, 16)

            def store(i):
                sp.wait_ge(x_added.sem, x_added.at(i, 4 * TT))
                sp.dma_start(out[bass.ds(i, 1)].rearrange("b (t p) h -> p (b t) h", p=P), x[:]).then_inc(x_stored.sem, 16)
                sp.wait_ge(x_stored.sem, x_stored.at(i, 16))

            load(0)
            with sp.Fori(0, B - 1) as i:
                store(i)
                load(i + 1)
            store(B - 1)

        @block.tensor
        def _(pe):
            pe.wait_ge(loaded, 16 * n_loads)
            pe.wait_ge(abs_summed, 1)
            nc.tensor.matmul(psum[0][:, 0:1], wmean, wabs[:], start=True, stop=True).then_inc(abs_total, 1)
            pe.wait_ge(thr_ready, 2)

            def row(i):
                def open_bank(key):
                    n = groups[key]
                    if n >= BANKS:
                        reader, k = order[n - BANKS]
                        pe.wait_ge(reader.sem, reader.at(i, k))
                    return bank(key)

                def transposes(l):
                    for c in range(CC):
                        dst = open_bank(("xT", l, c))
                        for tt in range(TT):
                            if c == 0:
                                pe.wait_ge(xh_ready.sem, xh_ready.at(i, l * TT + tt + 1))
                            mm = nc.tensor.transpose(dst[:, tt * P:(tt + 1) * P], xh[:, tt, c * P:(c + 1) * P], C["ident"][:])
                        mm.then_inc(xT_psum.sem, 1)

                def mix(s):
                    n = ORDER[s]
                    lo = R * (n % 2)
                    pe.wait_ge(lr_ready.sem, lr_ready.at(i, n // 2 + 1))
                    for c in range(CC):
                        dst = open_bank(("mus", s, c))
                        nc.tensor.matmul(dst[:], W["wx2"][lo:lo + R, n // 2, c * P:(c + 1) * P], lrT[lo:lo + R, n // 2, :],
                                         start=True, stop=True).then_inc(mus_psum.sem, 1)

                def project(s):
                    n = ORDER[s]
                    for hf in range(1 if n in (MW, MG) else HF):
                        dst = open_bank(("proj", n, hf))
                        for c in range(CC):
                            if hf == 0:
                                pe.wait_ge(xm_ready.sem, xm_ready.at(i, s * CC + c + 1))
                            if n == MW:
                                o, w = dst[0:R, :], W["ab_a"][:, c, 0:R]
                            elif n == MG:
                                o, w = dst[R:P, :], W["ab_a"][:, c, R:P]
                            else:
                                o, w = dst[:], W[{MR: "wr", MK: "wk", MV: "wv"}[n]][:, c, hf * P:(hf + 1) * P]
                            mm = nc.tensor.matmul(o, w, xm[s % XM][:, c, :], start=(c == 0), stop=(c == CC - 1))
                        mm.then_inc(proj_psum.sem, 1)

                def spread_v(hf, q):
                    for g in range(4):
                        dst = open_bank(("vb", hf, 4 * q + g))
                        rows = slice(32 * g, 32 * g + 32)
                        nc.tensor.matmul(dst[:], C["sel_row"][rows, q, :], vT[rows, hf, :], start=True, stop=True)\
                            .then_inc(vb_psum.sem, 1)

                def sum_dk(hf, q):
                    for g in range(4):
                        pe.wait_ge(rs_ready.sem, rs_ready.at(i, hf * DV + 4 * q + g + 1))
                        mm = nc.tensor.matmul(scan_sum[32 * g:32 * g + 32, :], C["sel_col"][:, q, :], rS[:, g, :],
                                              start=(q == 0), stop=(q == 3))
                        mm.then_inc(o_psum.sem, 1)

                def out_groups(l, lhs, w, n_k, ready):
                    for tt in range(TT):
                        dst = open_bank(("out", l, tt))
                        for c in range(n_k):
                            if tt == 0:
                                ready(c)
                            mm = nc.tensor.matmul(dst[:], lhs[:, c, tt * P:(tt + 1) * P], w[:, c, :],
                                                  start=(c == 0), stop=(c == n_k - 1))
                        mm.then_inc(out_psum.sem, 1)

                transposes(0)
                for m in range(3):
                    dst = open_bank(("lr", m))
                    w = P if m < 2 else R
                    for c in range(CC):
                        if m == 0:
                            pe.wait_ge(xx_ready.sem, xx_ready.at(i, c + 1))
                        mm = nc.tensor.matmul(dst[0:w, :], W["wx1"][:, c, m * P:m * P + w], xm[1][:, c, :],
                                              start=(c == 0), stop=(c == CC - 1))
                    mm.then_inc(lr_psum.sem, 1)
                for kind, s in steps:
                    (mix if kind == "mus" else project)(s)
                for j in range(2):
                    n = (MW, MG)[j]
                    pe.wait_ge(proj_ready.sem, proj_ready.at(i, proj_no[n, 0]))
                    for hf in range(HF):
                        dst = open_bank(("lowb", j, hf))
                        nc.tensor.matmul(dst[:], W["ab_b"][R * j:R * j + R, hf * P:(hf + 1) * P], low[R * j:R * j + R, :],
                                         start=True, stop=True).then_inc(lowb_psum.sem, 1)
                pe.wait_ge(proj_ready.sem, proj_ready.at(i, proj_no[MV, HF - 1]))
                for hf in range(HF):
                    spread_v(hf, 0)
                    for q in range(4):
                        if q < 3:
                            spread_v(hf, q + 1)
                        if q == 0 and hf > 0:
                            pe.wait_ge(o_ready.sem, o_ready.at(i, hf))
                        sum_dk(hf, q)
                    dst = open_bank(("bonus", hf))
                    pe.wait_ge(rk_ready.sem, rk_ready.at(i, hf + 1))
                    nc.tensor.matmul(dst[:], C["head_sum"][:], rk[:, hf, :], start=True, stop=True).then_inc(bonus_psum.sem, 1)
                    dst = open_bank(("mean", hf))
                    pe.wait_ge(o_ready.sem, o_ready.at(i, hf + 1))
                    nc.tensor.matmul(dst[:], C["head_mean"][:], oT[:, hf, :], start=True, stop=True).then_inc(mean_psum.sem, 1)
                    dst = open_bank(("var", hf))
                    pe.wait_ge(sq_ready.sem, sq_ready.at(i, hf + 1))
                    nc.tensor.matmul(dst[:], C["head_mean"][:], sq[:, hf, :], start=True, stop=True).then_inc(var_psum.sem, 1)
                out_groups(0, sg, W["wo_a"], HF, lambda c: pe.wait_ge(og_ready.sem, og_ready.at(i, c + 1)))

                def ffn(l):
                    transposes(l)
                    out_groups(l, xnT[:, :, 1:T + 1], W["wq"], CC,
                               lambda c: pe.wait_ge(xT_ready.sem, xT_ready.at(i, l * CC + c + 1)))

                ffn(1)

                transposes(2)
                pe.wait_ge(xT_ready.sem, xT_ready.at(i, 3 * CC))

                def chan_group(key, w, col, sig):
                    dst = open_bank(key)
                    for c in range(CC):
                        mm = nc.tensor.matmul(dst[:], w[:, c, col:col + P], xnT[:, c, 1:T + 1], start=(c == 0), stop=(c == CC - 1))
                    mm.then_inc(sig.sem, 1)

                for j in range(2):
                    for q in range(QUADS):
                        chan_group(("rot", j, q), W[("q_b", "k_b")[j]], q * P, rot_psum)
                for j in range(2):
                    for q in range(QUADS):
                        chan_group(("pas", j, q), W[("q_b", "k_b")[j]], (QUADS + q) * P, pas_psum)
                for tt in range(TT):
                    dst = open_bank(("v", tt))
                    for c in range(CC):
                        mm = nc.tensor.matmul(dst[:], xnT[:, c, 1 + tt * P:1 + (tt + 1) * P], W["v_b"][:, c, :],
                                              start=(c == 0), stop=(c == CC - 1))
                    mm.then_inc(v_psum.sem, 1)
                for c in range(CC):
                    chan_group(("g", c), W["g_b"], c * P, g_psum)
                pe.wait_ge(rot_ready.sem, rot_ready.at(i, 4))
                pe.wait_ge(pas_ready.sem, pas_ready.at(i, 4))
                pe.wait_ge(v_ready.sem, v_ready.at(i, TT))
                for q in range(QUADS):
                    for jt in range(TT):
                        for h in range(4):
                            dst = open_bank(("sc", q, jt, h))
                            rows = slice(32 * h, 32 * h + 32)
                            n = T - jt * P
                            for kk, qq, first in ((kR, qR, True), (kP, qP, False)):
                                mm = nc.tensor.matmul(dst[:, 0:n], kk[rows, q, jt * P:(jt + 1) * P], qq[rows, q, jt * P:T],
                                                      start=first, stop=not first)
                            mm.then_inc(sc_psum.sem, 1)
                    for c in range(2):
                        dst = open_bank(("ret", 2 * q + c))
                        for jt in range(TT):
                            for e in range(2):
                                h = 2 * c + e
                                pe.wait_ge(at_masked.sem, at_masked.at(i, (q * TT + jt) * 4 + h + 1))
                                mm = nc.tensor.matmul(dst[64 * e:64 * e + 64, jt * P:T],
                                                      vB[:, jt, (4 * q + h) * HD:(4 * q + h + 1) * HD],
                                                      AT[h][:, AT_AT[jt]:AT_AT[jt] + T - jt * P], start=(jt == 0), stop=(jt == TT - 1))
                        mm.then_inc(ret_psum.sem, 1)
                dst = open_bank("gn")
                pe.wait_ge(gn_in.sem, gn_in.at(i, 1))
                nc.tensor.matmul(dst[:, 0:2 * CC], C["pair_mean"][:], ge[:].rearrange("p a c -> p (a c)"),
                                 start=True, stop=True).then_inc(gn_psum.sem, 1)
                out_groups(2, retT, W["o_b"], CC, lambda c: pe.wait_ge(y_ready.sem, y_ready.at(i, c + 1)))
                ffn(3)
                pe.wait_ge(x_stored.sem, x_stored.at(i, 16))

            with pe.Fori(0, B) as i:
                row(i)

        @block.scalar
        def _(act):
            act.wait_ge(loaded, 16 * n_loads)
            act.wait_ge(consts_set, 4)

            def row(i):
                def copy_xT(l):
                    for c in range(CC):
                        act.wait_ge(xT_psum.sem, xT_psum.at(i, l * CC + c + 1))
                        src, dst = bank(("xT", l, c))[:], xnT[:, c, 1:T + 1]
                        if l % 2:
                            ins = nc.scalar.activation(dst, src, ACT.Identity, scale=V["gamma"][:, c:c + 1], bias=V["beta"][:, c:c + 1])
                        else:
                            ins = nc.scalar.activation(dst, src, ACT.Copy)
                        ins.then_inc(xT_ready.sem, 1)

                copy_xT(0)
                for m in range(3):
                    rows = slice(0, P if m < 2 else R)
                    act.wait_ge(lr_psum.sem, lr_psum.at(i, m + 1))
                    nc.scalar.activation(lrT[rows, m, :], bank(("lr", m))[rows, :], ACT.Tanh).then_inc(lr_ready.sem, 1)
                for n in ORDER:
                    for hf in range(1 if n in (MW, MG) else HF):
                        act.wait_ge(proj_psum.sem, proj_psum.at(i, proj_no[n, hf]))
                        src = bank(("proj", n, hf))
                        if n in (MW, MG):
                            rows = slice(0, R) if n == MW else slice(R, P)
                            ins = nc.scalar.activation(low[rows, :], src[rows, :], ACT.Tanh)
                        else:
                            ins = nc.scalar.activation({MR: rT, MK: kT, MV: vT}[n][:, hf, :], src[:], ACT.Copy)
                        ins.then_inc(proj_ready.sem, 1)
                for hf in range(HF):
                    act.wait_ge(lowb_psum.sem, lowb_psum.at(i, hf + 1))
                    nc.scalar.activation(dT[:, hf, :], bank(("lowb", 0, hf))[:], ACT.Exp, bias=V["bw"][:, hf:hf + 1])\
                        .then_inc(lowb_out.sem, 1)
                for hf in range(HF):
                    act.wait_ge(lowb_psum.sem, lowb_psum.at(i, HF + hf + 1))
                    nc.scalar.activation(gT[:, hf, :], bank(("lowb", 1, hf))[:], ACT.Identity, bias=V["bg"][:, hf:hf + 1])\
                        .then_inc(lowb_out.sem, 1)
                for hf in range(HF):
                    act.wait_ge(lowb_out.sem, lowb_out.at(i, hf + 1))
                    nc.scalar.activation(dT[:, hf, :], dT[:, hf, :], ACT.Exp, scale=-1.0).then_inc(decay_ready.sem, 1)
                for hf in range(HF):
                    act.wait_ge(lowb_out.sem, lowb_out.at(i, HF + hf + 1))
                    nc.scalar.activation(sg[:, hf, :], gT[:, hf, :], ACT.Tanh, scale=0.5).then_inc(th_ready.sem, 1)
                for hf in range(HF):
                    act.wait_ge(oc_ready.sem, oc_ready.at(i, hf + 1))
                    nc.scalar.activation(sq[:, hf, :], oc[:, hf, :], ACT.Square).then_inc(sq_ready.sem, 1)
                    act.wait_ge(var_psum.sem, var_psum.at(i, hf + 1))
                    nc.scalar.activation(sq[:, hf, :], bank(("var", hf))[:], ACT.Ln, bias=eps_t[:, 0:1]).then_inc(rstd_step.sem, 1)
                    act.wait_ge(rstd_step.sem, rstd_step.at(i, hf + 1))
                    nc.scalar.activation(sq[:, hf, :], sq[:, hf, :], ACT.Exp, scale=-0.5).then_inc(rstd_ready.sem, 1)
                copy_xT(1)
                copy_xT(2)
                for tt in range(TT):
                    act.wait_ge(v_psum.sem, v_psum.at(i, tt + 1))
                    nc.scalar.activation(vB[:, tt, :], bank(("v", tt))[:], ACT.Copy).then_inc(v_ready.sem, 1)
                for c in range(CC):
                    act.wait_ge(g_psum.sem, g_psum.at(i, c + 1))
                    nc.scalar.activation(gB[:, c, :], bank(("g", c))[:], ACT.Copy).then_inc(g_ready.sem, 1)
                act.wait_ge(g_cut.sem, g_cut.at(i, 1))
                nc.scalar.activation(mish[:], mish[:], ACT.Exp).then_inc(mish_step.sem, 1)
                act.wait_ge(mish_step.sem, mish_step.at(i, 1))
                nc.scalar.activation(mish[:], mish[:], ACT.Ln, bias=one_t[:, 0:1]).then_inc(mish_step.sem, 1)
                act.wait_ge(mish_step.sem, mish_step.at(i, 2))
                nc.scalar.activation(mish[:], mish[:], ACT.Tanh).then_inc(mish_step.sem, 1)
                for q in range(QUADS):
                    for jt in range(TT):
                        for h in range(4):
                            act.wait_ge(sc_psum.sem, sc_psum.at(i, (q * TT + jt) * 4 + h + 1))
                            if q > 0 and jt == 0:
                                act.wait_ge(ret_psum.sem, ret_psum.at(i, 2 * (q - 1) + h // 2 + 1))
                            n = T - jt * P
                            nc.scalar.activation(AT[h][:, AT_AT[jt]:AT_AT[jt] + n], bank(("sc", q, jt, h))[:, 0:n], ACT.Copy)\
                                .then_inc(at_copied.sem, 1)
                    for c in range(2 * q, 2 * q + 2):
                        act.wait_ge(ret_psum.sem, ret_psum.at(i, c + 1))
                        nc.scalar.activation(retT[:, c, :], bank(("ret", c))[:], ACT.Copy).then_inc(ret_ready.sem, 1)
                copy_xT(3)
                act.wait_ge(x_stored.sem, x_stored.at(i, 16))

            with act.Fori(0, B) as i:
                row(i)

        @block.vector
        def _(dve):
            nc.vector.memset(eps_t[:], EPS).then_inc(consts_set, 1)
            nc.vector.memset(one_t[:], 1.0).then_inc(consts_set, 1)
            nc.vector.memset(wmean, 1.0 / (H * H)).then_inc(consts_set, 1)
            nc.vector.memset(xnT[:, :, 0:1], 0.0).then_inc(consts_set, 1)
            dve.wait_ge(loaded, 16 * n_loads)
            nc.vector.tensor_reduce(wabs[:], W["wq"][:], mybir.AxisListType.XY, ALU.add, apply_absolute_value=True)\
                .then_inc(abs_summed, 1)
            dve.wait_ge(abs_total, 1)
            nc.vector.tensor_scalar(thr[:, 0:1], psum[0][:, 0:1], 1e-5, 0.5, ALU.add, ALU.mult).then_inc(wq_step, 1)
            dve.wait_ge(wq_step, 1)
            nc.vector.tensor_scalar(thr[:, 1:2], thr[:, 0:1], -1.0, None, ALU.mult).then_inc(wq_step, 1)
            dve.wait_ge(wq_step, 2)
            nc.vector.tensor_scalar(wlow, W["wq"][:], thr[:, 1:2], None, ALU.is_lt).then_inc(thr_ready, 1)
            dve.wait_ge(thr_ready, 1)
            nc.vector.scalar_tensor_tensor(W["wq"][:], W["wq"][:], thr[:, 0:1], wlow, ALU.is_gt, ALU.subtract).then_inc(thr_ready, 1)
            dve.wait_ge(thr_ready, 2)

            def row(i):
                def layer_norm(l):
                    for tt in range(TT):
                        if l == 0:
                            if tt == 0:
                                dve.wait_ge(x_loaded.sem, x_loaded.at(i, 16))
                        else:
                            dve.wait_ge(x_added.sem, x_added.at(i, (l - 1) * TT + tt + 1))
                        nc.vector.bn_stats(stats[:, tt, :], x[:, tt, :]).then_inc(stats_step.sem, 1)
                    wait_apart(stats_step.sem, stats_step.at(i, (l + 1) * TT))
                    for tt in range(TT):
                        nc.vector.bn_aggr(mv[:, tt, :], stats[:, tt, :]).then_inc(mv_ready.sem, 1)
                    dve.wait_ge(ln_scale.sem, ln_scale.at(i, l + 1))
                    for tt in range(TT):
                        nc.vector.tensor_scalar(xh[:, tt, :], x[:, tt, :], mv[:, tt, 0:1], sc[:, 2, tt:tt + 1], ALU.subtract, ALU.mult)\
                            .then_inc(xh_ready.sem, 1)

                def add_to_x(l):
                    for tt in range(TT):
                        k = l * TT + tt + 1
                        dve.wait_ge(out_psum.sem, out_psum.at(i, k))
                        if l % 2:
                            dve.wait_ge(biased.sem, biased.at(i, (l // 2) * TT + tt + 1))
                        nc.vector.tensor_tensor(x[:, tt, :], bank(("out", l, tt))[:], x[:, tt, :], ALU.add).then_inc(x_added.sem, 1)

                layer_norm(0)
                for c in range(CC):
                    dve.wait_ge(xT_ready.sem, xT_ready.at(i, c + 1))
                    nc.vector.tensor_tensor(delta[:, c, :], xnT[:, c, 0:T], xnT[:, c, 1:T + 1], ALU.subtract).then_inc(delta_ready.sem, 1)
                for c in range(CC):
                    dve.wait_ge(delta_ready.sem, delta_ready.at(i, c + 1))
                    nc.vector.scalar_tensor_tensor(xm[1][:, c, :], delta[:, c, :], V["mu"][:, c:c + 1], xnT[:, c, 1:T + 1],
                                                   ALU.mult, ALU.add).then_inc(xx_ready.sem, 1)
                for s, n in enumerate(ORDER):
                    for c in range(CC):
                        dve.wait_ge(mus_psum.sem, mus_psum.at(i, s * CC + c + 1))
                        nc.vector.scalar_tensor_tensor(xm[s % XM][:, c, :], bank(("mus", s, c))[:], V["xb"][:, n * CC + c:n * CC + c + 1],
                                                       delta[:, c, :], ALU.add, ALU.mult).then_inc(dm_ready.sem, 1)
                dve.wait_ge(dm_ready.sem, dm_ready.at(i, 5 * CC))
                nc.vector.memset(St[:, :, 0:1], 0.0).then_inc(st_zero.sem, 1)
                for hf in range(HF):
                    dve.wait_ge(th_ready.sem, th_ready.at(i, hf + 1))
                    nc.vector.scalar_tensor_tensor(sg[:, hf, :], sg[:, hf, :], 1.0, gT[:, hf, :], ALU.add, ALU.mult).then_inc(sg_ready.sem, 1)
                dve.wait_ge(proj_ready.sem, proj_ready.at(i, proj_no[MR, 1]))
                for hf in range(HF):
                    nc.vector.scalar_tensor_tensor(rk[:, hf, :], rT[:, hf, :], V["bonus"][:, hf:hf + 1], kT[:, hf, :], ALU.mult, ALU.mult)\
                        .then_inc(rk_ready.sem, 1)

                def kv_products(m):
                    dve.wait_ge(vb_psum.sem, vb_psum.at(i, m + 1))
                    if m >= RING:
                        dve.wait_ge(state_ready.sem, state_ready.at(i, m - RING + 1))
                    nc.vector.tensor_tensor(kv[:, m % RING, :], bank(("vb", m // DV, m % DV))[:], kT[:, m // DV, :], ALU.mult)\
                        .then_inc(kv_ready.sem, 1)

                def scan(m):
                    dve.wait_ge(kv_ready.sem, kv_ready.at(i, m + 1))
                    if m % DV == 0:
                        dve.wait_ge(decay_ready.sem, decay_ready.at(i, m // DV + 1))
                    if m >= RING:
                        dve.wait_ge(rs_ready.sem, rs_ready.at(i, m - RING + 1))
                    nc.vector.tensor_tensor_scan(St[:, m % RING, 1:T + 1], dT[:, m // DV, :], kv[:, m % RING, :], 0.0, ALU.mult, ALU.add)\
                        .then_inc(state_ready.sem, 1)

                for hf in range(HF):
                    kv_products(hf * DV)
                    for n in range(DV):
                        if n + 1 < DV:
                            kv_products(hf * DV + n + 1)
                        scan(hf * DV + n)
                    dve.wait_ge(bonus_psum.sem, bonus_psum.at(i, hf + 1))
                    nc.vector.tensor_tensor(bv[:, hf, :], bank(("bonus", hf))[:], vT[:, hf, :], ALU.mult).then_inc(bv_ready.sem, 1)
                    dve.wait_ge(bv_ready.sem, bv_ready.at(i, hf + 1))
                    dve.wait_ge(o_psum.sem, o_psum.at(i, (hf + 1) * DV))
                    nc.vector.tensor_tensor(oT[:, hf, :], scan_sum[:], bv[:, hf, :], ALU.add).then_inc(o_ready.sem, 1)
                    dve.wait_ge(o_ready.sem, o_ready.at(i, hf + 1))
                    dve.wait_ge(mean_psum.sem, mean_psum.at(i, hf + 1))
                    nc.vector.scalar_tensor_tensor(oc[:, hf, :], bank(("mean", hf))[:], -1.0, oT[:, hf, :], ALU.mult, ALU.add).then_inc(oc_ready.sem, 1)
                    dve.wait_ge(rstd_ready.sem, rstd_ready.at(i, hf + 1))
                    nc.vector.tensor_tensor(oc[:, hf, :], oc[:, hf, :], sq[:, hf, :], ALU.mult).then_inc(on_step.sem, 1)
                    dve.wait_ge(on_step.sem, on_step.at(i, 2 * hf + 1))
                    nc.vector.tensor_scalar(oc[:, hf, :], oc[:, hf, :], V["lnw"][:, 0:1], V["lnb"][:, 0:1], ALU.mult, ALU.add).then_inc(on_step.sem, 1)
                    dve.wait_ge(on_step.sem, on_step.at(i, 2 * hf + 2))
                    nc.vector.scalar_tensor_tensor(sg[:, hf, :], oc[:, hf, :], 0.5, sg[:, hf, :], ALU.mult, ALU.mult).then_inc(og_ready.sem, 1)
                add_to_x(0)
                layer_norm(1)
                add_to_x(1)
                layer_norm(2)
                swap = [k ^ 1 for k in range(32)]
                for m in range(4):
                    j, q = m // QUADS, m % QUADS
                    dve.wait_ge(rot_psum.sem, rot_psum.at(i, m + 1))
                    if m >= 2:
                        dve.wait_ge(rot_ready.sem, rot_ready.at(i, m - 1))
                    nc.vector.tensor_tensor(t1[:, m % 2, :], bank(("rot", j, q))[:], C["cos"][:, m, :], ALU.mult).then_inc(rot_parts.sem, 1)
                    nc.vector.stream_shuffle(t2[:, m % 2, :], bank(("rot", j, q))[:], swap).then_inc(rot_parts.sem, 1)
                for m in range(4):
                    j, q = m // QUADS, m % QUADS
                    dve.wait_ge(pas_psum.sem, pas_psum.at(i, m + 1))
                    nc.vector.tensor_tensor((qP, kP)[j][:, q, :], bank(("pas", j, q))[:], C["pow"][:, m, :], ALU.mult).then_inc(pas_ready.sem, 1)
                dve.wait_ge(g_ready.sem, g_ready.at(i, CC))
                nc.vector.tensor_scalar(mish[:], gB[:], 30.0, None, ALU.min).then_inc(g_cut.sem, 1)
                for c in range(CC):
                    dve.wait_ge(ret_ready.sem, ret_ready.at(i, c + 1))
                    nc.vector.bn_stats(gst[:, c, :], retT[:, c, :]).then_inc(gst_step.sem, 1)
                wait_apart(gst_step.sem, gst_step.at(i, CC))
                for c in range(CC):
                    nc.vector.bn_aggr(gmv[:, c, :], gst[:, c, :]).then_inc(gst_step.sem, 1)
                dve.wait_ge(gst_step.sem, gst_step.at(i, 2 * CC))
                nc.vector.tensor_copy(ge[:, 0, :], gmv[:, :, 0]).then_inc(gst_step.sem, 1)
                nc.vector.tensor_tensor(ge[:, 1, :], gmv[:, :, 0], gmv[:, :, 0], ALU.mult).then_inc(gst_step.sem, 1)
                dve.wait_ge(gst_step.sem, gst_step.at(i, 2 * CC + 2))
                nc.vector.tensor_tensor(ge[:, 1, :], ge[:, 1, :], gmv[:, :, 1], ALU.add).then_inc(gn_in.sem, 1)
                dve.wait_ge(gn_psum.sem, gn_psum.at(i, 1))
                nc.vector.tensor_copy(gs[:].rearrange("p a c -> p (a c)"), bank("gn")[:, 0:2 * CC]).then_inc(gn_out.sem, 1)
                dve.wait_ge(gn_coef.sem, gn_coef.at(i, 1))
                for c in range(CC):
                    nc.vector.tensor_scalar(retT[:, c, :], retT[:, c, :], gc[:, 4, c:c + 1], gc[:, 5, c:c + 1], ALU.mult, ALU.add)\
                        .then_inc(y_norm.sem, 1)
                add_to_x(2)
                layer_norm(3)
                add_to_x(3)
                dve.wait_ge(x_stored.sem, x_stored.at(i, 16))

            with dve.Fori(0, B) as i:
                row(i)

        @block.gpsimd
        def _(pool):
            nc.gpsimd.memset(mhalf[:], -0.5).then_inc(mhalf_set, 1)
            nc.gpsimd.memset(eps4[:], EPS).then_inc(mhalf_set, 1)
            pool.wait_ge(mhalf_set, 2)
            pool.wait_ge(loaded, 16 * n_loads)

            def row(i):
                def ln_scales(l, k):
                    def step(ins):
                        nonlocal k
                        k += 1
                        ins.then_inc(ln_step.sem, 1)
                        pool.wait_ge(ln_step.sem, ln_step.at(i, k))

                    var, a, b, s = mv[:, :, 1], sc[:, 0, :], sc[:, 1, :], sc[:, 2, :]
                    pool.wait_ge(mv_ready.sem, mv_ready.at(i, (l + 1) * TT))
                    step(nc.gpsimd.tensor_tensor(a, var, eps4[:], ALU.add))
                    if l % 2 == 0:
                        nc.gpsimd.tensor_tensor(s, a, mhalf[:], ALU.pow).then_inc(ln_scale.sem, 1)
                        return k
                    step(nc.gpsimd.tensor_tensor(a, a, mhalf[:], ALU.pow))
                    step(nc.gpsimd.tensor_tensor(b, var, a, ALU.mult))
                    step(nc.gpsimd.tensor_tensor(b, b, a, ALU.mult))
                    step(nc.gpsimd.tensor_tensor(b, b, eps4[:], ALU.add))
                    step(nc.gpsimd.tensor_tensor(b, b, mhalf[:], ALU.pow))
                    nc.gpsimd.tensor_tensor(s, a, b, ALU.mult).then_inc(ln_scale.sem, 1)
                    return k

                def add_bias(l):
                    for tt in range(TT):
                        pool.wait_ge(xh_ready.sem, xh_ready.at(i, l * TT + tt + 1))
                        nc.gpsimd.tensor_tensor(x[:, tt, :], x[:, tt, :], bias_bc[:], ALU.add).then_inc(biased.sem, 1)

                k = ln_scales(0, 0)
                for s in range(5):
                    for c in range(CC):
                        pool.wait_ge(dm_ready.sem, dm_ready.at(i, s * CC + c + 1))
                        nc.gpsimd.tensor_tensor(xm[s % XM][:, c, :], xm[s % XM][:, c, :], xnT[:, c, 1:T + 1], ALU.add).then_inc(xm_ready.sem, 1)
                pool.wait_ge(st_zero.sem, st_zero.at(i, 1))
                for m in range(HF * DV):
                    pool.wait_ge(state_ready.sem, state_ready.at(i, m + 1))
                    if m >= RING:
                        pool.wait_ge(o_psum.sem, o_psum.at(i, m - RING + 1))
                    nc.gpsimd.tensor_tensor(rS[:, m % RING, :], St[:, m % RING, 0:T], rT[:, m // DV, :], ALU.mult).then_inc(rs_ready.sem, 1)
                k = ln_scales(1, k)
                add_bias(1)
                k = ln_scales(2, k)
                for m in range(4):
                    j, q = m // QUADS, m % QUADS
                    pool.wait_ge(rot_parts.sem, rot_parts.at(i, 2 * m + 2))
                    nc.gpsimd.tensor_tensor(t2[:, m % 2, :], t2[:, m % 2, :], C["sin"][:, m, :], ALU.mult).then_inc(rot_step.sem, 1)
                    pool.wait_ge(rot_step.sem, rot_step.at(i, m + 1))
                    nc.gpsimd.tensor_tensor((qR, kR)[j][:, q, :], t1[:, m % 2, :], t2[:, m % 2, :], ALU.add).then_inc(rot_ready.sem, 1)
                for q in range(QUADS):
                    for jt in range(TT):
                        for h in range(4):
                            pool.wait_ge(at_copied.sem, at_copied.at(i, (q * TT + jt) * 4 + h + 1))
                            blk = AT[h][:, AT_AT[jt]:AT_AT[jt] + P]
                            nc.gpsimd.tensor_tensor(blk, blk, C["causal"][:], ALU.mult).then_inc(at_masked.sem, 1)
                pool.wait_ge(mish_step.sem, mish_step.at(i, 3))
                nc.gpsimd.tensor_tensor(mish[:], mish[:], gB[:], ALU.mult).then_inc(mish_ready.sem, 1)

                gk = 0

                def step(ins):
                    nonlocal gk
                    gk += 1
                    ins.then_inc(gn_step.sem, 1)
                    pool.wait_ge(gn_step.sem, gn_step.at(i, gk))

                pool.wait_ge(gn_out.sem, gn_out.at(i, 1))
                step(nc.gpsimd.tensor_tensor(gc[:, 0, :], gs[:, 0, :], gs[:, 0, :], ALU.mult))
                step(nc.gpsimd.tensor_tensor(gc[:, 1, :], gs[:, 1, :], gc[:, 0, :], ALU.subtract))
                step(nc.gpsimd.tensor_tensor(gc[:, 2, :], gc[:, 1, :], eps4[:], ALU.add))
                step(nc.gpsimd.tensor_tensor(gc[:, 3, :], gc[:, 2, :], mhalf[:], ALU.pow))
                step(nc.gpsimd.tensor_tensor(gc[:, 4, :], gc[:, 3, :], V["gnw"][:], ALU.mult))
                step(nc.gpsimd.tensor_tensor(gc[:, 0, :], gs[:, 0, :], gc[:, 4, :], ALU.mult))
                nc.gpsimd.tensor_tensor(gc[:, 5, :], V["gnb"][:], gc[:, 0, :], ALU.subtract).then_inc(gn_coef.sem, 1)
                pool.wait_ge(mish_ready.sem, mish_ready.at(i, 1))
                for c in range(CC):
                    pool.wait_ge(y_norm.sem, y_norm.at(i, c + 1))
                    nc.gpsimd.tensor_tensor(retT[:, c, :], retT[:, c, :], mish[:, c, :], ALU.mult).then_inc(y_ready.sem, 1)
                k = ln_scales(3, k)
                add_bias(3)
                pool.wait_ge(x_stored.sem, x_stored.at(i, 16))

            with pool.Fori(0, B) as i:
                row(i)


def kernel(**inputs):
    import numpy as np
    import concourse.bacc as bacc
    from concourse import mybir as mb
    from concourse.bass_utils import run_bass_kernel_spmd

    a = {k.replace("L0_", ""): np.asarray(v) for k, v in inputs.items()}

    def rows(w):
        return np.ascontiguousarray(w.reshape(-1, P, w.shape[1]).transpose(1, 0, 2))

    def cols(v):
        return np.ascontiguousarray(v.reshape(-1, P).T)

    def by_dv(w):
        return w.reshape(*w.shape[:-1], HF, HH, DV).swapaxes(-1, -2).reshape(w.shape)

    wx2 = a["attn_a_Wx2"].transpose(1, 2, 0)
    wx2 = np.concatenate([wx2, wx2[4:5]]).reshape(3, 2 * R, H).transpose(1, 0, 2)
    qkv = a["attn_b_wqkv"].reshape(NHB, 3, HD, H)

    def quads(w):
        return np.concatenate([w[:, :ROT].reshape(-1, H), w[:, ROT:].reshape(-1, H)]).T

    weights = {
        "wx1": rows(a["attn_a_Wx1"]), "wx2": np.ascontiguousarray(wx2),
        "wr": rows(a["attn_a_Wr"]), "wk": rows(a["attn_a_Wk"]), "wv": rows(by_dv(a["attn_a_Wv"])),
        "ab_a": rows(np.concatenate([a["attn_a_Ww_a"], a["attn_a_Wg_a"]], axis=1)),
        "ab_b": np.ascontiguousarray(np.concatenate([a["attn_a_Ww_b"], by_dv(a["attn_a_Wg_b"])], axis=0)),
        "wo_a": rows(by_dv(a["attn_a_Wo"].T).T),
        "wq": rows(a["ffn_weight"].T),
        "q_b": rows(quads(qkv[:, 0])), "k_b": rows(quads(qkv[:, 1])), "v_b": rows(qkv[:, 2].reshape(-1, H).T),
        "g_b": rows(a["attn_b_wg"].T), "o_b": rows(a["attn_b_wo"].T),
    }
    vectors = {
        "mu": cols(a["attn_a_mu_x"]), "xb": cols(a["attn_a_x_bias"].reshape(-1)),
        "bw": cols(a["attn_a_bw"]), "bg": cols(by_dv(a["attn_a_bg"])), "bonus": cols(a["attn_a_bonus"].reshape(-1)),
        "lnw": np.repeat(a["attn_a_ln_w"], HH)[:, None].copy(), "lnb": np.repeat(a["attn_a_ln_b"], HH)[:, None].copy(),
        "gamma": cols(a["ffn_ln_gamma"]), "beta": cols(a["ffn_ln_beta"]),
        "gnw": cols(np.repeat(a["attn_b_gn_weight"], HD)), "gnb": cols(np.repeat(a["attn_b_gn_bias"], HD)),
    }
    f = np.float32
    p = np.arange(P)
    sel_row = np.zeros((P, 4, P), f)
    sel_col = np.zeros((P, 4, 32), f)
    for q in range(4):
        for h in range(HH):
            for g in range(4):
                sel_row[32 * g + 8 * q + h, q, DK * h:DK * h + DK] = 1
            sel_col[DK * h:DK * h + DK, q, 8 * q + h] = 1
    t = np.arange(T, dtype=np.float64)
    inv = 1.0 / 10000.0 ** (np.arange(0, ROT, 2) / ROT)
    fr = np.repeat(t[:, None] * inv[None], 2, axis=1)
    base = (np.arange(0, ROT, 2) + 0.4 * ROT) / (1.4 * ROT)
    scale = base[None] ** ((t - T // 2) / 512.0)[:, None]
    scale = np.concatenate([scale, scale], axis=1)
    sign = np.where(np.arange(ROT) % 2 == 0, -1.0, 1.0)
    cos, sin, pw = np.zeros((P, 4, T)), np.zeros((P, 4, T)), np.zeros((P, 4, T))
    for j in range(2):
        for q in range(2):
            for h in range(4):
                gamma = 1.0 - 2.0 ** (-5.0 - (4 * q + h))
                g = gamma ** ((t - T // 2) * (1 if j == 0 else -1))
                s = scale if j == 0 else 1.0 / scale
                r = slice(32 * h, 32 * h + 32)
                cos[r, 2 * j + q] = (np.cos(fr) * s).T * g
                sin[r, 2 * j + q] = (np.sin(fr) * s * sign).T * g
                pw[r, 2 * j + q] = g
    consts = {
        "ident": np.eye(P, dtype=f), "sel_row": sel_row, "sel_col": sel_col,
        "head_sum": (p[:, None] // DK == p[None] % HH).astype(f),
        "head_mean": (p[:, None] % HH == p[None] % HH).astype(f) / f(DV),
        "pair_mean": (p[:, None] // HD == p[None] // HD).astype(f) / f(HD),
        "causal": (p[None] >= p[:, None]).astype(f),
        "cos": cos.astype(f), "sin": sin.astype(f), "pow": pw.astype(f),
    }
    layout = {"weights": {n: w.shape[1:] for n, w in weights.items()},
              "vectors": {n: v.shape[1] for n, v in vectors.items()},
              "consts": {n: c.shape[1:] for n, c in consts.items()}}

    nc = bacc.Bacc("TRN2", target_bir_lowering=False, num_devices=1)
    arrays = {}

    def dram(name, arr):
        arrays[name] = arr
        return nc.dram_tensor(name, arr.shape, mb.dt.from_np(arr.dtype), kind="ExternalInput").ap()

    x_in = dram("x_in", np.ascontiguousarray(a["attn_a_x"]))
    ws = {n: dram("w_in_" + n, w) for n, w in weights.items()}
    vs = {n: dram("v_in_" + n, v) for n, v in vectors.items()}
    bias = dram("bias_in", np.ascontiguousarray(a["ffn_bias"]))
    cs = {n: dram("c_in_" + n, c) for n, c in consts.items()}
    out = nc.dram_tensor("out", (B, T, H), mb.dt.float32, kind="ExternalOutput").ap()
    hybrid_block(nc, x_in, ws, vs, bias, cs, out, layout)
    r = run_bass_kernel_spmd(nc, [arrays], core_ids=[0])
    return r.results[0]["out"]
```

```python
from contextlib import ExitStack

import concourse.bass as bass
from concourse import mybir

ALU = mybir.AluOpType
ACT = mybir.ActivationFunctionType
F32 = mybir.dt.float32
F32R = mybir.dt.float32r

P = 128
B, T, H = 4, 512, 512
TT = T // P
CC = H // P
NH, DK, DV = 16, 16, 16
KD = NH * DK
HF = KD // P
HH = NH // HF
R = 64
MR, MW, MK, MV, MG = range(5)
ORDER = (MK, MV, MW, MR, MG)
NHB, HD = 8, 64
PAIRS = NHB // 2
ROT = 32
EPS = 1e-5
RING = 4
KV_RING = 2
LO, UP = slice(0, R), slice(R, P)
AT_AT = [0, 4 * P, 7 * P, 9 * P]


class Signal:

    def __init__(self, ctx, nc, name, per, started):
        self.sem = ctx.enter_context(nc.semaphore(name))
        self.per = per
        started.append(self)

    def at(self, i, k, turns=0):
        assert 1 <= k <= self.per, (self.per, k)
        return (i + (1 + turns)) * self.per + k

    def before(self, i, k):
        assert 1 <= k <= self.per, (self.per, k)
        return i * self.per + k


class Banks:

    def __init__(self, banks):
        self.banks, self.order, self.place = banks, [], {}

    def group(self, key, reader, k, lag=0):
        self.place[key] = len(self.order)
        self.order.append((reader, k, lag))

    def bank(self, key):
        return self.banks[self.place[key] % len(self.banks)]

    def open(self, pe, i, key):
        n, size = self.place[key], len(self.banks)
        lag = self.order[n][2]
        for back in range(3):
            same_bank = [m for m in range(n % size, len(self.order), size) if back or m < n]
            for m in reversed(same_bank):
                reader, k, lag_m = self.order[m]
                turns = lag - lag_m - back
                if isinstance(i, int) and not 0 <= i + turns < B:
                    continue
                pe.wait_ge(reader.sem, reader.at(i, k, turns))
                return self.bank(key)
        return self.bank(key)


def hybrid_block(nc, x_in, weights, vectors, ffn_bias, consts, out, layout):
    with ExitStack() as ctx:
        psum = [ctx.enter_context(nc.psum_tensor(f"bank{n}", [P, 512], F32)) for n in range(8)]

        def sb(name, shape, dt=F32, ctx=ctx):
            return ctx.enter_context(nc.sbuf_tensor(name, shape, dt))

        x = sb("x", [P, B * TT, H])
        wq = sb("wq", [P, CC, H], F32R)
        xh = sb("xh", [P, TT, H])
        hiT = sb("hiT", [P, CC, T], F32R)
        loT = sb("loT", [P, CC, T], F32R)
        tmp = sb("tmp", [P, 2, T])
        V = {n: sb("v_" + n, [P, s]) for n, s in layout["vectors"].items()}
        ident = sb("ident", [P, P])
        bias_rows = sb("bias_rows", [P, H], F32R)
        two_rows = sb("two_rows", [P, P], F32R)
        eps_t = sb("eps_t", [P, 1])
        one_t = sb("one_t", [P, 1])
        mhalf = sb("mhalf", [P, TT])
        eps4 = sb("eps4", [P, TT])
        minus4 = sb("minus4", [P, TT])
        var_scale = sb("var_scale", [P, TT])
        var_shift = sb("var_shift", [P, TT])
        scratch = sb("scratch", [P, 64])
        scratch_act = sb("scratch_act", [P, 8])
        wabs = sb("wabs", [P, 1])
        thr = sb("thr", [P, 2])
        stats = sb("stats", [P, TT, 6])
        mv = sb("mv", [P, TT, 2])
        sc = sb("sc", [P, 4, TT])

        def shape_of(n, kind="weights"):
            return [P, *layout[kind][n]]

        part_a = ExitStack()

        def sba(name, shape, dt=F32):
            return sb(name, shape, dt, part_a)

        WA = {n: sba("w_" + n, shape_of(n)) for n in ("wx1", "wr", "wk", "wv", "ab_a", "wo_a")}
        wx2_hi, wx2_lo = (sba("wx2_" + s, shape_of("wx2"), F32R) for s in ("hi", "lo"))
        abb_hi, abb_lo = (sba("abb_" + s, shape_of("ab_b"), F32R) for s in ("hi", "lo"))
        sel_row = sba("sel_row", shape_of("sel_row", "consts"), F32R)
        CA = {n: sba("c_" + n, shape_of(n, "consts")) for n in ("sel_col", "head_sum", "head_mean", "head_center")}
        xnT = sba("xnT", [P, CC, T + 1])
        delta = sba("delta", [P, CC, T])
        xm = [sba(f"xm{n}", [P, CC, T]) for n in range(2)]
        lr4 = sba("lr4", [P, T], F32R)
        lowS = sba("lowS", [P, 2, T], F32R)
        kT, rT, dT, sg, vT = (sba(n, [P, HF, T]) for n in ("kT", "rT", "dT", "sg", "vT"))
        kv = sba("kv", [P, KV_RING, T])
        St = sba("St", [P, RING, T + 1])
        rS = sba("rS", [P, RING, T])
        oc = sba("oc", [P, T])
        sq = sba("sq", [P, T])
        part_a.close()
        bv = vT

        def lrS(n):
            return lr4[:] if n == 4 else hiT[:, n, :]

        def vS(hf, a):
            return loT[:, 2 * hf + a, :]

        part_b = ExitStack()

        def sbb(name, shape, dt=F32):
            return sb(name, shape, dt, part_b)

        WB = {n: (sbb(f"{n}_hi", shape_of(n), F32R), sbb(f"{n}_lo", shape_of(n), F32R)) for n in ("q_b", "k_b", "v_b", "g_b")}
        wo_b = sbb("wo_b", shape_of("o_b"))
        CB = {n: sbb("c_" + n, shape_of(n, "consts")) for n in ("cos", "sin", "grow", "shrink", "causal", "pair_mean")}
        qT = sbb("qT", [P, 2, T])
        kz = sbb("kz", [P, 2, 2, T])
        vB = sbb("vB", [P, TT, H])
        mish = sbb("mish", [P, CC, T])
        retT = sbb("retT", [P, CC, T])
        AT = [sbb(f"AT{n}", [P, 10 * P]) for n in range(2)]
        gst = sbb("gst", [P, CC, 6])
        gmv = sbb("gmv", [P, CC, 2])
        gs = sbb("gs", [P, CC, 2])
        gc = sbb("gc", [P, 6, CC])
        part_b.close()
        ffn_val = [AT[u][:, 0:CC * T // 2].rearrange("p (c t) -> p c t", c=CC) for u in range(2)]
        raw = {"q_b": mish, "k_b": retT, "v_b": vB, "g_b": mish}

        def sem(name):
            return ctx.enter_context(nc.semaphore(name))

        started = []

        def signal(name, per):
            return Signal(ctx, nc, name, per, started)

        loaded, x_loaded, head_start = sem("weights_loaded"), sem("x_loaded"), sem("head_start")
        consts_set, abs_summed, abs_total = sem("consts_set"), sem("abs_summed"), sem("abs_total")
        mhalf_set = sem("mhalf_set")
        wq_step, wq_ready, split_hi, split_lo = sem("wq_step"), sem("wq_ready"), sem("split_hi"), sem("split_lo")
        b_loaded, raw_loaded, b_hi, b_lo, kz_zero = sem("b_loaded"), sem("raw_loaded"), sem("b_hi"), sem("b_lo"), sem("kz_zero")
        x_stored = sem("x_stored")

        class Norm:

            def __init__(self, name, double):
                self.double = double
                self.stats_step = signal(name + "_stats_step", TT)
                self.mv_ready = signal(name + "_mv_ready", TT)
                self.step = signal(name + "_ln_step", 4 if double else 3)
                self.scale = signal(name + "_ln_scale", 1)
                self.xh_ready = signal(name + "_xh_ready", TT)
                self.xT_psum = signal(name + "_xT_psum", CC)
                self.out_psum = signal(name + "_out_psum", TT)
                self.x_added = signal(name + "_x_added", TT)

        NA, NF1, NB, NF2 = Norm("a", False), Norm("f1", True), Norm("b", False), Norm("f2", True)
        F_hi = {n: signal(s + "_hi", 2 * CC) for n, s in ((NF1, "f1"), (NF2, "f2"))}
        F_val = {n: signal(s + "_val", 2 * CC) for n, s in ((NF1, "f1"), (NF2, "f2"))}
        F_lo = {n: signal(s + "_lo", 4) for n, s in ((NF1, "f1"), (NF2, "f2"))}

        xn_ready = signal("xn_ready", CC)
        delta_ready = signal("delta_ready", CC)
        xx_ready = signal("xx_ready", CC)
        lr_psum = signal("lr_psum", 3)
        lr_val = signal("lr_val", 3)
        lr_hi = signal("lr_hi", 5)
        lr_lo = signal("lr_lo", 5)
        mus_psum = signal("mus_psum", 5 * CC)
        dm_ready = signal("dm_ready", 5 * CC)
        xm_ready = signal("xm_ready", 5 * CC)
        proj_psum = signal("proj_psum", 8)
        proj_ready = signal("proj_ready", 8)
        low_hi = signal("low_hi", 2)
        low_lo = signal("low_lo", 2)
        v_hi = signal("v_hi", 4)
        v_lo = signal("v_lo", 4)
        lowb_psum = signal("lowb_psum", 4)
        lowb_out = signal("lowb_out", 4)
        decay_ready = signal("decay_ready", HF)
        th_ready = signal("th_ready", HF)
        sg_ready = signal("sg_ready", HF)
        rk_ready = signal("rk_ready", HF)
        bonus_psum = signal("bonus_psum", HF)
        bv_ready = signal("bv_ready", HF)
        vb_psum = signal("vb_psum", HF * DV)
        kv_ready = signal("kv_ready", HF * DV)
        state_ready = signal("state_ready", HF * DV)
        rs_ready = signal("rs_ready", HF * DV)
        o_psum = signal("o_psum", HF * DV)
        o_ready = signal("o_ready", HF)
        cen_psum = signal("cen_psum", HF)
        oc_ready = signal("oc_ready", HF)
        sq_ready = signal("sq_ready", HF)
        var_psum = signal("var_psum", HF)
        rstd_step = signal("rstd_step", HF)
        rstd_ready = signal("rstd_ready", HF)
        on_ready = signal("on_ready", HF)
        on_scaled = signal("on_scaled", HF)
        og_ready = signal("og_ready", HF)

        n_hi = signal("n_hi", CC)
        n_lo = signal("n_lo", CC)
        qk_psum = signal("qk_psum", 2 * PAIRS)
        rot_cos = signal("rot_cos", 3 * PAIRS)
        rot_swap = signal("rot_swap", 2 * PAIRS)
        rot_sin = signal("rot_sin", 2 * PAIRS)
        qk_ready = signal("qk_ready", 3 * PAIRS)
        v_psum = signal("v_psum", TT)
        v_ready = signal("v_ready", TT)
        g_psum = signal("g_psum", CC)
        g_ready = signal("g_ready", CC)
        exp_ready = signal("exp_ready", CC)
        g_cut = signal("g_cut", CC)
        sp_ready = signal("sp_ready", CC)
        tanh_ready = signal("tanh_ready", CC)
        gate_ready = signal("gate_ready", CC)
        sc_psum = signal("sc_psum", NHB * TT)
        at_copied = signal("at_copied", NHB * TT)
        at_masked = signal("at_masked", NHB * TT)
        ret_psum = signal("ret_psum", PAIRS)
        ret_ready = signal("ret_ready", PAIRS)
        gst_step = signal("gst_step", 2 * CC)
        gn_in = signal("gn_in", PAIRS)
        gn_psum = signal("gn_psum", PAIRS)
        gn_out = signal("gn_out", PAIRS)
        gn_step = signal("gn_step", 6 * PAIRS)
        gn_coef = signal("gn_coef", PAIRS)
        y_norm = signal("y_norm", CC)
        y_ready = signal("y_ready", CC)

        pre = Banks(psum[0:3])
        main = Banks(psum[3:7])
        scan_sum = psum[7]
        QS = 4 * HF

        def lr_groups(m):
            pre.group(("lr", m), lr_hi, min(2 * m + 2, 5))

        pre.group(("proj", MG, 0), low_hi, 2, lag=1)
        for hf in range(HF):
            pre.group(("lowb", 1, hf), lowb_out, HF + hf + 1, lag=1)
        for c in range(CC):
            pre.group(("xT", c), xn_ready, c + 1)
        pre.group(("cen", 0), sq_ready, 1, lag=1)
        lr_groups(0)
        pre.group(("var", 0), rstd_step, 1, lag=1)
        lr_groups(1)
        lr_groups(2)
        for c in range(CC):
            pre.group(("mus", 0, c), dm_ready, c + 1)
        pre.group(("cen", 1), sq_ready, 2, lag=1)
        pre.group(("var", 1), rstd_step, 2, lag=1)
        for tt in range(TT):
            pre.group(("out", tt), NA.x_added, tt + 1, lag=1)
        for hf in range(HF):
            pre.group(("bonus", hf), bv_ready, hf + 1)

        proj_no = {(MK, 0): 1, (MK, 1): 2, (MV, 0): 3, (MV, 1): 4, (MW, 0): 5, (MR, 0): 6, (MR, 1): 7, (MG, 0): 8}

        def mus_groups(s):
            for c in range(CC):
                main.group(("mus", s, c), dm_ready, s * CC + c + 1)

        def proj_group(n, hf):
            if n == MW:
                main.group(("proj", n, hf), low_hi, 1)
            else:
                main.group(("proj", n, hf), proj_ready, proj_no[n, hf])

        def spread_groups(q):
            for g in range(4):
                main.group(("vb", 4 * q + g), kv_ready, 4 * q + g + 1)

        mus_groups(1)
        for s, n in ((2, MK), (3, MV)):
            for hf in range(HF):
                proj_group(n, hf)
            mus_groups(s)
        proj_group(MW, 0)
        mus_groups(4)
        proj_group(MR, 0)
        for hf in range(HF):
            main.group(("lowb", 0, hf), lowb_out, hf + 1)
        spread_groups(0)
        proj_group(MR, 1)
        for q in range(1, QS):
            spread_groups(q)

        ffn_banks = {}
        for norm in (NF1, NF2):
            b = ffn_banks[norm] = Banks(psum)
            for u in range(2):
                for k in range(2):
                    b.group(("xT", u, k), F_hi[norm], CC * u + 2 * k + 2)
                for tt in (2 * (1 - u), 2 * (1 - u) + 1):
                    b.group(("out", tt), norm.x_added, tt + 1, lag=1 - u)

        rb = Banks(psum)
        for c in range(CC):
            rb.group(("xT", c), n_lo, c + 1)
        rb.group(("gn", PAIRS - 1), gn_out, PAIRS, lag=1)
        for tt in range(TT):
            rb.group(("out", tt), NB.x_added, tt + 1, lag=1)

        def qk_groups(p):
            rb.group(("qk", p, 0), rot_swap, 2 * p + 1)
            rb.group(("qk", p, 1), rot_swap, 2 * p + 2)

        qk_groups(0)
        for tt in range(TT):
            rb.group(("v", tt), v_ready, tt + 1)
        for p in range(PAIRS):
            for e in range(2):
                for jt in range(TT):
                    rb.group(("sc", 2 * p + e, jt), at_copied, (2 * p + e) * TT + jt + 1)
            if p:
                rb.group(("gn", p - 1), gn_out, p)
            if p + 1 < PAIRS:
                qk_groups(p + 1)
            rb.group(("g", p), g_ready, p + 1)
            rb.group(("ret", p), ret_ready, p + 1)

        wmean = St[:, 0, 0:P]
        wq_raw = xh
        wlow = delta
        abb_raw, sel_raw, bias_raw, two_raw = xm[1][:, 0, :], xm[1][:, 1:3, :], xm[1][0:2, 3, :], kT[:, 0, 0:P]
        n_loads = layout["n_loads"]
        block = ctx.enter_context(nc.Block())

        def rows_of(dram, i):
            return dram[bass.ds(i, 1)].rearrange("b (t p) h -> p (b t) h", p=P)

        @block.sync
        def _(sp):
            sp.dma_start(x[:], x_in.rearrange("b (t p) h -> p (b t) h", p=P)).then_inc(x_loaded, 16)
            for n in V:
                sp.dma_start(V[n][:], vectors[n]).then_inc(loaded, 16)
            sp.dma_start(ident[:], consts["ident"]).then_inc(loaded, 16)
            sp.dma_start(wq_raw[:], weights["wq"]).then_inc(loaded, 16)
            sp.dma_start(xm[0][:], weights["wx2"][:, 0:4, :]).then_inc(loaded, 16)
            sp.dma_start(rS[:, 0, :], weights["wx2"][:, 4, :]).then_inc(loaded, 16)
            sp.dma_start(abb_raw, weights["ab_b"].rearrange("p a b -> p (a b)")).then_inc(loaded, 16)
            sp.dma_start(sel_raw, consts["sel_row"].rearrange("p (a b) c -> p a (b c)", a=2)).then_inc(loaded, 16)
            sp.dma_start(bias_raw, ffn_bias.rearrange("(a n) -> a n", a=1).to_broadcast([2, H])).then_inc(loaded, 16)
            sp.dma_start(two_raw, consts["two_rows"]).then_inc(loaded, 16)
            for n in WA:
                sp.dma_start(WA[n][:], weights[n]).then_inc(loaded, 16)
            for n in CA:
                sp.dma_start(CA[n][:], consts[n]).then_inc(loaded, 16)
            sp.wait_ge(NA.x_added.sem, NA.x_added.at(B - 1, TT))
            for m, n in enumerate(("q_b", "k_b", "v_b", "g_b")):
                if n == "g_b":
                    sp.wait_ge(b_lo, 1)
                sp.dma_start(raw[n][:], weights[n]).then_inc(raw_loaded, 16)
                sp.wait_ge(raw_loaded, 16 * (m + 1))
            sp.dma_start(wo_b[:], weights["o_b"]).then_inc(b_loaded, 16)
            for n in CB:
                sp.dma_start(CB[n][:], consts[n]).then_inc(b_loaded, 16)
            with sp.Fori(0, B) as i:
                sp.wait_ge(NF2.x_added.sem, NF2.x_added.at(i, TT))
                sp.dma_start(rows_of(out, i), x[:, bass.ds(i * TT, TT), :]).then_inc(x_stored, 16)
            sp.wait_ge(x_stored, 16 * B)

        @block.tensor
        def _(pe):
            pe.wait_ge(abs_summed, 1)
            pe.wait_ge(consts_set, 1)
            nc.tensor.matmul(psum[0][:, 0:1], wmean, wabs[:], start=True, stop=True).then_inc(abs_total, 1)
            pe.wait_ge(head_start, 1)
            pe.wait_ge(loaded, 16 * n_loads)
            pe.wait_ge(wq_ready, 1)
            pe.wait_ge(split_hi, 5)
            pe.wait_ge(split_lo, 4)

            def transposes(norm, banks, i):
                for c in range(CC):
                    dst = banks.open(pe, i, ("xT", c))
                    for tt in range(TT):
                        if c == 0:
                            pe.wait_ge(norm.xh_ready.sem, norm.xh_ready.at(i, tt + 1))
                        mm = nc.tensor.transpose(dst[:, tt * P:(tt + 1) * P], xh[:, tt, c * P:(c + 1) * P], ident[:])
                    mm.then_inc(norm.xT_psum.sem, 1)

            def three(dst, pairs):
                for n, (wh, wl, xa, xb) in enumerate(pairs):
                    nc.tensor.matmul(dst, wh, xa, start=(n == 0), stop=False)
                    nc.tensor.matmul(dst, wh, xb, start=False, stop=False)
                    mm = nc.tensor.matmul(dst, wl, xa, start=False, stop=(n == len(pairs) - 1))
                return mm

            def mix(s, i):
                n, banks = ORDER[s], main if s else pre
                pe.wait_ge(lr_hi.sem, lr_hi.at(i, n + 1))
                pe.wait_ge(lr_lo.sem, lr_lo.at(i, n + 1))
                for c in range(CC):
                    dst = banks.open(pe, i, ("mus", s, c))
                    nc.tensor.matmul(dst[:], wx2_hi[:, n, c * P:(c + 1) * P], lrS(n), start=True, stop=False)
                    nc.tensor.matmul(dst[:], wx2_lo[:, n, c * P:(c + 1) * P], lrS(n), start=False, stop=True)\
                        .then_inc(mus_psum.sem, 1)

            def low_rank(m, i):
                dst = pre.open(pe, i, ("lr", m))
                w = P if m < 2 else R
                for c in range(CC):
                    if m == 0:
                        pe.wait_ge(xx_ready.sem, xx_ready.at(i, c + 1))
                    mm = nc.tensor.matmul(dst[0:w, :], WA["wx1"][:, c, m * P:m * P + w], xm[1][:, c, :],
                                          start=(c == 0), stop=(c == CC - 1))
                mm.then_inc(lr_psum.sem, 1)

            def project(s, hf, i):
                n = ORDER[s]
                dst = (pre if n == MG else main).open(pe, i, ("proj", n, hf))
                for c in range(CC):
                    if hf == 0:
                        pe.wait_ge(xm_ready.sem, xm_ready.at(i, s * CC + c + 1))
                    if n in (MW, MG):
                        o, w = dst[0:R, :], WA["ab_a"][:, c, LO if n == MW else UP]
                    else:
                        o, w = dst[:], WA[{MR: "wr", MK: "wk", MV: "wv"}[n]][:, c, hf * P:(hf + 1) * P]
                    mm = nc.tensor.matmul(o, w, xm[s % 2][:, c, :], start=(c == 0), stop=(c == CC - 1))
                mm.then_inc(proj_psum.sem, 1)

            def low_b(j, i):
                pe.wait_ge(low_lo.sem, low_lo.at(i, j + 1))
                for hf in range(HF):
                    dst = (pre if j else main).open(pe, i, ("lowb", j, hf))
                    cols = slice(hf * P, (hf + 1) * P)
                    nc.tensor.matmul(dst[:], abb_hi[:, j, cols], lowS[:, j, :], start=True, stop=False)
                    nc.tensor.matmul(dst[:], abb_lo[:, j, cols], lowS[:, j, :], start=False, stop=True).then_inc(lowb_psum.sem, 1)

            def spread_v(q, i):
                hf = q // 4
                for g in range(4):
                    dv = 4 * g + q % 4
                    dst = main.open(pe, i, ("vb", 4 * q + g))
                    if q % 4 == 0 and g in (0, 2):
                        pe.wait_ge(v_lo.sem, v_lo.at(i, 2 * hf + g // 2 + 1))
                        pe.wait_ge(v_hi.sem, v_hi.at(i, 2 * hf + g // 2 + 1))
                    nc.tensor.matmul(dst[:], sel_row[:, dv % 8, :], vS(hf, dv // 8), start=True, stop=True).then_inc(vb_psum.sem, 1)

            def quarter(q, i):
                if q + 1 < QS:
                    spread_v(q + 1, i)
                if q == 0:
                    pe.wait_ge(o_ready.sem, o_ready.before(i, HF))
                if q == 4:
                    pe.wait_ge(o_ready.sem, o_ready.at(i, 1))
                for g in range(4):
                    pe.wait_ge(rs_ready.sem, rs_ready.at(i, 4 * q + g + 1))
                    nc.tensor.matmul(scan_sum[32 * g:32 * g + 32, :], CA["sel_col"][:, q % 4, :], rS[:, g, :],
                                     start=(q % 4 == 0), stop=(q % 4 == 3)).then_inc(o_psum.sem, 1)

            def one_group(key, sig, w, act_in, sig_in, k, i):
                dst = pre.open(pe, i, key)
                pe.wait_ge(sig_in.sem, sig_in.at(i, k))
                nc.tensor.matmul(dst[:], w[:], act_in, start=True, stop=True).then_inc(sig.sem, 1)

            def center(hf, i):
                one_group(("cen", hf), cen_psum, CA["head_center"], bv[:, hf, :], o_ready, hf + 1, i)

            def variance(hf, i):
                one_group(("var", hf), var_psum, CA["head_mean"], sq[:], sq_ready, hf + 1, i)

            def project_out(tt, i):
                dst = pre.open(pe, i, ("out", tt))
                for hf in range(HF):
                    if tt == 0:
                        pe.wait_ge(og_ready.sem, og_ready.at(i, hf + 1))
                    mm = nc.tensor.matmul(dst[:], sg[:, hf, tt * P:(tt + 1) * P], WA["wo_a"][:, hf, :],
                                          start=(hf == 0), stop=(hf == HF - 1))
                mm.then_inc(NA.out_psum.sem, 1)

            def first(i):
                transposes(NA, pre, i)
                for m in range(3):
                    low_rank(m, i)
                mix(0, i)

            def open_row(i, last):
                mix(1, i)
                project(0, 0, i)
                if last is not None:
                    center(1, last)
                project(0, 1, i)
                if last is not None:
                    variance(1, last)
                mix(2, i)
                project(1, 0, i)
                project(1, 1, i)
                mix(3, i)
                project(2, 0, i)
                mix(4, i)
                project(3, 0, i)
                low_b(0, i)
                spread_v(0, i)
                project(3, 1, i)
                if last is not None:
                    project_out(0, last)
                    project_out(1, last)
                quarter(0, i)
                if last is not None:
                    project_out(2, last)
                    project_out(3, last)
                quarter(1, i)
                for hf in range(HF):
                    one_group(("bonus", hf), bonus_psum, CA["head_sum"], sq[:] if hf else oc[:], rk_ready, hf + 1, i)

            def close_row(i, following):
                more = following is not None
                quarter(2, i)
                project(4, 0, i)
                low_b(1, i)
                quarter(3, i)
                if more:
                    transposes(NA, pre, following)
                quarter(4, i)
                center(0, i)
                if more:
                    low_rank(0, following)
                quarter(5, i)
                variance(0, i)
                if more:
                    low_rank(1, following)
                quarter(6, i)
                if more:
                    low_rank(2, following)
                quarter(7, i)
                if more:
                    mix(0, following)

            first(0)
            open_row(0, None)
            with pe.Fori(0, B - 1) as i:
                close_row(i, i + 1)
                open_row(i + 1, i)
            close_row(B - 1, None)
            center(1, B - 1)
            variance(1, B - 1)
            for tt in range(TT):
                project_out(tt, B - 1)

            def unit_transposes(norm, u, i):
                for k in range(2):
                    dst = ffn_banks[norm].open(pe, i, ("xT", u, k))
                    for n in range(4):
                        c, tt = 2 * k + n // 2, 2 * u + n % 2
                        if k == 0 and n < 2:
                            pe.wait_ge(norm.xh_ready.sem, norm.xh_ready.at(i, tt + 1))
                        mm = nc.tensor.transpose(dst[:, n * P:(n + 1) * P], xh[:, tt, c * P:(c + 1) * P], ident[:])
                    mm.then_inc(norm.xT_psum.sem, 1)

            def unit_products(norm, u, i):
                for tt in (2 * u, 2 * u + 1):
                    dst = ffn_banks[norm].open(pe, i, ("out", tt))
                    nc.tensor.matmul(dst[:], two_rows[:], bias_rows[:], start=True, stop=False)
                    for c in range(CC):
                        if tt == 2 * u and c % 2 == 0:
                            pe.wait_ge(F_hi[norm].sem, F_hi[norm].at(i, CC * u + c + 2))
                            pe.wait_ge(F_lo[norm].sem, F_lo[norm].at(i, 2 * u + c // 2 + 1))
                        nc.tensor.matmul(dst[:], hiT[:, c, tt * P:(tt + 1) * P], wq[:, c, :], start=False, stop=False)
                        mm = nc.tensor.matmul(dst[:], loT[:, c, tt * P:(tt + 1) * P], wq[:, c, :], start=False, stop=(c == CC - 1))
                    mm.then_inc(norm.out_psum.sem, 1)

            def ffn(norm):
                unit_transposes(norm, 0, 0)
                with pe.Fori(0, B - 1) as i:
                    unit_transposes(norm, 1, i)
                    unit_products(norm, 0, i)
                    unit_transposes(norm, 0, i + 1)
                    unit_products(norm, 1, i)
                unit_transposes(norm, 1, B - 1)
                unit_products(norm, 0, B - 1)
                unit_products(norm, 1, B - 1)

            pe.wait_ge(NA.x_added.sem, NA.x_added.at(B - 1, TT))
            ffn(NF1)

            def tiles(w, cols):
                return [(w[0][:, c, cols], w[1][:, c, cols], hiT[:, c, :], loT[:, c, :]) for c in range(CC)]

            def qk(p, i):
                for j in range(2):
                    dst = rb.open(pe, i, ("qk", p, j))
                    three(dst[:], tiles(WB[("k_b", "q_b")[j]], slice(p * P, (p + 1) * P))).then_inc(qk_psum.sem, 1)

            def head_norm(p, i):
                dst = rb.open(pe, i, ("gn", p))
                pe.wait_ge(gn_in.sem, gn_in.at(i, p + 1))
                nc.tensor.matmul(dst[:, 0:2], CB["pair_mean"][:], gmv[:, p, :], start=True, stop=True).then_inc(gn_psum.sem, 1)

            def heads(i):
                pe.wait_ge(n_hi.sem, n_hi.at(i, CC))
                pe.wait_ge(n_lo.sem, n_lo.at(i, CC))
                qk(0, i)
                for tt in range(TT):
                    dst = rb.open(pe, i, ("v", tt))
                    t = slice(tt * P, (tt + 1) * P)
                    three(dst[:], [(hiT[:, c, t], loT[:, c, t], WB["v_b"][0][:, c, :], WB["v_b"][1][:, c, :]) for c in range(CC)])\
                        .then_inc(v_psum.sem, 1)
                for p in range(PAIRS):
                    pe.wait_ge(qk_ready.sem, qk_ready.at(i, 3 * p + 3))
                    for e in range(2):
                        for jt in range(TT):
                            dst = rb.open(pe, i, ("sc", 2 * p + e, jt))
                            nc.tensor.matmul(dst[:, 0:T - jt * P], kz[:, p % 2, e, jt * P:(jt + 1) * P], qT[:, p % 2, jt * P:T],
                                             start=True, stop=True).then_inc(sc_psum.sem, 1)
                    if p:
                        head_norm(p - 1, i)
                    if p + 1 < PAIRS:
                        qk(p + 1, i)
                    dst = rb.open(pe, i, ("g", p))
                    three(dst[:], tiles(WB["g_b"], slice(p * P, (p + 1) * P))).then_inc(g_psum.sem, 1)
                    dst = rb.open(pe, i, ("ret", p))
                    if p == 0:
                        pe.wait_ge(v_ready.sem, v_ready.at(i, TT))
                    for jt in range(TT):
                        for e in range(2):
                            h = 2 * p + e
                            pe.wait_ge(at_masked.sem, at_masked.at(i, h * TT + jt + 1))
                            mm = nc.tensor.matmul(dst[64 * e:64 * e + 64, jt * P:T], vB[:, jt, h * HD:(h + 1) * HD],
                                                  AT[e][:, AT_AT[jt]:AT_AT[jt] + T - jt * P], start=(jt == 0), stop=(jt == TT - 1))
                    mm.then_inc(ret_psum.sem, 1)

            def project_out_b(i):
                for tt in range(TT):
                    dst = rb.open(pe, i, ("out", tt))
                    for c in range(CC):
                        if tt == 0:
                            pe.wait_ge(y_ready.sem, y_ready.at(i, c + 1))
                        mm = nc.tensor.matmul(dst[:], retT[:, c, tt * P:(tt + 1) * P], wo_b[:, c, :], start=(c == 0), stop=(c == CC - 1))
                    mm.then_inc(NB.out_psum.sem, 1)

            pe.wait_ge(NF1.x_added.sem, NF1.x_added.at(B - 1, TT))
            transposes(NB, rb, 0)
            pe.wait_ge(b_loaded, 16 * (1 + len(CB)))
            pe.wait_ge(b_hi, 4)
            pe.wait_ge(b_lo, 4)
            pe.wait_ge(kz_zero, 2)
            with pe.Fori(0, B - 1) as i:
                heads(i)
                transposes(NB, rb, i + 1)
                head_norm(PAIRS - 1, i)
                project_out_b(i)
            heads(B - 1)
            head_norm(PAIRS - 1, B - 1)
            project_out_b(B - 1)
            pe.wait_ge(NB.x_added.sem, NB.x_added.at(B - 1, TT))
            ffn(NF2)

        @block.scalar
        def _(act):
            def activation(dst, src, func, sig, **kw):
                nc.scalar.activation(dst, src, func, **kw).then_inc(sig.sem, 1)

            act.wait_ge(consts_set, 3)
            act.wait_ge(loaded, 16 * n_loads)
            nc.scalar.activation(wx2_hi[:, 0:4, :], xm[0][:], ACT.Copy).then_inc(split_hi, 1)
            nc.scalar.activation(wx2_hi[:, 4, :], rS[:, 0, :], ACT.Copy).then_inc(split_hi, 1)
            nc.scalar.activation(abb_hi[:].rearrange("p a b -> p (a b)"), abb_raw, ACT.Copy).then_inc(split_hi, 1)
            nc.scalar.activation(sel_row[:].rearrange("p (a b) c -> p a (b c)", a=2), sel_raw, ACT.Copy).then_inc(split_hi, 1)
            nc.scalar.activation(two_rows[:], two_raw, ACT.Copy).then_inc(split_hi, 1)
            act.wait_ge(head_start, 1)
            act.wait_ge(split_lo, 4)
            act.wait_ge(wq_ready, 1)

            act_spots = iter(range(8))

            def normalise(norm, i):
                at = next(act_spots)
                act.wait_ge(norm.scale.sem, norm.scale.at(i, 1))
                act.wait_ge(norm.xT_psum.sem, norm.xT_psum.before(i, CC))
                nc.scalar.activation(scratch_act[:, at:at + 1], eps_t[:], ACT.Copy)
                for tt in range(TT):
                    activation(xh[:, tt, :], x[:, bass.ds(i * TT + tt, 1), :].rearrange("p a h -> p (a h)"), ACT.Identity, norm.xh_ready,
                               scale=sc[:, 2, tt:tt + 1], bias=sc[:, 3, tt:tt + 1])

            def copy_xn(i):
                for c in range(CC):
                    act.wait_ge(NA.xT_psum.sem, NA.xT_psum.at(i, c + 1))
                    if c == 0:
                        act.wait_ge(xm_ready.sem, xm_ready.before(i, 5 * CC))
                    activation(xnT[:, c, 1:T + 1], pre.bank(("xT", c))[:], ACT.Copy, xn_ready)

            def low_rank(m, i):
                rows = slice(0, P if m < 2 else R)
                src = pre.bank(("lr", m))
                act.wait_ge(lr_psum.sem, lr_psum.at(i, m + 1))
                if m == 0:
                    act.wait_ge(sg_ready.sem, sg_ready.before(i, HF))
                if m == 2:
                    act.wait_ge(lr_lo.sem, lr_lo.at(i, 2))
                activation(tmp[rows, m % 2, :], src[rows, :], ACT.Tanh, lr_val)
                for e in range(2 if m < 2 else 1):
                    rows = (LO, UP)[e]
                    activation(lrS(2 * m + e)[rows, :], src[rows, :], ACT.Tanh, lr_hi)

            def projected(n, hf, i):
                act.wait_ge(proj_psum.sem, proj_psum.at(i, proj_no[n, hf]))
                src = (pre if n == MG else main).bank(("proj", n, hf))
                if n in (MW, MG):
                    j = 0 if n == MW else 1
                    if j == 0:
                        act.wait_ge(lr_lo.sem, lr_lo.at(i, 5))
                    activation(tmp[LO, j, :], src[LO, :], ACT.Tanh, proj_ready)
                    activation(lowS[LO, j, :], src[LO, :], ACT.Tanh, low_hi)
                    return
                activation({MR: rT, MK: kT, MV: vT}[n][:, hf, :], src[:], ACT.Copy, proj_ready)
                if n == MV:
                    act.wait_ge(proj_ready.sem, proj_ready.at(i, proj_no[n, hf]))
                    for a in range(2):
                        rows = (LO, UP)[a]
                        activation(vS(hf, a)[rows, :], vT[rows, hf, :], ACT.Copy, v_hi)

            def center(hf, i):
                act.wait_ge(cen_psum.sem, cen_psum.at(i, hf + 1))
                if hf:
                    act.wait_ge(og_ready.sem, og_ready.at(i, hf))
                activation(oc[:], pre.bank(("cen", hf))[:], ACT.Copy, oc_ready)
                activation(sq[:], pre.bank(("cen", hf))[:], ACT.Square, sq_ready)

            def rstd(hf, i):
                act.wait_ge(var_psum.sem, var_psum.at(i, hf + 1))
                activation(sq[:], pre.bank(("var", hf))[:], ACT.Ln, rstd_step, bias=eps_t[:, 0:1])
                act.wait_ge(rstd_step.sem, rstd_step.at(i, hf + 1))
                activation(sq[:], sq[:], ACT.Exp, rstd_ready, scale=-0.5)

            def scale_out(hf, i):
                act.wait_ge(on_ready.sem, on_ready.at(i, hf + 1))
                activation(oc[:], oc[:], ACT.Identity, on_scaled, scale=V["lnw"][:, 0:1], bias=V["lnb"][:, 0:1])

            def open_row(i, last):
                projected(MK, 0, i)
                if last is not None:
                    center(1, last)
                projected(MK, 1, i)
                if last is not None:
                    rstd(1, last)
                projected(MV, 0, i)
                projected(MV, 1, i)
                if last is not None:
                    scale_out(1, last)
                projected(MW, 0, i)
                projected(MR, 0, i)
                for hf in range(HF):
                    act.wait_ge(lowb_psum.sem, lowb_psum.at(i, hf + 1))
                    activation(dT[:, hf, :], main.bank(("lowb", 0, hf))[:], ACT.Exp, lowb_out, bias=V["bw"][:, hf:hf + 1])
                for hf in range(HF):
                    act.wait_ge(lowb_out.sem, lowb_out.at(i, hf + 1))
                    activation(dT[:, hf, :], dT[:, hf, :], ACT.Exp, decay_ready, scale=-1.0)
                projected(MR, 1, i)

            def close_row(i, following):
                more = following is not None
                projected(MG, 0, i)
                for hf in range(HF):
                    act.wait_ge(lowb_psum.sem, lowb_psum.at(i, HF + hf + 1))
                    activation(sg[:, hf, :], pre.bank(("lowb", 1, hf))[:], ACT.Identity, lowb_out, bias=V["bg"][:, hf:hf + 1])
                for hf in range(HF):
                    act.wait_ge(lowb_out.sem, lowb_out.at(i, HF + hf + 1))
                    activation(tmp[:, hf, :], sg[:, hf, :], ACT.Tanh, th_ready, scale=0.5)
                if more:
                    normalise(NA, following)
                    copy_xn(following)
                center(0, i)
                if more:
                    low_rank(0, following)
                rstd(0, i)
                if more:
                    low_rank(1, following)
                    low_rank(2, following)
                scale_out(0, i)

            normalise(NA, 0)
            copy_xn(0)
            for m in range(3):
                low_rank(m, 0)
            open_row(0, None)
            with act.Fori(0, B - 1) as i:
                close_row(i, i + 1)
                open_row(i + 1, i)
            close_row(B - 1, None)
            center(1, B - 1)
            rstd(1, B - 1)
            scale_out(1, B - 1)

            def unit(norm, u, i):
                half = slice(u * T // 2, (u + 1) * T // 2)
                for c in range(CC):
                    k = c // 2
                    src = ffn_banks[norm].bank(("xT", u, k))[:, (c % 2) * T // 2:(c % 2 + 1) * T // 2]
                    if c % 2 == 0:
                        act.wait_ge(norm.xT_psum.sem, norm.xT_psum.at(i, 2 * u + k + 1))
                        act.wait_ge(F_lo[norm].sem, F_lo[norm].before(i, 2 * u + k + 1))
                    if c == 0:
                        act.wait_ge(norm.out_psum.sem, norm.out_psum.before(i, 2 * u + 2))
                    kw = dict(scale=V["gamma"][:, c:c + 1], bias=V["beta"][:, c:c + 1])
                    activation(ffn_val[u][:, c, :], src, ACT.Identity, F_val[norm], **kw)
                    activation(hiT[:, c, half], src, ACT.Identity, F_hi[norm], **kw)

            def ffn(norm):
                normalise(norm, 0)
                unit(norm, 0, 0)
                with act.Fori(0, B - 1) as i:
                    unit(norm, 1, i)
                    normalise(norm, i + 1)
                    unit(norm, 0, i + 1)
                unit(norm, 1, B - 1)

            ffn(NF1)
            for m, n in enumerate(("q_b", "k_b", "v_b", "g_b")):
                act.wait_ge(raw_loaded, 16 * (m + 1))
                nc.scalar.activation(WB[n][0][:], raw[n][:], ACT.Copy).then_inc(b_hi, 1)
            act.wait_ge(b_loaded, 16 * (1 + len(CB)))

            def x_hi(i):
                for c in range(CC):
                    act.wait_ge(NB.xT_psum.sem, NB.xT_psum.at(i, c + 1))
                    activation(hiT[:, c, :], rb.bank(("xT", c))[:], ACT.Copy, n_hi)

            def heads(i, following):
                for tt in range(TT):
                    act.wait_ge(v_psum.sem, v_psum.at(i, tt + 1))
                    activation(vB[:, tt, :], rb.bank(("v", tt))[:], ACT.Copy, v_ready)
                for p in range(PAIRS):
                    for e in range(2):
                        h = 2 * p + e
                        if p > 0:
                            act.wait_ge(ret_psum.sem, ret_psum.at(i, p))
                        for jt in range(TT):
                            act.wait_ge(sc_psum.sem, sc_psum.at(i, h * TT + jt + 1))
                            activation(AT[e][:, AT_AT[jt]:AT_AT[jt] + T - jt * P], rb.bank(("sc", h, jt))[:, 0:T - jt * P], ACT.Identity,
                                       at_copied, scale=CB["shrink"][:, h * TT + jt:h * TT + jt + 1])
                    act.wait_ge(g_psum.sem, g_psum.at(i, p + 1))
                    activation(mish[:, p, :], rb.bank(("g", p))[:], ACT.Copy, g_ready)
                    th = retT[:, p, :]
                    act.wait_ge(g_cut.sem, g_cut.at(i, p + 1))
                    activation(th, th, ACT.Exp, exp_ready)
                    act.wait_ge(exp_ready.sem, exp_ready.at(i, p + 1))
                    activation(th, th, ACT.Ln, sp_ready, bias=one_t[:, 0:1])
                    act.wait_ge(sp_ready.sem, sp_ready.at(i, p + 1))
                    activation(th, th, ACT.Tanh, tanh_ready)
                    if p == 2 and following is not None:
                        normalise(NB, following)

            normalise(NB, 0)
            x_hi(0)
            with act.Fori(0, B - 1) as i:
                heads(i, i + 1)
                x_hi(i + 1)
            heads(B - 1, None)
            ffn(NF2)

        @block.vector
        def _(dve):
            spots = iter(range(64))

            def wait_apart(sem, value):
                at = next(spots)
                dve.wait_ge(sem, value)
                nc.vector.memset(scratch[:, at:at + 1], 0.0)

            def tensor_tensor(dst, a, b, op, sig):
                nc.vector.tensor_tensor(dst, a, b, op).then_inc(sig.sem, 1)

            def stt(dst, a, s, b, op0, op1, sig):
                nc.vector.scalar_tensor_tensor(dst, a, s, b, op0, op1).then_inc(sig.sem, 1)

            nc.vector.memset(wmean, 1.0 / (H * H)).then_inc(consts_set, 1)
            nc.vector.memset(eps_t[:], EPS).then_inc(consts_set, 1)
            nc.vector.memset(one_t[:], 1.0).then_inc(consts_set, 1)
            nc.vector.memset(xnT[:, :, 0:1], 0.0).then_inc(consts_set, 1)
            nc.vector.memset(bias_rows[:].bitcast(mybir.dt.uint32), 0).then_inc(consts_set, 1)
            dve.wait_ge(loaded, 16 * n_loads)
            nc.vector.tensor_reduce(wabs[:], wq_raw[:], mybir.AxisListType.XY, ALU.add, apply_absolute_value=True)\
                .then_inc(abs_summed, 1)
            dve.wait_ge(consts_set, 5)
            dve.wait_ge(split_hi, 5)
            nc.vector.tensor_copy(bias_rows[0:2, :], bias_raw).then_inc(split_lo, 1)
            nc.vector.tensor_tensor(wx2_lo[:, 0:4, :], xm[0][:], wx2_hi[:, 0:4, :].bitcast(F32), ALU.subtract).then_inc(split_lo, 1)
            nc.vector.tensor_tensor(wx2_lo[:, 4, :], rS[:, 0, :], wx2_hi[:, 4, :].bitcast(F32), ALU.subtract).then_inc(split_lo, 1)
            nc.vector.tensor_tensor(abb_lo[:].rearrange("p a b -> p (a b)"), abb_raw, abb_hi[:].rearrange("p a b -> p (a b)").bitcast(F32),
                                    ALU.subtract).then_inc(split_lo, 1)
            dve.wait_ge(split_lo, 4)
            nc.vector.scalar_tensor_tensor(bias_rows[0:2, :], bias_rows[0:2, :].bitcast(F32), V["minus_row1"][0:2, 0:1], bias_raw,
                                           ALU.mult, ALU.add).then_inc(wq_step, 1)
            dve.wait_ge(abs_total, 1)
            nc.vector.tensor_scalar(thr[:, 0:1], psum[0][:, 0:1], 1e-5, 0.5, ALU.add, ALU.mult).then_inc(wq_step, 1)
            dve.wait_ge(wq_step, 2)
            nc.vector.tensor_scalar(thr[:, 1:2], thr[:, 0:1], -1.0, None, ALU.mult).then_inc(wq_step, 1)
            dve.wait_ge(wq_step, 3)
            nc.vector.tensor_scalar(wlow[:], wq_raw[:], thr[:, 1:2], None, ALU.is_lt).then_inc(wq_step, 1)
            dve.wait_ge(wq_step, 4)
            nc.vector.scalar_tensor_tensor(wq[:], wq_raw[:], thr[:, 0:1], wlow[:], ALU.is_gt, ALU.subtract).then_inc(wq_ready, 1)
            dve.wait_ge(wq_ready, 1)
            dve.wait_ge(x_loaded, 16)
            dve.wait_ge(head_start, 1)

            def layer_norm(norm, i):
                wait_apart(norm.scale.sem, norm.scale.before(i, 1))
                for tt in range(TT):
                    nc.vector.bn_stats(stats[:, tt, :], x[:, bass.ds(i * TT + tt, 1), :].rearrange("p a h -> p (a h)")).then_inc(norm.stats_step.sem, 1)
                wait_apart(norm.stats_step.sem, norm.stats_step.at(i, TT))
                for tt in range(TT):
                    nc.vector.bn_aggr(mv[:, tt, :], stats[:, tt, :]).then_inc(norm.mv_ready.sem, 1)

            def add_to_x(norm, banks, i, tiles=range(TT)):
                for tt in tiles:
                    dve.wait_ge(norm.out_psum.sem, norm.out_psum.at(i, tt + 1))
                    row = x[:, bass.ds(i * TT + tt, 1), :].rearrange("p a h -> p (a h)")
                    tensor_tensor(row, banks.bank(("out", tt))[:], row, ALU.add, norm.x_added)

            def mix(s, i):
                n, banks = ORDER[s], main if s else pre
                for c in range(CC):
                    dve.wait_ge(mus_psum.sem, mus_psum.at(i, s * CC + c + 1))
                    stt(xm[s % 2][:, c, :], banks.bank(("mus", s, c))[:], V["xb"][:, n * CC + c:n * CC + c + 1], delta[:, c, :],
                        ALU.add, ALU.mult, dm_ready)

            def shift(i):
                dve.wait_ge(proj_psum.sem, proj_psum.before(i, proj_no[MR, 1]))
                for c in range(CC):
                    dve.wait_ge(xn_ready.sem, xn_ready.at(i, c + 1))
                    tensor_tensor(delta[:, c, :], xnT[:, c, 0:T], xnT[:, c, 1:T + 1], ALU.subtract, delta_ready)
                for c in range(CC):
                    dve.wait_ge(delta_ready.sem, delta_ready.at(i, c + 1))
                    stt(xm[1][:, c, :], delta[:, c, :], V["mu"][:, c:c + 1], xnT[:, c, 1:T + 1], ALU.mult, ALU.add, xx_ready)

            def low_rank_lo(ks, i):
                for k in ks:
                    m, rows = k // 2, (LO, UP)[k % 2]
                    dve.wait_ge(lr_val.sem, lr_val.at(i, m + 1))
                    dve.wait_ge(lr_hi.sem, lr_hi.at(i, k + 1))
                    tensor_tensor(lrS(k)[(UP, LO)[k % 2], :], tmp[rows, m % 2, :], lrS(k)[rows, :].bitcast(F32), ALU.subtract, lr_lo)

            def v_low(i):
                for k in range(4):
                    hf, a = k // 2, k % 2
                    rows = (LO, UP)[a]
                    dve.wait_ge(v_hi.sem, v_hi.at(i, k + 1))
                    tensor_tensor(vS(hf, a)[(UP, LO)[a], :], vT[rows, hf, :], vS(hf, a)[rows, :].bitcast(F32), ALU.subtract, v_lo)

            def low_b_lo(j, i):
                dve.wait_ge(low_hi.sem, low_hi.at(i, j + 1))
                tensor_tensor(lowS[UP, j, :], tmp[LO, j, :], lowS[LO, j, :].bitcast(F32), ALU.subtract, low_lo)

            def kv_product(m, i):
                dve.wait_ge(vb_psum.sem, vb_psum.at(i, m + 1))
                if m >= KV_RING:
                    dve.wait_ge(state_ready.sem, state_ready.at(i, m - KV_RING + 1))
                tensor_tensor(kv[:, m % KV_RING, :], main.bank(("vb", m))[:], kT[:, m // DV, :], ALU.mult, kv_ready)

            def scan(m, i):
                dve.wait_ge(kv_ready.sem, kv_ready.at(i, m + 1))
                if m % DV == 0:
                    dve.wait_ge(decay_ready.sem, decay_ready.at(i, m // DV + 1))
                if m >= RING:
                    dve.wait_ge(rs_ready.sem, rs_ready.at(i, m - RING + 1))
                nc.vector.tensor_tensor_scan(St[:, m % RING, 1:T + 1], dT[:, m // DV, :], kv[:, m % KV_RING, :], 0.0, ALU.mult, ALU.add)\
                    .then_inc(state_ready.sem, 1)

            def scans(ms, i):
                for m in ms:
                    if m == 0:
                        kv_product(0, i)
                    if m + 1 < HF * DV and m != 7:
                        kv_product(m + 1, i)
                    scan(m, i)

            def bonus(i):
                for hf in range(HF):
                    if hf == 0:
                        dve.wait_ge(proj_ready.sem, proj_ready.at(i, proj_no[MR, 1]))
                    stt((sq if hf else oc)[:], rT[:, hf, :], V["bonus"][:, hf:hf + 1], kT[:, hf, :], ALU.mult, ALU.mult, rk_ready)

            def bonus_times_v(i):
                for hf in range(HF):
                    dve.wait_ge(bonus_psum.sem, bonus_psum.at(i, hf + 1))
                    tensor_tensor(bv[:, hf, :], pre.bank(("bonus", hf))[:], vT[:, hf, :], ALU.mult, bv_ready)

            def gate(i):
                for hf in range(HF):
                    dve.wait_ge(th_ready.sem, th_ready.at(i, hf + 1))
                    stt(sg[:, hf, :], tmp[:, hf, :], 1.0, sg[:, hf, :], ALU.add, ALU.mult, sg_ready)

            def sum_up(hf, i):
                dve.wait_ge(o_psum.sem, o_psum.at(i, (hf + 1) * DV))
                dve.wait_ge(bv_ready.sem, bv_ready.at(i, hf + 1))
                tensor_tensor(bv[:, hf, :], scan_sum[:], bv[:, hf, :], ALU.add, o_ready)

            def times_rstd(hf, i):
                dve.wait_ge(rstd_ready.sem, rstd_ready.at(i, hf + 1))
                tensor_tensor(oc[:], oc[:], sq[:], ALU.mult, on_ready)

            def times_gate(hf, i):
                dve.wait_ge(on_scaled.sem, on_scaled.at(i, hf + 1))
                dve.wait_ge(sg_ready.sem, sg_ready.at(i, hf + 1))
                stt(sg[:, hf, :], oc[:], 0.5, sg[:, hf, :], ALU.mult, ALU.mult, og_ready)

            def open_row(i, last):
                if last is not None:
                    sum_up(1, last)
                mix(0, i)
                mix(1, i)
                mix(2, i)
                if last is not None:
                    times_rstd(1, last)
                mix(3, i)
                v_low(i)
                if last is not None:
                    times_gate(1, last)
                low_b_lo(0, i)
                mix(4, i)
                scans(range(0, 4), i)
                bonus(i)
                if last is not None:
                    add_to_x(NA, pre, last, (0, 1))
                scans(range(4, 8), i)
                if last is not None:
                    add_to_x(NA, pre, last, (2, 3))

            def close_row(i, following):
                more = following is not None
                kv_product(8, i)
                scans(range(8, 12), i)
                bonus_times_v(i)
                if more:
                    layer_norm(NA, following)
                scans(range(12, 14), i)
                low_b_lo(1, i)
                scans(range(14, 18), i)
                gate(i)
                sum_up(0, i)
                scans(range(18, 20), i)
                if more:
                    shift(following)
                scans(range(20, 28), i)
                if more:
                    low_rank_lo(range(4), following)
                times_rstd(0, i)
                scans(range(28, 32), i)
                if more:
                    low_rank_lo((4,), following)
                times_gate(0, i)

            nc.vector.memset(St[:, :, 0:1], 0.0).then_inc(wq_ready, 1)
            layer_norm(NA, 0)
            shift(0)
            low_rank_lo(range(5), 0)
            open_row(0, None)
            with dve.Fori(0, B - 1) as i:
                close_row(i, i + 1)
                open_row(i + 1, i)
            close_row(B - 1, None)
            sum_up(1, B - 1)
            times_rstd(1, B - 1)
            times_gate(1, B - 1)
            add_to_x(NA, pre, B - 1)

            def ffn(norm):
                layer_norm(norm, 0)
                layer_norm(norm, 1)
                with dve.Fori(0, B - 2) as i:
                    add_to_x(norm, ffn_banks[norm], i, (0, 1))
                    layer_norm(norm, i + 2)
                    add_to_x(norm, ffn_banks[norm], i, (2, 3))
                add_to_x(norm, ffn_banks[norm], B - 2)
                add_to_x(norm, ffn_banks[norm], B - 1)

            ffn(NF1)

            dve.wait_ge(NA.x_added.sem, NA.x_added.at(B - 1, TT))
            nc.vector.memset(kz[UP, :, 0, :], 0.0).then_inc(kz_zero, 1)
            nc.vector.memset(kz[LO, :, 1, :], 0.0).then_inc(kz_zero, 1)
            dve.wait_ge(b_loaded, 16 * (1 + len(CB)))
            dve.wait_ge(kz_zero, 2)
            swap = [k ^ 1 for k in range(32)]

            def rotate(p, i):
                s = p % 2
                for j in range(2):
                    m = 2 * p + j
                    src = rb.bank(("qk", p, j))
                    dve.wait_ge(qk_psum.sem, qk_psum.at(i, m + 1))
                    if p >= 2:
                        dve.wait_ge(sc_psum.sem, sc_psum.at(i, (2 * p - 2) * TT))
                    else:
                        dve.wait_ge(sc_psum.sem, sc_psum.before(i, NHB * TT))
                    if j == 1:
                        tensor_tensor(qT[:, s, :], src[:], CB["cos"][:, 0, :], ALU.mult, rot_cos)
                    else:
                        for e in range(2):
                            rows = (LO, UP)[e]
                            tensor_tensor(kz[rows, s, e, :], src[rows, :], CB["cos"][rows, 1, :], ALU.mult, rot_cos)
                    if p >= 1:
                        wait_apart(qk_ready.sem, qk_ready.at(i, 3 * (p - 1) + 2 + j))
                    else:
                        wait_apart(qk_ready.sem, qk_ready.before(i, 3 * (PAIRS - 1) + 2 + j))
                    nc.vector.stream_shuffle(tmp[:, j, :], src[:], swap).then_inc(rot_swap.sem, 1)

            def x_lo(i):
                for c in range(CC):
                    dve.wait_ge(n_hi.sem, n_hi.at(i, c + 1))
                    tensor_tensor(loT[:, c, :], rb.bank(("xT", c))[:], hiT[:, c, :].bitcast(F32), ALU.subtract, n_lo)

            def head_sums(p, i):
                dve.wait_ge(gn_psum.sem, gn_psum.at(i, p + 1))
                nc.vector.tensor_copy(gs[:, p, :], rb.bank(("gn", p))[:, 0:2]).then_inc(gn_out.sem, 1)

            def cut_gate(p, i):
                dve.wait_ge(g_ready.sem, g_ready.at(i, p + 1))
                nc.vector.tensor_scalar(retT[:, p, :], mish[:, p, :], 30.0, None, ALU.min).then_inc(g_cut.sem, 1)

            def gate(p, i):
                dve.wait_ge(tanh_ready.sem, tanh_ready.at(i, p + 1))
                tensor_tensor(mish[:, p, :], mish[:, p, :], retT[:, p, :], ALU.mult, gate_ready)

            def gated(p, i):
                dve.wait_ge(gn_coef.sem, gn_coef.at(i, p + 1))
                nc.vector.tensor_scalar(retT[:, p, :], retT[:, p, :], gc[:, 4, p:p + 1], gc[:, 5, p:p + 1], ALU.mult, ALU.add)\
                    .then_inc(y_norm.sem, 1)
                dve.wait_ge(y_norm.sem, y_norm.at(i, p + 1))
                dve.wait_ge(gate_ready.sem, gate_ready.at(i, p + 1))
                tensor_tensor(retT[:, p, :], retT[:, p, :], mish[:, p, :], ALU.mult, y_ready)

            def heads(i, following):
                rotate(0, i)
                for p in range(PAIRS):
                    if p:
                        head_sums(p - 1, i)
                    if p + 1 < PAIRS:
                        rotate(p + 1, i)
                    cut_gate(p, i)
                    if p:
                        gated(p - 1, i)
                    if p == 1 and following is not None:
                        layer_norm(NB, following)
                    gate(p, i)
                    dve.wait_ge(ret_psum.sem, ret_psum.at(i, p + 1))
                    dve.wait_ge(gate_ready.sem, gate_ready.at(i, p + 1))
                    tensor_tensor(retT[:, p, :], rb.bank(("ret", p))[:], CB["grow"][:, p, :], ALU.mult, ret_ready)
                    dve.wait_ge(ret_ready.sem, ret_ready.at(i, p + 1))
                    nc.vector.bn_stats(gst[:, p, :], retT[:, p, :]).then_inc(gst_step.sem, 1)
                    wait_apart(gst_step.sem, gst_step.at(i, 2 * p + 1))
                    nc.vector.bn_aggr(gmv[:, p, :], gst[:, p, :]).then_inc(gst_step.sem, 1)
                    dve.wait_ge(gst_step.sem, gst_step.at(i, 2 * p + 2))
                    stt(gmv[:, p, 1:2], gmv[:, p, 0:1], gmv[:, p, 0:1], gmv[:, p, 1:2], ALU.mult, ALU.add, gn_in)
                if following is not None:
                    x_lo(following)
                head_sums(PAIRS - 1, i)
                gated(PAIRS - 1, i)
                add_to_x(NB, rb, i)

            dve.wait_ge(NF1.x_added.sem, NF1.x_added.at(B - 1, TT))
            layer_norm(NB, 0)
            x_lo(0)
            dve.wait_ge(b_lo, 4)
            with dve.Fori(0, B - 1) as i:
                heads(i, i + 1)
            heads(B - 1, None)
            ffn(NF2)

        @block.gpsimd
        def _(pool):
            for s in started:
                pool.sem_inc(s.sem, s.per)
            nc.gpsimd.memset(mhalf[:], -0.5).then_inc(mhalf_set, 1)
            nc.gpsimd.memset(eps4[:], EPS).then_inc(mhalf_set, 1)
            nc.gpsimd.memset(minus4[:], -1.0).then_inc(mhalf_set, 1)
            nc.gpsimd.memset(var_scale[:], 1.0 + EPS).then_inc(mhalf_set, 1)
            nc.gpsimd.memset(var_shift[:], EPS * EPS).then_inc(mhalf_set, 1)
            pool.wait_ge(mhalf_set, 5)
            pool.sem_inc(head_start, 1)

            def tensor_tensor(dst, a, b, op, sig):
                nc.gpsimd.tensor_tensor(dst, a, b, op).then_inc(sig.sem, 1)

            def ln_scales(norm, i):
                k = 0

                def step(*args):
                    nonlocal k
                    k += 1
                    tensor_tensor(*args, norm.step)
                    pool.wait_ge(norm.step.sem, norm.step.at(i, k))

                mean, var = mv[:, :, 0], mv[:, :, 1]
                a, nm, s, shift = (sc[:, n, :] for n in range(4))
                pool.wait_ge(norm.mv_ready.sem, norm.mv_ready.at(i, TT))
                pool.wait_ge(norm.xh_ready.sem, norm.xh_ready.before(i, TT))
                step(nm, mean, minus4[:], ALU.mult)
                if norm.double:
                    step(a, var, var_scale[:], ALU.mult)
                    step(a, a, var_shift[:], ALU.add)
                else:
                    step(a, var, eps4[:], ALU.add)
                step(s, a, mhalf[:], ALU.pow)
                tensor_tensor(shift, nm, s, ALU.mult, norm.scale)

            def mix(s, i):
                for c in range(CC):
                    pool.wait_ge(dm_ready.sem, dm_ready.at(i, s * CC + c + 1))
                    tensor_tensor(xm[s % 2][:, c, :], xm[s % 2][:, c, :], xnT[:, c, 1:T + 1], ALU.add, xm_ready)

            def times_r(ms, i):
                for m in ms:
                    pool.wait_ge(state_ready.sem, state_ready.at(i, m + 1))
                    if m >= RING:
                        pool.wait_ge(o_psum.sem, o_psum.at(i, m - RING + 1))
                    else:
                        pool.wait_ge(o_psum.sem, o_psum.before(i, HF * DV - RING + m + 1))
                    if m % DV == 0:
                        n = proj_no[MR, m // DV]
                        pool.wait_ge(proj_ready.sem, proj_ready.at(i, n))
                    tensor_tensor(rS[:, m % RING, :], St[:, m % RING, 0:T], rT[:, m // DV, :], ALU.mult, rs_ready)

            def open_row(i):
                for s in range(5):
                    mix(s, i)
                times_r(range(8), i)

            def close_row(i, following):
                times_r(range(8, 12), i)
                if following is not None:
                    ln_scales(NA, following)
                times_r(range(12, 32), i)

            pool.wait_ge(wq_ready, 2)
            ln_scales(NA, 0)
            open_row(0)
            with pool.Fori(0, B - 1) as i:
                close_row(i, i + 1)
                open_row(i + 1)
            close_row(B - 1, None)

            def unit(norm, u, i):
                half = slice(u * T // 2, (u + 1) * T // 2)
                for k in range(2):
                    cs = slice(2 * k, 2 * k + 2)
                    pool.wait_ge(F_val[norm].sem, F_val[norm].at(i, CC * u + 2 * k + 2))
                    pool.wait_ge(F_hi[norm].sem, F_hi[norm].at(i, CC * u + 2 * k + 2))
                    tensor_tensor(loT[:, cs, half], ffn_val[u][:, cs, :], hiT[:, cs, half].bitcast(F32), ALU.subtract, F_lo[norm])

            def ffn(norm):
                ln_scales(norm, 0)
                unit(norm, 0, 0)
                with pool.Fori(0, B - 1) as i:
                    ln_scales(norm, i + 1)
                    unit(norm, 1, i)
                    unit(norm, 0, i + 1)
                unit(norm, 1, B - 1)

            ffn(NF1)
            for m, n in enumerate(("q_b", "k_b", "v_b", "g_b")):
                pool.wait_ge(b_hi, m + 1)
                nc.gpsimd.tensor_tensor(WB[n][1][:], raw[n][:], WB[n][0][:].bitcast(F32), ALU.subtract).then_inc(b_lo, 1)
            pool.wait_ge(b_loaded, 16 * (1 + len(CB)))

            def rotate(p, i):
                s = p % 2
                for j in range(2):
                    m = 2 * p + j
                    pool.wait_ge(rot_swap.sem, rot_swap.at(i, m + 1))
                    tensor_tensor(tmp[:, j, :], tmp[:, j, :], CB["sin"][:, 1 - j, :], ALU.mult, rot_sin)
                    pool.wait_ge(rot_sin.sem, rot_sin.at(i, m + 1))
                    if j == 1:
                        tensor_tensor(qT[:, s, :], qT[:, s, :], tmp[:, 1, :], ALU.add, qk_ready)
                    else:
                        for e in range(2):
                            rows = (LO, UP)[e]
                            tensor_tensor(kz[rows, s, e, :], kz[rows, s, e, :], tmp[rows, 0, :], ALU.add, qk_ready)
                        pool.wait_ge(qk_ready.sem, qk_ready.at(i, 3 * p + 2))

            def head_coefficients(p, i):
                k = 6 * p

                def step(*args):
                    nonlocal k
                    k += 1
                    tensor_tensor(*args, gn_step)
                    pool.wait_ge(gn_step.sem, gn_step.at(i, k))

                at = slice(p, p + 1)
                mean, squares = gs[:, p, 0:1], gs[:, p, 1:2]
                pool.wait_ge(gn_out.sem, gn_out.at(i, p + 1))
                step(gc[:, 0, at], mean, mean, ALU.mult)
                step(gc[:, 1, at], squares, gc[:, 0, at], ALU.subtract)
                step(gc[:, 2, at], gc[:, 1, at], eps4[:, at], ALU.add)
                step(gc[:, 3, at], gc[:, 2, at], mhalf[:, at], ALU.pow)
                step(gc[:, 4, at], gc[:, 3, at], V["gnw"][:, at], ALU.mult)
                step(gc[:, 0, at], mean, gc[:, 4, at], ALU.mult)
                tensor_tensor(gc[:, 5, at], V["gnb"][:, at], gc[:, 0, at], ALU.subtract, gn_coef)

            def heads(i, following):
                rotate(0, i)
                for p in range(PAIRS):
                    for e in range(2):
                        h = 2 * p + e
                        for jt in range(TT):
                            pool.wait_ge(at_copied.sem, at_copied.at(i, h * TT + jt + 1))
                            blk = AT[e][:, AT_AT[jt]:AT_AT[jt] + P]
                            tensor_tensor(blk, blk, CB["causal"][:], ALU.mult, at_masked)
                    if p:
                        head_coefficients(p - 1, i)
                    if p + 1 < PAIRS:
                        rotate(p + 1, i)
                    if p == 1 and following is not None:
                        ln_scales(NB, following)
                head_coefficients(PAIRS - 1, i)

            ln_scales(NB, 0)
            with pool.Fori(0, B - 1) as i:
                heads(i, i + 1)
            heads(B - 1, None)
            ffn(NF2)


def kernel(**inputs):
    import numpy as np
    import concourse.bacc as bacc
    from concourse import mybir as mb
    from concourse.bass_utils import run_bass_kernel_spmd

    a = {k.replace("L0_", ""): np.asarray(v) for k, v in inputs.items()}

    def rows(w):
        return np.ascontiguousarray(w.reshape(-1, P, w.shape[1]).transpose(1, 0, 2))

    def cols(v):
        return np.ascontiguousarray(v.reshape(-1, P).T)

    def by_dv(w):
        return w.reshape(*w.shape[:-1], HF, HH, DV).swapaxes(-1, -2).reshape(w.shape)

    wx2 = a["attn_a_Wx2"].transpose(1, 2, 0)
    wx2 = np.concatenate([wx2, wx2], axis=1).transpose(1, 0, 2)
    qkv = a["attn_b_wqkv"].reshape(NHB, 3, HD, H)

    weights = {
        "wx1": rows(a["attn_a_Wx1"]), "wx2": np.ascontiguousarray(wx2),
        "wr": rows(a["attn_a_Wr"]), "wk": rows(a["attn_a_Wk"]), "wv": rows(by_dv(a["attn_a_Wv"])),
        "ab_a": rows(np.concatenate([a["attn_a_Ww_a"], a["attn_a_Wg_a"]], axis=1)),
        "ab_b": np.tile(np.stack([a["attn_a_Ww_b"], by_dv(a["attn_a_Wg_b"])], axis=1), (2, 1, 1)),
        "wo_a": rows(by_dv(a["attn_a_Wo"].T).T),
        "wq": rows(a["ffn_weight"].T),
        "q_b": rows(qkv[:, 0].reshape(-1, H).T), "k_b": rows(qkv[:, 1].reshape(-1, H).T), "v_b": rows(qkv[:, 2].reshape(-1, H).T),
        "g_b": rows(a["attn_b_wg"].T), "o_b": rows(a["attn_b_wo"].T),
    }
    vectors = {
        "mu": cols(a["attn_a_mu_x"]), "xb": cols(a["attn_a_x_bias"].reshape(-1)),
        "bw": cols(a["attn_a_bw"]), "bg": cols(by_dv(a["attn_a_bg"])), "bonus": cols(a["attn_a_bonus"].reshape(-1)),
        "lnw": np.repeat(a["attn_a_ln_w"], HH)[:, None].copy(), "lnb": np.repeat(a["attn_a_ln_b"], HH)[:, None].copy(),
        "minus_row1": -(np.arange(P) == 1).astype(np.float32)[:, None],
        "gamma": cols(a["ffn_ln_gamma"]), "beta": cols(a["ffn_ln_beta"]),
        "gnw": cols(np.repeat(a["attn_b_gn_weight"], HD)), "gnb": cols(np.repeat(a["attn_b_gn_bias"], HD)),
    }
    f = np.float32
    p = np.arange(P)
    sel_row = np.zeros((P, 8, P), f)
    sel_col = np.zeros((P, 4, 32), f)
    for h in range(HH):
        for d in range(8):
            sel_row[[8 * d + h, R + 8 * d + h], d, DK * h:DK * h + DK] = 1
        for q in range(4):
            sel_col[DK * h:DK * h + DK, q, 8 * q + h] = 1
    t = np.arange(T, dtype=np.float64)
    inv = 1.0 / 10000.0 ** (np.arange(0, ROT, 2) / ROT)
    fr = np.repeat(t[:, None] * inv[None], 2, axis=1)
    base = (np.arange(0, ROT, 2) + 0.4 * ROT) / (1.4 * ROT)
    scale = base[None] ** ((t - T // 2) / 512.0)[:, None]
    scale = np.concatenate([scale, scale], axis=1)
    sign = np.where(np.arange(ROT) % 2 == 0, -1.0, 1.0)
    cos, sin = np.zeros((P, 2, T)), np.zeros((P, 2, T))
    grow, shrink = np.zeros((P, PAIRS, T)), np.zeros((P, NHB * TT))
    for e in range(2):
        for j in range(2):
            s = scale if j == 0 else 1.0 / scale
            cos[HD * e:HD * e + ROT, j] = (np.cos(fr) * s).T
            sin[HD * e:HD * e + ROT, j] = (np.sin(fr) * s * sign).T
            cos[HD * e + ROT:HD * (e + 1), j] = 1
        for q in range(PAIRS):
            h = 2 * q + e
            gamma = 1.0 - 2.0 ** (-5.0 - h)
            grow[HD * e:HD * (e + 1), q] = gamma ** (t - T // 2)
            shrink[:, h * TT:(h + 1) * TT] = (gamma ** (T // 2 - t)).reshape(TT, P).T
    consts = {
        "ident": np.eye(P, dtype=f), "sel_row": sel_row, "sel_col": sel_col,
        "head_sum": (p[:, None] // DK == p[None] % HH).astype(f),
        "head_mean": (p[:, None] % HH == p[None] % HH).astype(f) / f(DV),
        "head_center": np.eye(P, dtype=f) - (p[:, None] % HH == p[None] % HH).astype(f) / f(DV),
        "pair_mean": (p[:, None] // HD == p[None] // HD).astype(f) / f(HD),
        "causal": (p[None] >= p[:, None]).astype(f),
        "two_rows": np.broadcast_to((p < 2)[:, None], (P, P)).astype(f),
        "cos": cos.astype(f), "sin": sin.astype(f), "grow": grow.astype(f), "shrink": shrink.astype(f),
    }
    layout = {"weights": {n: w.shape[1:] for n, w in weights.items()},
              "vectors": {n: v.shape[1] for n, v in vectors.items()},
              "consts": {n: c.shape[1:] for n, c in consts.items()},
              "n_loads": len(vectors) + 8 + 6 + 4}

    nc = bacc.Bacc("TRN2", target_bir_lowering=False, num_devices=1)
    arrays = {}

    def dram(name, arr):
        arrays[name] = arr
        return nc.dram_tensor(name, arr.shape, mb.dt.from_np(arr.dtype), kind="ExternalInput").ap()

    x_in = dram("x_in", np.ascontiguousarray(a["attn_a_x"]))
    ws = {n: dram("w_in_" + n, w) for n, w in weights.items()}
    vs = {n: dram("v_in_" + n, v) for n, v in vectors.items()}
    bias = dram("bias_in", np.ascontiguousarray(a["ffn_bias"]))
    cs = {n: dram("c_in_" + n, c) for n, c in consts.items()}
    out = nc.dram_tensor("out", (B, T, H), mb.dt.float32, kind="ExternalOutput").ap()
    hybrid_block(nc, x_in, ws, vs, bias, cs, out, layout)
    r = run_bass_kernel_spmd(nc, [arrays], core_ids=[0])
    return r.results[0]["out"]
```

```python
from contextlib import ExitStack

import concourse.bass as bass
from concourse import mybir

ALU = mybir.AluOpType
ACT = mybir.ActivationFunctionType
F32 = mybir.dt.float32
F32R = mybir.dt.float32r

P = 128
B, T, H = 4, 512, 512
TT = T // P
CC = H // P
NH, DK, DV = 16, 16, 16
KD = NH * DK
HF = KD // P
HH = NH // HF
R = 64
MR, MW, MK, MV, MG = range(5)
ORDER = (MK, MV, MW, MR, MG)
NHB, HD = 8, 64
PAIRS = NHB // 2
ROT = 32
EPS = 1e-5
RING = 4
KV_RING = 3
LO, UP = slice(0, R), slice(R, P)
AT_AT = [0, 4 * P, 7 * P, 9 * P]


class Signal:

    def __init__(self, ctx, nc, name, per, started):
        self.sem = ctx.enter_context(nc.semaphore(name))
        self.per = per
        started.append(self)

    def at(self, i, k, turns=0):
        assert 1 <= k <= self.per, (self.per, k)
        return (i + (1 + turns)) * self.per + k

    def before(self, i, k):
        assert 1 <= k <= self.per, (self.per, k)
        return i * self.per + k


class Banks:

    def __init__(self, banks):
        self.banks, self.order, self.place = banks, [], {}

    def group(self, key, reader, k, lag=0):
        self.place[key] = len(self.order)
        self.order.append((reader, k, lag))

    def bank(self, key):
        return self.banks[self.place[key] % len(self.banks)]

    def open(self, pe, i, key):
        n, size = self.place[key], len(self.banks)
        lag = self.order[n][2]
        for back in range(3):
            same_bank = [m for m in range(n % size, len(self.order), size) if back or m < n]
            for m in reversed(same_bank):
                reader, k, lag_m = self.order[m]
                turns = lag - lag_m - back
                if isinstance(i, int) and not 0 <= i + turns < B:
                    continue
                pe.wait_ge(reader.sem, reader.at(i, k, turns))
                return self.bank(key)
        return self.bank(key)


def hybrid_block(nc, x_in, weights, vectors, ffn_bias, consts, out, layout):
    with ExitStack() as ctx:
        psum = [ctx.enter_context(nc.psum_tensor(f"bank{n}", [P, 512], F32)) for n in range(8)]

        def sb(name, shape, dt=F32, ctx=ctx):
            return ctx.enter_context(nc.sbuf_tensor(name, shape, dt))

        x = sb("x", [P, B * TT, H])
        wq = sb("wq", [P, CC, H], F32R)
        xh = sb("xh", [P, TT, H])
        hiT = sb("hiT", [P, CC, T], F32R)
        loT = sb("loT", [P, CC, T], F32R)
        tmp = sb("tmp", [P, 2, T])
        vecs = sb("vecs", [P, layout["n_vectors"]])
        V = {n: vecs[:, a:b] for n, (a, b) in layout["vectors"].items()}
        ident = sb("ident", [P, P])
        bias_rows = sb("bias_rows", [P, H], F32R)
        two_rows = sb("two_rows", [P, P], F32R)
        eps_t = sb("eps_t", [P, 1])
        one_t = sb("one_t", [P, 1])
        mhalf = sb("mhalf", [P, TT])
        eps4 = sb("eps4", [P, TT])
        minus4 = sb("minus4", [P, TT])
        var_scale = sb("var_scale", [P, TT])
        var_shift = sb("var_shift", [P, TT])
        scratch = sb("scratch", [P, 64])
        scratch_act = sb("scratch_act", [P, 9])
        wabs = sb("wabs", [P, 1])
        thr = sb("thr", [P, 2])
        stats = sb("stats", [P, TT, 6])
        mv = sb("mv", [P, TT, 2])
        sc = sb("sc", [P, 4, TT])

        def shape_of(n, kind="weights"):
            return [P, *layout[kind][n]]

        part_a = ExitStack()

        def sba(name, shape, dt=F32):
            return sb(name, shape, dt, part_a)

        WA = {n: sba("w_" + n, shape_of(n)) for n in ("wx1", "wr", "wk", "wv", "ab_a", "wo_a")}
        wx2_hi, wx2_lo = (sba("wx2_" + s, shape_of("wx2"), F32R) for s in ("hi", "lo"))
        abb_hi, abb_lo = (sba("abb_" + s, shape_of("ab_b"), F32R) for s in ("hi", "lo"))
        sel_row = sba("sel_row", shape_of("sel_row", "consts"), F32R)
        CA = {n: sba("c_" + n, shape_of(n, "consts")) for n in ("sel_col", "head_sum", "head_mean", "head_center")}
        xnT = sba("xnT", [P, CC, T + 1])
        delta = sba("delta", [P, CC, T])
        xm = [sba(f"xm{n}", [P, CC, T]) for n in range(2)]
        lr4 = sba("lr4", [P, T], F32R)
        lowS = sba("lowS", [P, T], F32R)
        kT, rT, dT, sg, vT = (sba(n, [P, HF, T]) for n in ("kT", "rT", "dT", "sg", "vT"))
        kv = sba("kv", [P, KV_RING, T])
        St = sba("St", [P, RING, T + 1])
        rS = sba("rS", [P, RING, T])
        oc = sba("oc", [P, T])
        sq = sba("sq", [P, T])
        part_a.close()
        gate_tanh = xm[0]
        bv = vT

        def lrS(n):
            return lr4[:] if n == 4 else hiT[:, n, :]

        def vS(hf, a):
            return loT[:, 2 * hf + a, :]

        part_b = ExitStack()

        def sbb(name, shape, dt=F32):
            return sb(name, shape, dt, part_b)

        WB = {n: (sbb(f"{n}_hi", shape_of(n), F32R), sbb(f"{n}_lo", shape_of(n), F32R)) for n in ("q_b", "k_b", "v_b", "g_b")}
        wo_b = sbb("wo_b", shape_of("o_b"))
        cos_b = sbb("c_cos", shape_of("cos", "consts"))
        AT = [sbb(f"AT{n}", [P, 10 * P]) for n in range(2)]
        CB = {"cos": cos_b} | {n: sbb("c_" + n, shape_of(n, "consts")) for n in ("sin", "grow", "shrink", "causal", "pair_mean")}
        qT = sbb("qT", [P, 2, T])
        kz = sbb("kz", [P, 2, 2, T])
        vB = sbb("vB", [P, TT, H])
        mish = sbb("mish", [P, CC, T])
        retT = sbb("retT", [P, CC, T])
        gst = sbb("gst", [P, CC, 6])
        gmv = sbb("gmv", [P, CC, 2])
        gs = sbb("gs", [P, CC, 2])
        gc = sbb("gc", [P, 6, CC])
        part_b.close()
        ffn_val = [AT[u][:, 0:CC * T // 2].rearrange("p (c t) -> p c t", c=CC) for u in range(2)]
        raw = {"q_b": mish[:], "k_b": retT[:], "v_b": vB[:], "g_b": mish[:]}

        def sem(name):
            return ctx.enter_context(nc.semaphore(name))

        started = []

        def signal(name, per):
            return Signal(ctx, nc, name, per, started)

        loaded, x_loaded, head_start = sem("weights_loaded"), sem("x_loaded"), sem("head_start")
        x_half_loaded, wx2_loaded = sem("x_half_loaded"), sem("wx2_loaded")
        ident_loaded, vecs_loaded, wx1_loaded, wq_loaded = sem("ident_loaded"), sem("vecs_loaded"), sem("wx1_loaded"), sem("wq_loaded")
        consts_set, abs_summed, abs_total = sem("consts_set"), sem("abs_summed"), sem("abs_total")
        mhalf_set = sem("mhalf_set")
        wq_step, wq_ready, split_hi, split_lo = sem("wq_step"), sem("wq_ready"), sem("split_hi"), sem("split_lo")
        b_loaded, raw_loaded, b_hi, b_lo, kz_zero = sem("b_loaded"), sem("raw_loaded"), sem("b_hi"), sem("b_lo"), sem("kz_zero")
        x_stored = sem("x_stored")

        class Norm:

            def __init__(self, name, double):
                self.double = double
                self.stats_step = signal(name + "_stats_step", TT)
                self.mv_ready = signal(name + "_mv_ready", TT)
                self.step = signal(name + "_ln_step", 4 if double else 3)
                self.scale = signal(name + "_ln_scale", 1)
                self.xh_ready = signal(name + "_xh_ready", TT)
                self.xT_psum = signal(name + "_xT_psum", CC)
                self.out_psum = signal(name + "_out_psum", TT)
                self.x_added = signal(name + "_x_added", TT)

        NA, NF1, NB, NF2 = Norm("a", False), Norm("f1", True), Norm("b", False), Norm("f2", True)
        F_hi = {n: signal(s + "_hi", 2 * CC) for n, s in ((NF1, "f1"), (NF2, "f2"))}
        F_val = {n: signal(s + "_val", 2 * CC) for n, s in ((NF1, "f1"), (NF2, "f2"))}
        F_lo = {n: signal(s + "_lo", 4) for n, s in ((NF1, "f1"), (NF2, "f2"))}

        xn_ready = signal("xn_ready", CC)
        delta_ready = signal("delta_ready", CC)
        xx_ready = signal("xx_ready", CC)
        lr_psum = signal("lr_psum", 3)
        lr_val = signal("lr_val", 3)
        lr_hi = signal("lr_hi", 5)
        lr_lo = signal("lr_lo", 5)
        mus_psum = signal("mus_psum", 5 * CC)
        dm_ready = signal("dm_ready", 5 * CC)
        xm_ready = signal("xm_ready", 5 * CC)
        proj_psum = signal("proj_psum", 8)
        proj_ready = signal("proj_ready", 8)
        low_hi = signal("low_hi", 2)
        low_lo = signal("low_lo", 2)
        v_hi = signal("v_hi", 4)
        v_lo = signal("v_lo", 4)
        lowb_psum = signal("lowb_psum", 4)
        lowb_out = signal("lowb_out", 4)
        decay_ready = signal("decay_ready", HF)
        th_ready = signal("th_ready", HF)
        sg_ready = signal("sg_ready", HF)
        rk_ready = signal("rk_ready", HF)
        bonus_psum = signal("bonus_psum", HF)
        bv_ready = signal("bv_ready", HF)
        vb_psum = signal("vb_psum", HF * DV)
        kv_ready = signal("kv_ready", HF * DV)
        state_ready = signal("state_ready", HF * DV)
        rs_ready = signal("rs_ready", HF * DV)
        o_psum = signal("o_psum", HF * DV)
        o_ready = signal("o_ready", HF)
        cen_psum = signal("cen_psum", HF)
        oc_ready = signal("oc_ready", HF)
        sq_ready = signal("sq_ready", HF)
        var_psum = signal("var_psum", HF)
        rstd_step = signal("rstd_step", HF)
        rstd_ready = signal("rstd_ready", HF)
        on_ready = signal("on_ready", HF)
        on_scaled = signal("on_scaled", HF)
        og_ready = signal("og_ready", HF)

        n_hi = signal("n_hi", CC)
        n_lo = signal("n_lo", CC)
        qk_psum = signal("qk_psum", 2 * PAIRS)
        rot_cos = signal("rot_cos", 3 * PAIRS)
        rot_swap = signal("rot_swap", 2 * PAIRS)
        k_sin = signal("k_sin", PAIRS)
        q_sin = signal("q_sin", PAIRS)
        k_ready = signal("k_ready", 2 * PAIRS)
        q_ready = signal("q_ready", PAIRS)
        v_psum = signal("v_psum", TT)
        v_ready = signal("v_ready", TT)
        g_psum = signal("g_psum", CC)
        g_ready = signal("g_ready", CC)
        exp_ready = signal("exp_ready", CC)
        g_cut = signal("g_cut", CC)
        sp_ready = signal("sp_ready", CC)
        tanh_ready = signal("tanh_ready", CC)
        gate_ready = signal("gate_ready", CC)
        sc_psum = signal("sc_psum", NHB * TT)
        at_copied = signal("at_copied", NHB * TT)
        at_masked = signal("at_masked", NHB * TT)
        ret_psum = signal("ret_psum", PAIRS)
        ret_ready = signal("ret_ready", PAIRS)
        gst_step = signal("gst_step", 2 * CC)
        gn_in = signal("gn_in", PAIRS)
        gn_psum = signal("gn_psum", PAIRS)
        gn_out = signal("gn_out", PAIRS)
        gn_step = signal("gn_step", 6 * PAIRS)
        gn_coef = signal("gn_coef", PAIRS)
        y_norm = signal("y_norm", CC)
        y_ready = signal("y_ready", CC)

        pre = Banks(psum[0:3])
        main = Banks(psum[3:7])
        scan_sum = psum[7]
        QS = 4 * HF

        def lr_groups(m):
            pre.group(("lr", m), lr_hi, min(2 * m + 2, 5))

        for c in range(CC):
            pre.group(("xT", c), xn_ready, c + 1)
        pre.group(("proj", MG, 0), low_hi, 2, lag=1)
        for hf in range(HF):
            pre.group(("lowb", 1, hf), lowb_out, HF + hf + 1, lag=1)
        pre.group(("cen", 0), sq_ready, 1, lag=1)
        pre.group(("var", 0), rstd_step, 1, lag=1)
        for m in range(3):
            lr_groups(m)
        for c in range(CC):
            pre.group(("mus", 0, c), dm_ready, c + 1)
        pre.group(("cen", 1), sq_ready, 2, lag=1)
        pre.group(("var", 1), rstd_step, 2, lag=1)
        for tt in range(TT):
            pre.group(("out", tt), NA.x_added, tt + 1, lag=1)
        for hf in range(HF):
            pre.group(("bonus", hf), bv_ready, hf + 1)

        proj_no = {(MK, 0): 1, (MK, 1): 2, (MV, 0): 3, (MV, 1): 4, (MW, 0): 5, (MR, 0): 6, (MR, 1): 7, (MG, 0): 8}

        def mus_groups(s):
            for c in range(CC):
                main.group(("mus", s, c), dm_ready, s * CC + c + 1)

        def proj_group(n, hf):
            if n == MW:
                main.group(("proj", n, hf), low_hi, 1)
            else:
                main.group(("proj", n, hf), proj_ready, proj_no[n, hf])

        def spread_groups(q):
            for g in range(4):
                main.group(("vb", 4 * q + g), kv_ready, 4 * q + g + 1)

        mus_groups(1)
        for s, n in ((2, MK), (3, MV)):
            for hf in range(HF):
                proj_group(n, hf)
            mus_groups(s)
        proj_group(MW, 0)
        mus_groups(4)
        proj_group(MR, 0)
        for hf in range(HF):
            main.group(("lowb", 0, hf), lowb_out, hf + 1)
        spread_groups(0)
        proj_group(MR, 1)
        for q in range(1, QS):
            spread_groups(q)

        ffn_banks = {}
        for norm in (NF1, NF2):
            first = [3, 4, 5, 6, 7, 0, 1, 2] if norm is NF1 else [4, 7, 0, 1, 2, 3, 5, 6]
            b = ffn_banks[norm] = Banks([psum[n] for n in first])
            for u in range(2):
                for k in range(2):
                    b.group(("xT", u, k), F_hi[norm], CC * u + 2 * k + 2)
                for tt in (2 * (1 - u), 2 * (1 - u) + 1):
                    b.group(("out", tt), norm.x_added, tt + 1, lag=1 - u)

        rb = Banks([psum[n] for n in (3, 4, 7, 0, 1, 2, 5, 6)])
        for c in range(CC):
            rb.group(("xT", c), n_lo, c + 1)
        for tt in range(TT):
            rb.group(("out", tt), NB.x_added, tt + 1, lag=1)
        rb.group(("gn", PAIRS - 1), gn_out, PAIRS, lag=1)

        def qk_groups(p):
            rb.group(("qk", p, 0), rot_swap, 2 * p + 1)
            rb.group(("qk", p, 1), rot_swap, 2 * p + 2)

        qk_groups(0)
        for tt in range(TT):
            rb.group(("v", tt), v_ready, tt + 1)
        for p in range(PAIRS):
            if p + 1 < PAIRS:
                qk_groups(p + 1)
            else:
                rb.group(("g", p), g_ready, p + 1)
            for e in range(2):
                for jt in range(TT):
                    rb.group(("sc", 2 * p + e, jt), at_copied, (2 * p + e) * TT + jt + 1)
            if p:
                rb.group(("gn", p - 1), gn_out, p)
            if p + 1 < PAIRS:
                rb.group(("g", p), g_ready, p + 1)
            rb.group(("ret", p), ret_ready, p + 1)

        wmean = rS[:, 1, 0:P]
        wx2_raw, wq_raw = x[:, TT:TT + 5, :], x[:, 3 * TT:4 * TT, :]
        abb_raw, sel_raw = x[:, TT + 5, :], x[:, TT + 6:TT + 8, :]
        bias_raw, two_raw = rS[0:2, 0, :], kT[:, 0, 0:P]
        n_loads = len(WA) - 1 + len(CA) + 4
        block = ctx.enter_context(nc.Block())

        def rows_of(dram, i):
            return dram[bass.ds(i, 1)].rearrange("b (t p) h -> p (b t) h", p=P)

        def raise_signals(engine, places):
            for n, s in enumerate(started):
                if n % 8 in places:
                    engine.sem_inc(s.sem, s.per)

        @block.sync
        def _(sp):
            first_row = x_in[0:1].rearrange("b (t p) h -> p (b t) h", p=P)
            sp.dma_start(x[:, 0:TT // 2, :], first_row[:, 0:TT // 2, :]).then_inc(x_half_loaded, 16)
            sp.dma_start(x[:, TT // 2:TT, :], first_row[:, TT // 2:, :]).then_inc(x_loaded, 16)
            sp.dma_start(ident[:], consts["ident"]).then_inc(ident_loaded, 16)
            sp.dma_start(vecs[:], vectors).then_inc(vecs_loaded, 16)
            sp.dma_start(WA["wx1"][:], weights["wx1"]).then_inc(wx1_loaded, 16)
            sp.dma_start(wx2_raw, weights["wx2"]).then_inc(wx2_loaded, 16)
            for n in ("wk", "wv"):
                sp.dma_start(WA[n][:], weights[n]).then_inc(loaded, 16)
            sp.dma_start(abb_raw, weights["ab_b"].rearrange("p a b -> p (a b)")).then_inc(loaded, 16)
            for n in ("ab_a", "wr"):
                sp.dma_start(WA[n][:], weights[n]).then_inc(loaded, 16)
            sp.dma_start(sel_raw, consts["sel_row"].rearrange("p (a b) c -> p a (b c)", a=2)).then_inc(loaded, 16)
            for n in CA:
                sp.dma_start(CA[n][:], consts[n]).then_inc(loaded, 16)
            sp.dma_start(WA["wo_a"][:], weights["wo_a"]).then_inc(loaded, 16)
            sp.dma_start(bias_raw, ffn_bias.rearrange("(a n) -> a n", a=1).to_broadcast([2, H])).then_inc(loaded, 16)
            sp.dma_start(two_raw, consts["two_rows"]).then_inc(loaded, 16)
            sp.dma_start(wq_raw, weights["wq"]).then_inc(wq_loaded, 16)
            sp.wait_ge(split_hi, 4)
            sp.wait_ge(split_lo, 3)
            sp.wait_ge(wq_ready, 1)
            sp.dma_start(x[:, TT:, :], x_in[1:B].rearrange("b (t p) h -> p (b t) h", p=P)).then_inc(x_loaded, 16)
            sp.wait_ge(NA.x_added.sem, NA.x_added.at(B - 1, TT))
            for m, n in enumerate(("q_b", "k_b", "v_b", "g_b")):
                if n == "g_b":
                    for c in CB:
                        sp.dma_start(CB[c][:], consts[c]).then_inc(b_loaded, 16)
                    sp.dma_start(wo_b[:], weights["o_b"]).then_inc(b_loaded, 16)
                    sp.wait_ge(b_lo, 1)
                sp.dma_start(raw[n], weights[n]).then_inc(raw_loaded, 16)
                sp.wait_ge(raw_loaded, 16 * (m + 1))
            with sp.Fori(0, B) as i:
                sp.wait_ge(NF2.x_added.sem, NF2.x_added.at(i, TT))
                sp.dma_start(rows_of(out, i), x[:, bass.ds(i * TT, TT), :]).then_inc(x_stored, 16)
            sp.wait_ge(x_stored, 16 * B)

        @block.tensor
        def _(pe):
            raise_signals(pe, (0, 4))
            pe.sem_inc(head_start, 1)
            pe.wait_ge(head_start, 3)
            pe.wait_ge(ident_loaded, 16)

            def mean_weight():
                pe.wait_ge(abs_summed, 1)
                pe.wait_ge(consts_set, 1)
                nc.tensor.matmul(scan_sum[:, 0:1], wmean, wabs[:], start=True, stop=True).then_inc(abs_total, 1)

            def transposes(norm, banks, i, chunks=range(CC)):
                for c in chunks:
                    dst = banks.open(pe, i, ("xT", c))
                    for tt in range(TT):
                        if c == 0:
                            pe.wait_ge(norm.xh_ready.sem, norm.xh_ready.at(i, tt + 1))
                        mm = nc.tensor.transpose(dst[:, tt * P:(tt + 1) * P], xh[:, tt, c * P:(c + 1) * P], ident[:])
                    mm.then_inc(norm.xT_psum.sem, 1)

            def unit_transposes(norm, u, i):
                for k in range(2):
                    dst = ffn_banks[norm].open(pe, i, ("xT", u, k))
                    for n in range(4):
                        c, tt = 2 * k + n // 2, 2 * u + n % 2
                        if k == 0 and n < 2:
                            pe.wait_ge(norm.xh_ready.sem, norm.xh_ready.at(i, tt + 1))
                        mm = nc.tensor.transpose(dst[:, n * P:(n + 1) * P], xh[:, tt, c * P:(c + 1) * P], ident[:])
                    mm.then_inc(norm.xT_psum.sem, 1)

            def three(dst, pairs):
                for n, (wh, wl, xa, xb) in enumerate(pairs):
                    nc.tensor.matmul(dst, wh, xa, start=(n == 0), stop=False)
                    nc.tensor.matmul(dst, wh, xb, start=False, stop=False)
                    mm = nc.tensor.matmul(dst, wl, xa, start=False, stop=(n == len(pairs) - 1))
                return mm

            def mix(s, i):
                n, banks = ORDER[s], main if s else pre
                pe.wait_ge(lr_hi.sem, lr_hi.at(i, n + 1))
                pe.wait_ge(lr_lo.sem, lr_lo.at(i, n + 1))
                for c in range(CC):
                    dst = banks.open(pe, i, ("mus", s, c))
                    nc.tensor.matmul(dst[:], wx2_hi[:, n, c * P:(c + 1) * P], lrS(n), start=True, stop=False)
                    nc.tensor.matmul(dst[:], wx2_lo[:, n, c * P:(c + 1) * P], lrS(n), start=False, stop=True)\
                        .then_inc(mus_psum.sem, 1)

            def low_rank(m, i):
                dst = pre.open(pe, i, ("lr", m))
                w = P if m < 2 else R
                for c in range(CC):
                    if m == 0:
                        pe.wait_ge(xx_ready.sem, xx_ready.at(i, c + 1))
                    mm = nc.tensor.matmul(dst[0:w, :], WA["wx1"][:, c, m * P:m * P + w], xm[1][:, c, :],
                                          start=(c == 0), stop=(c == CC - 1))
                mm.then_inc(lr_psum.sem, 1)

            def project(s, hf, i):
                n = ORDER[s]
                dst = (pre if n == MG else main).open(pe, i, ("proj", n, hf))
                for c in range(CC):
                    if hf == 0:
                        pe.wait_ge(xm_ready.sem, xm_ready.at(i, s * CC + c + 1))
                    if n in (MW, MG):
                        o, w = dst[0:R, :], WA["ab_a"][:, c, LO if n == MW else UP]
                    else:
                        o, w = dst[:], WA[{MR: "wr", MK: "wk", MV: "wv"}[n]][:, c, hf * P:(hf + 1) * P]
                    mm = nc.tensor.matmul(o, w, xm[s % 2][:, c, :], start=(c == 0), stop=(c == CC - 1))
                mm.then_inc(proj_psum.sem, 1)

            def low_b(j, i):
                pe.wait_ge(low_lo.sem, low_lo.at(i, j + 1))
                for hf in range(HF):
                    dst = (pre if j else main).open(pe, i, ("lowb", j, hf))
                    cols = slice(hf * P, (hf + 1) * P)
                    nc.tensor.matmul(dst[:], abb_hi[:, j, cols], lowS[:], start=True, stop=False)
                    nc.tensor.matmul(dst[:], abb_lo[:, j, cols], lowS[:], start=False, stop=True).then_inc(lowb_psum.sem, 1)

            def spread_v(q, i):
                hf = q // 4
                for g in range(4):
                    dv = 4 * g + q % 4
                    dst = main.open(pe, i, ("vb", 4 * q + g))
                    if q % 4 == 0 and g in (0, 2):
                        pe.wait_ge(v_lo.sem, v_lo.at(i, 2 * hf + g // 2 + 1))
                        pe.wait_ge(v_hi.sem, v_hi.at(i, 2 * hf + g // 2 + 1))
                    nc.tensor.matmul(dst[:], sel_row[:, dv % 8, :], vS(hf, dv // 8), start=True, stop=True).then_inc(vb_psum.sem, 1)

            def quarter(q, i, *beside):
                if q + 1 < QS:
                    spread_v(q + 1, i)
                if q == 0:
                    pe.wait_ge(o_ready.sem, o_ready.before(i, HF))
                if q == 4:
                    pe.wait_ge(o_ready.sem, o_ready.at(i, 1))
                for g in range(4):
                    for before, step, *args in beside:
                        if before == g:
                            step(*args)
                    pe.wait_ge(rs_ready.sem, rs_ready.at(i, 4 * q + g + 1))
                    nc.tensor.matmul(scan_sum[32 * g:32 * g + 32, :], CA["sel_col"][:, q % 4, :], rS[:, g, :],
                                     start=(q % 4 == 0), stop=(q % 4 == 3)).then_inc(o_psum.sem, 1)

            def one_product(key, sig, w, act_in, sig_in, k, i):
                dst = pre.open(pe, i, key)
                pe.wait_ge(sig_in.sem, sig_in.at(i, k))
                nc.tensor.matmul(dst[:], w[:], act_in, start=True, stop=True).then_inc(sig.sem, 1)

            def center(hf, i):
                one_product(("cen", hf), cen_psum, CA["head_center"], bv[:, hf, :], o_ready, hf + 1, i)

            def variance(hf, i):
                one_product(("var", hf), var_psum, CA["head_mean"], sq[:], sq_ready, hf + 1, i)

            def project_out(tt, i):
                dst = pre.open(pe, i, ("out", tt))
                for hf in range(HF):
                    if tt == 0:
                        pe.wait_ge(og_ready.sem, og_ready.at(i, hf + 1))
                    mm = nc.tensor.matmul(dst[:], sg[:, hf, tt * P:(tt + 1) * P], WA["wo_a"][:, hf, :],
                                          start=(hf == 0), stop=(hf == HF - 1))
                mm.then_inc(NA.out_psum.sem, 1)

            def first(i):
                transposes(NA, pre, i)
                pe.wait_ge(wx1_loaded, 16)
                for m in range(3):
                    low_rank(m, i)
                pe.wait_ge(split_hi, 1)
                pe.wait_ge(split_lo, 1)
                mix(0, i)
                pe.wait_ge(loaded, 16 * n_loads)
                pe.wait_ge(split_hi, 5)
                pe.wait_ge(split_lo, 3)

            def open_row(i, last):
                mix(1, i)
                project(0, 0, i)
                if last is not None:
                    center(1, last)
                project(0, 1, i)
                if last is not None:
                    variance(1, last)
                else:
                    mean_weight()
                mix(2, i)
                project(1, 0, i)
                project(1, 1, i)
                mix(3, i)
                project(2, 0, i)
                mix(4, i)
                if last is not None:
                    project_out(0, last)
                project(3, 0, i)
                low_b(0, i)
                spread_v(0, i)
                project(3, 1, i)
                outs = [(0, project_out, tt, last) for tt in range(1, TT)] if last is not None else []
                quarter(0, i, *outs[0:2])
                quarter(1, i, *outs[2:])
                for hf in range(HF):
                    one_product(("bonus", hf), bonus_psum, CA["head_sum"], sq[:] if hf else oc[:], rk_ready, hf + 1, i)

            def close_row(i, following):
                def then(*besides):
                    return besides if following is not None else ()

                quarter(2, i, *then(*((c, transposes, NA, pre, following, (c,)) for c in range(CC))))
                quarter(3, i, (0, project, 4, 0, i))
                quarter(4, i, (0, low_b, 1, i), (0, center, 0, i))
                quarter(5, i, (0, variance, 0, i), *then((0, low_rank, 0, following)))
                quarter(6, i, *then((0, low_rank, 1, following)))
                quarter(7, i, *then((0, low_rank, 2, following)))
                if following is not None:
                    mix(0, following)

            first(0)
            open_row(0, None)
            with pe.Fori(0, B - 1) as i:
                close_row(i, i + 1)
                open_row(i + 1, i)
            close_row(B - 1, None)
            center(1, B - 1)
            variance(1, B - 1)
            unit_transposes(NF1, 0, 0)
            for tt in range(TT):
                project_out(tt, B - 1)

            def unit_products(norm, u, i):
                for tt in (2 * u, 2 * u + 1):
                    dst = ffn_banks[norm].open(pe, i, ("out", tt))
                    nc.tensor.matmul(dst[:], two_rows[:], bias_rows[:], start=True, stop=False)
                    for c in range(CC):
                        if tt == 2 * u and c % 2 == 0:
                            pe.wait_ge(F_hi[norm].sem, F_hi[norm].at(i, CC * u + c + 2))
                            pe.wait_ge(F_lo[norm].sem, F_lo[norm].at(i, 2 * u + c // 2 + 1))
                        nc.tensor.matmul(dst[:], hiT[:, c, tt * P:(tt + 1) * P], wq[:, c, :], start=False, stop=False)
                        mm = nc.tensor.matmul(dst[:], loT[:, c, tt * P:(tt + 1) * P], wq[:, c, :], start=False, stop=(c == CC - 1))
                    mm.then_inc(norm.out_psum.sem, 1)

            def ffn(norm, following):
                with pe.Fori(0, B - 1) as i:
                    unit_transposes(norm, 1, i)
                    unit_products(norm, 0, i)
                    unit_transposes(norm, 0, i + 1)
                    unit_products(norm, 1, i)
                unit_transposes(norm, 1, B - 1)
                unit_products(norm, 0, B - 1)
                following()
                unit_products(norm, 1, B - 1)

            def first_of_retention():
                pe.wait_ge(F_hi[NF1].sem, F_hi[NF1].at(B - 1, 2 * CC))
                transposes(NB, rb, 0)

            pe.wait_ge(NA.x_added.sem, NA.x_added.at(B - 1, TT))
            ffn(NF1, first_of_retention)

            def tiles(w, cols):
                return [(w[0][:, c, cols], w[1][:, c, cols], hiT[:, c, :], loT[:, c, :]) for c in range(CC)]

            def qk(p, i):
                for j in range(2):
                    dst = rb.open(pe, i, ("qk", p, j))
                    three(dst[:], tiles(WB[("k_b", "q_b")[j]], slice(p * P, (p + 1) * P))).then_inc(qk_psum.sem, 1)

            def head_norm(p, i):
                dst = rb.open(pe, i, ("gn", p))
                pe.wait_ge(gn_in.sem, gn_in.at(i, p + 1))
                nc.tensor.matmul(dst[:, 0:2], CB["pair_mean"][:], gmv[:, p, :], start=True, stop=True).then_inc(gn_psum.sem, 1)

            def project_gate(p, i):
                dst = rb.open(pe, i, ("g", p))
                if p == 0:
                    pe.wait_ge(b_lo, 4)
                three(dst[:], tiles(WB["g_b"], slice(p * P, (p + 1) * P))).then_inc(g_psum.sem, 1)

            def heads(i):
                pe.wait_ge(n_hi.sem, n_hi.at(i, CC))
                pe.wait_ge(n_lo.sem, n_lo.at(i, CC))
                qk(0, i)
                for tt in range(TT):
                    dst = rb.open(pe, i, ("v", tt))
                    t = slice(tt * P, (tt + 1) * P)
                    three(dst[:], [(hiT[:, c, t], loT[:, c, t], WB["v_b"][0][:, c, :], WB["v_b"][1][:, c, :]) for c in range(CC)])\
                        .then_inc(v_psum.sem, 1)
                for p in range(PAIRS):
                    if p + 1 < PAIRS:
                        qk(p + 1, i)
                    else:
                        project_gate(p, i)
                    if p == 0:
                        pe.wait_ge(kz_zero, 2)
                    pe.wait_ge(k_ready.sem, k_ready.at(i, 2 * p + 2))
                    pe.wait_ge(q_ready.sem, q_ready.at(i, p + 1))
                    for e in range(2):
                        for jt in range(TT):
                            dst = rb.open(pe, i, ("sc", 2 * p + e, jt))
                            nc.tensor.matmul(dst[:, 0:T - jt * P], kz[:, p % 2, e, jt * P:(jt + 1) * P], qT[:, p % 2, jt * P:T],
                                             start=True, stop=True).then_inc(sc_psum.sem, 1)
                    if p:
                        head_norm(p - 1, i)
                    if p + 1 < PAIRS:
                        project_gate(p, i)
                    dst = rb.open(pe, i, ("ret", p))
                    if p == 0:
                        pe.wait_ge(v_ready.sem, v_ready.at(i, TT))
                    for jt in range(TT):
                        for e in range(2):
                            h = 2 * p + e
                            pe.wait_ge(at_masked.sem, at_masked.at(i, h * TT + jt + 1))
                            mm = nc.tensor.matmul(dst[64 * e:64 * e + 64, jt * P:T], vB[:, jt, h * HD:(h + 1) * HD],
                                                  AT[e][:, AT_AT[jt]:AT_AT[jt] + T - jt * P], start=(jt == 0), stop=(jt == TT - 1))
                    mm.then_inc(ret_psum.sem, 1)

            def project_out_b(i):
                for c in range(CC):
                    pe.wait_ge(y_ready.sem, y_ready.at(i, c + 1))
                    for tt in range(TT):
                        dst = rb.open(pe, i, ("out", tt)) if c == 0 else rb.bank(("out", tt))
                        mm = nc.tensor.matmul(dst[:], retT[:, c, tt * P:(tt + 1) * P], wo_b[:, c, :], start=(c == 0), stop=(c == CC - 1))
                        if c == CC - 1:
                            mm.then_inc(NB.out_psum.sem, 1)
                    if c == 0:
                        head_norm(PAIRS - 1, i)

            pe.wait_ge(NF1.x_added.sem, NF1.x_added.at(B - 1, TT))
            pe.wait_ge(b_loaded, 16 * (1 + len(CB)))
            pe.wait_ge(b_hi, 3)
            pe.wait_ge(b_lo, 3)
            with pe.Fori(0, B - 1) as i:
                heads(i)
                transposes(NB, rb, i + 1)
                project_out_b(i)
            heads(B - 1)
            pe.wait_ge(at_copied.sem, at_copied.at(B - 1, NHB * TT))
            pe.wait_ge(g_ready.sem, g_ready.at(B - 1, CC))
            unit_transposes(NF2, 0, 0)
            project_out_b(B - 1)
            pe.wait_ge(NB.x_added.sem, NB.x_added.at(B - 1, TT))
            ffn(NF2, lambda: None)

        @block.scalar
        def _(act):
            def activation(dst, src, func, sig, **kw):
                nc.scalar.activation(dst, src, func, **kw).then_inc(sig.sem, 1)

            def split_wx2():
                act.wait_ge(wx2_loaded, 16)
                nc.scalar.activation(wx2_hi[:], wx2_raw, ACT.Copy).then_inc(split_hi, 1)

            def split_weights():
                act.wait_ge(loaded, 16 * n_loads)
                nc.scalar.activation(abb_hi[:].rearrange("p a b -> p (a b)"), abb_raw, ACT.Copy).then_inc(split_hi, 1)
                nc.scalar.activation(sel_row[:].rearrange("p (a b) c -> p a (b c)", a=2), sel_raw, ACT.Copy).then_inc(split_hi, 1)
                nc.scalar.activation(bias_rows[0:2, :], bias_raw, ACT.Copy).then_inc(split_hi, 1)
                nc.scalar.activation(two_rows[:], two_raw, ACT.Copy).then_inc(split_hi, 1)

            act.wait_ge(consts_set, 6)
            raise_signals(act, (2, 6))
            act.sem_inc(head_start, 1)
            act.wait_ge(head_start, 3)
            nc.scalar.activation(scratch_act[:, 8:9], eps_t[:], ACT.Copy)
            act.wait_ge(x_half_loaded, 16)
            act.wait_ge(x_loaded, 16)

            act_spots = iter(range(8))

            def normalise(norm, i, after=None):
                at = next(act_spots)
                if after:
                    act.wait_ge(after.xT_psum.sem, after.xT_psum.at(B - 1, CC))
                act.wait_ge(norm.scale.sem, norm.scale.at(i, 1))
                act.wait_ge(norm.xT_psum.sem, norm.xT_psum.before(i, CC))
                nc.scalar.activation(scratch_act[:, at:at + 1], eps_t[:], ACT.Copy)
                for tt in range(TT):
                    activation(xh[:, tt, :], x[:, bass.ds(i * TT + tt, 1), :].rearrange("p a h -> p (a h)"), ACT.Identity, norm.xh_ready,
                               scale=sc[:, 2, tt:tt + 1], bias=sc[:, 3, tt:tt + 1])

            def copy_xn(i):
                for c in range(CC):
                    act.wait_ge(NA.xT_psum.sem, NA.xT_psum.at(i, c + 1))
                    if c == 0:
                        act.wait_ge(xm_ready.sem, xm_ready.before(i, 5 * CC))
                    activation(xnT[:, c, 1:T + 1], pre.bank(("xT", c))[:], ACT.Copy, xn_ready)

            def low_rank(m, i):
                rows = slice(0, P if m < 2 else R)
                src = pre.bank(("lr", m))
                act.wait_ge(lr_psum.sem, lr_psum.at(i, m + 1))
                if m == 2:
                    act.wait_ge(lr_lo.sem, lr_lo.at(i, 2))
                activation(tmp[rows, m % 2, :], src[rows, :], ACT.Tanh, lr_val)
                for e in range(2 if m < 2 else 1):
                    rows = (LO, UP)[e]
                    activation(lrS(2 * m + e)[rows, :], src[rows, :], ACT.Tanh, lr_hi)

            def projected(n, hf, i):
                act.wait_ge(proj_psum.sem, proj_psum.at(i, proj_no[n, hf]))
                src = (pre if n == MG else main).bank(("proj", n, hf))
                if n in (MW, MG):
                    j = 0 if n == MW else 1
                    if j == 0:
                        act.wait_ge(lr_lo.sem, lr_lo.at(i, 5))
                    activation(tmp[LO, j, :], src[LO, :], ACT.Tanh, proj_ready)
                    activation(lowS[LO, :], src[LO, :], ACT.Tanh, low_hi)
                    return
                activation({MR: rT, MK: kT, MV: vT}[n][:, hf, :], src[:], ACT.Copy, proj_ready)
                if n == MV:
                    act.wait_ge(proj_ready.sem, proj_ready.at(i, proj_no[n, hf]))
                    for a in range(2):
                        rows = (LO, UP)[a]
                        activation(vS(hf, a)[rows, :], vT[rows, hf, :], ACT.Copy, v_hi)

            def center(hf, i):
                act.wait_ge(cen_psum.sem, cen_psum.at(i, hf + 1))
                if hf:
                    act.wait_ge(og_ready.sem, og_ready.at(i, hf))
                activation(oc[:], pre.bank(("cen", hf))[:], ACT.Copy, oc_ready)
                activation(sq[:], pre.bank(("cen", hf))[:], ACT.Square, sq_ready)

            def rstd(hf, i):
                act.wait_ge(var_psum.sem, var_psum.at(i, hf + 1))
                activation(sq[:], pre.bank(("var", hf))[:], ACT.Ln, rstd_step, bias=eps_t[:, 0:1])
                act.wait_ge(rstd_step.sem, rstd_step.at(i, hf + 1))
                activation(sq[:], sq[:], ACT.Exp, rstd_ready, scale=-0.5)

            def scale_out(hf, i):
                act.wait_ge(on_ready.sem, on_ready.at(i, hf + 1))
                activation(oc[:], oc[:], ACT.Identity, on_scaled, scale=V["lnw"][:, 0:1], bias=V["lnb"][:, 0:1])

            def open_row(i, last):
                projected(MK, 0, i)
                if last is not None:
                    center(1, last)
                projected(MK, 1, i)
                if last is not None:
                    rstd(1, last)
                projected(MV, 0, i)
                projected(MV, 1, i)
                if last is not None:
                    scale_out(1, last)
                projected(MW, 0, i)
                projected(MR, 0, i)
                for hf in range(HF):
                    act.wait_ge(lowb_psum.sem, lowb_psum.at(i, hf + 1))
                    activation(dT[:, hf, :], main.bank(("lowb", 0, hf))[:], ACT.Exp, lowb_out, bias=V["bw"][:, hf:hf + 1])
                for hf in range(HF):
                    act.wait_ge(lowb_out.sem, lowb_out.at(i, hf + 1))
                    activation(dT[:, hf, :], dT[:, hf, :], ACT.Exp, decay_ready, scale=-1.0)
                projected(MR, 1, i)

            def close_row(i, following):
                more = following is not None
                if more:
                    normalise(NA, following)
                    copy_xn(following)
                projected(MG, 0, i)
                for hf in range(HF):
                    act.wait_ge(lowb_psum.sem, lowb_psum.at(i, HF + hf + 1))
                    activation(sg[:, hf, :], pre.bank(("lowb", 1, hf))[:], ACT.Identity, lowb_out, bias=V["bg"][:, hf:hf + 1])
                for hf in range(HF):
                    act.wait_ge(lowb_out.sem, lowb_out.at(i, HF + hf + 1))
                    activation(gate_tanh[:, hf, :], sg[:, hf, :], ACT.Tanh, th_ready, scale=0.5)
                center(0, i)
                rstd(0, i)
                if more:
                    for m in range(3):
                        low_rank(m, following)
                scale_out(0, i)

            normalise(NA, 0)
            copy_xn(0)
            split_wx2()
            low_rank(0, 0)
            split_weights()
            for m in (1, 2):
                low_rank(m, 0)
            open_row(0, None)
            act.wait_ge(x_loaded, 32)
            with act.Fori(0, B - 1) as i:
                close_row(i, i + 1)
                open_row(i + 1, i)
            close_row(B - 1, None)
            center(1, B - 1)
            rstd(1, B - 1)
            normalise(NF1, 0, after=NA)
            scale_out(1, B - 1)

            def unit(norm, u, i):
                half = slice(u * T // 2, (u + 1) * T // 2)
                for c in range(CC):
                    k = c // 2
                    src = ffn_banks[norm].bank(("xT", u, k))[:, (c % 2) * T // 2:(c % 2 + 1) * T // 2]
                    if c % 2 == 0:
                        act.wait_ge(norm.xT_psum.sem, norm.xT_psum.at(i, 2 * u + k + 1))
                        act.wait_ge(F_lo[norm].sem, F_lo[norm].before(i, 2 * u + k + 1))
                    if c == 0:
                        act.wait_ge(norm.out_psum.sem, norm.out_psum.before(i, 2 * u + 2))
                    kw = dict(scale=V["gamma"][:, c:c + 1], bias=V["beta"][:, c:c + 1])
                    activation(ffn_val[u][:, c, :], src, ACT.Identity, F_val[norm], **kw)
                    activation(hiT[:, c, half], src, ACT.Identity, F_hi[norm], **kw)

            def ffn(norm, following=None):
                unit(norm, 0, 0)
                with act.Fori(0, B - 1) as i:
                    unit(norm, 1, i)
                    unit(norm, 0, i + 1)
                unit(norm, 1, B - 1)
                if following:
                    normalise(following, 0, after=norm)

            ffn(NF1, NB)

            def x_hi(i):
                for c in range(CC):
                    act.wait_ge(NB.xT_psum.sem, NB.xT_psum.at(i, c + 1))
                    activation(hiT[:, c, :], rb.bank(("xT", c))[:], ACT.Copy, n_hi)

            def copy_scores(p, i):
                for e in range(2):
                    h = 2 * p + e
                    if p > 0:
                        act.wait_ge(ret_psum.sem, ret_psum.at(i, p))
                    for jt in range(TT):
                        act.wait_ge(sc_psum.sem, sc_psum.at(i, h * TT + jt + 1))
                        activation(AT[e][:, AT_AT[jt]:AT_AT[jt] + T - jt * P], rb.bank(("sc", h, jt))[:, 0:T - jt * P], ACT.Identity,
                                   at_copied, scale=CB["shrink"][:, h * TT + jt:h * TT + jt + 1])

            def exp_gate(p, i):
                act.wait_ge(g_psum.sem, g_psum.at(i, p + 1))
                activation(mish[:, p, :], rb.bank(("g", p))[:], ACT.Copy, g_ready)
                th = retT[:, p, :]
                act.wait_ge(g_cut.sem, g_cut.at(i, p + 1))
                activation(th, th, ACT.Exp, exp_ready)

            def tanh_gate(p, i):
                th = retT[:, p, :]
                act.wait_ge(exp_ready.sem, exp_ready.at(i, p + 1))
                activation(th, th, ACT.Ln, sp_ready, bias=one_t[:, 0:1])
                act.wait_ge(sp_ready.sem, sp_ready.at(i, p + 1))
                activation(th, th, ACT.Tanh, tanh_ready)

            def heads(i, norm, following):
                for tt in range(TT):
                    act.wait_ge(v_psum.sem, v_psum.at(i, tt + 1))
                    activation(vB[:, tt, :], rb.bank(("v", tt))[:], ACT.Copy, v_ready)
                for p in range(PAIRS):
                    if p + 1 == PAIRS:
                        exp_gate(p, i)
                    copy_scores(p, i)
                    if p + 1 < PAIRS:
                        exp_gate(p, i)
                    tanh_gate(p, i)
                    if p == 1:
                        normalise(norm, following, after=None if norm is NB else NB)

            act.wait_ge(NF1.out_psum.sem, NF1.out_psum.at(B - 1, TT))
            x_hi(0)
            act.wait_ge(b_loaded, 16 * (1 + len(CB)))
            with act.Fori(0, B - 1) as i:
                heads(i, NB, i + 1)
                x_hi(i + 1)
            heads(B - 1, NF2, 0)
            ffn(NF2)

        @block.vector
        def _(dve):
            spots = iter(range(64))

            def wait_apart(sem, value):
                at = next(spots)
                dve.wait_ge(sem, value)
                nc.vector.memset(scratch[:, at:at + 1], 0.0)

            def tensor_tensor(dst, a, b, op, sig):
                nc.vector.tensor_tensor(dst, a, b, op).then_inc(sig.sem, 1)

            def stt(dst, a, s, b, op0, op1, sig):
                nc.vector.scalar_tensor_tensor(dst, a, s, b, op0, op1).then_inc(sig.sem, 1)

            nc.vector.memset(wmean, 1.0 / (H * H)).then_inc(consts_set, 1)
            nc.vector.memset(eps_t[:], EPS).then_inc(consts_set, 1)
            nc.vector.memset(one_t[:], 1.0).then_inc(consts_set, 1)
            nc.vector.memset(xnT[:, :, 0:1], 0.0).then_inc(consts_set, 1)
            nc.vector.memset(bias_rows[:].bitcast(mybir.dt.uint32), 0).then_inc(consts_set, 1)
            nc.vector.memset(St[:, :, 0:1], 0.0).then_inc(consts_set, 1)
            dve.wait_ge(consts_set, 6)

            def split_wx2():
                dve.wait_ge(split_hi, 1)
                nc.vector.tensor_tensor(wx2_lo[:], wx2_raw, wx2_hi[:].bitcast(F32), ALU.subtract).then_inc(split_lo, 1)

            def split_weights():
                dve.wait_ge(split_hi, 4)
                nc.vector.tensor_tensor(abb_lo[:].rearrange("p a b -> p (a b)"), abb_raw, abb_hi[:].rearrange("p a b -> p (a b)").bitcast(F32),
                                        ALU.subtract).then_inc(split_lo, 1)
                nc.vector.scalar_tensor_tensor(bias_rows[0:2, :], bias_rows[0:2, :].bitcast(F32), V["minus_row1"][0:2, 0:1], bias_raw,
                                               ALU.mult, ALU.add).then_inc(split_lo, 1)

            def sum_weight():
                dve.wait_ge(wq_loaded, 16)
                nc.vector.tensor_reduce(wabs[:], wq_raw, mybir.AxisListType.XY, ALU.add, apply_absolute_value=True)\
                    .then_inc(abs_summed, 1)

            def quantise_weight():
                dve.wait_ge(abs_total, 1)
                nc.vector.tensor_scalar(thr[:, 0:1], scan_sum[:, 0:1], 1e-5, 0.5, ALU.add, ALU.mult).then_inc(wq_step, 1)
                dve.wait_ge(wq_step, 1)
                nc.vector.tensor_scalar(thr[:, 1:2], thr[:, 0:1], -1.0, None, ALU.mult).then_inc(wq_step, 1)
                dve.wait_ge(wq_step, 2)
                nc.vector.tensor_scalar(wq[:], wq_raw, thr[:, 1:2], None, ALU.is_lt).then_inc(wq_step, 1)
                dve.wait_ge(wq_step, 3)
                nc.vector.scalar_tensor_tensor(wq[:], wq_raw, thr[:, 0:1], wq[:].bitcast(F32), ALU.is_gt, ALU.subtract).then_inc(wq_ready, 1)

            dve.wait_ge(head_start, 3)
            def layer_norm(norm, i, after=None, arriving=False):
                if after:
                    wait_apart(after.scale.sem, after.scale.at(B - 1, 1))
                wait_apart(norm.scale.sem, norm.scale.before(i, 1))
                for tt in range(TT):
                    if arriving and tt == 0:
                        dve.wait_ge(x_half_loaded, 16)
                    if arriving and tt == TT // 2:
                        dve.wait_ge(x_loaded, 16)
                    nc.vector.bn_stats(stats[:, tt, :], x[:, bass.ds(i * TT + tt, 1), :].rearrange("p a h -> p (a h)")).then_inc(norm.stats_step.sem, 1)
                wait_apart(norm.stats_step.sem, norm.stats_step.at(i, TT))
                for tt in range(TT):
                    nc.vector.bn_aggr(mv[:, tt, :], stats[:, tt, :]).then_inc(norm.mv_ready.sem, 1)

            def add_to_x(norm, banks, i, tiles=range(TT)):
                for tt in tiles:
                    dve.wait_ge(norm.out_psum.sem, norm.out_psum.at(i, tt + 1))
                    row = x[:, bass.ds(i * TT + tt, 1), :].rearrange("p a h -> p (a h)")
                    tensor_tensor(row, banks.bank(("out", tt))[:], row, ALU.add, norm.x_added)

            def mix(s, i):
                n, banks = ORDER[s], main if s else pre
                if s == 0:
                    dve.wait_ge(sg_ready.sem, sg_ready.before(i, HF))
                for c in range(CC):
                    dve.wait_ge(mus_psum.sem, mus_psum.at(i, s * CC + c + 1))
                    stt(xm[s % 2][:, c, :], banks.bank(("mus", s, c))[:], V["xb"][:, n * CC + c:n * CC + c + 1], delta[:, c, :],
                        ALU.add, ALU.mult, dm_ready)

            def shift(i):
                dve.wait_ge(proj_psum.sem, proj_psum.before(i, proj_no[MR, 1]))
                for c in range(CC):
                    dve.wait_ge(delta_ready.sem, delta_ready.at(i, c + 1))
                    stt(xm[1][:, c, :], delta[:, c, :], V["mu"][:, c:c + 1], xnT[:, c, 1:T + 1], ALU.mult, ALU.add, xx_ready)

            def low_rank_lo(ks, i):
                for k in ks:
                    m, rows = k // 2, (LO, UP)[k % 2]
                    dve.wait_ge(lr_val.sem, lr_val.at(i, m + 1))
                    dve.wait_ge(lr_hi.sem, lr_hi.at(i, k + 1))
                    tensor_tensor(lrS(k)[(UP, LO)[k % 2], :], tmp[rows, m % 2, :], lrS(k)[rows, :].bitcast(F32), ALU.subtract, lr_lo)

            def v_low(i):
                for k in range(4):
                    hf, a = k // 2, k % 2
                    rows = (LO, UP)[a]
                    dve.wait_ge(v_hi.sem, v_hi.at(i, k + 1))
                    tensor_tensor(vS(hf, a)[(UP, LO)[a], :], vT[rows, hf, :], vS(hf, a)[rows, :].bitcast(F32), ALU.subtract, v_lo)

            def low_b_lo(j, i):
                dve.wait_ge(low_hi.sem, low_hi.at(i, j + 1))
                tensor_tensor(lowS[UP, :], tmp[LO, j, :], lowS[LO, :].bitcast(F32), ALU.subtract, low_lo)

            def kv_product(m, i):
                dve.wait_ge(vb_psum.sem, vb_psum.at(i, m + 1))
                if m >= KV_RING:
                    dve.wait_ge(state_ready.sem, state_ready.at(i, m - KV_RING + 1))
                tensor_tensor(kv[:, m % KV_RING, :], main.bank(("vb", m))[:], kT[:, m // DV, :], ALU.mult, kv_ready)

            def scan(m, i):
                dve.wait_ge(kv_ready.sem, kv_ready.at(i, m + 1))
                if m % DV == 0:
                    dve.wait_ge(decay_ready.sem, decay_ready.at(i, m // DV + 1))
                if m >= RING:
                    dve.wait_ge(rs_ready.sem, rs_ready.at(i, m - RING + 1))
                nc.vector.tensor_tensor_scan(St[:, m % RING, 1:T + 1], dT[:, m // DV, :], kv[:, m % KV_RING, :], 0.0, ALU.mult, ALU.add)\
                    .then_inc(state_ready.sem, 1)

            def scans(ms, i):
                for m in ms:
                    if m == 0:
                        kv_product(0, i)
                    if m + 1 < HF * DV and m != 7:
                        kv_product(m + 1, i)
                    scan(m, i)

            def bonus(i):
                for hf in range(HF):
                    if hf == 0:
                        dve.wait_ge(proj_ready.sem, proj_ready.at(i, proj_no[MR, 1]))
                    stt((sq if hf else oc)[:], rT[:, hf, :], V["bonus"][:, hf:hf + 1], kT[:, hf, :], ALU.mult, ALU.mult, rk_ready)

            def bonus_times_v(i):
                for hf in range(HF):
                    dve.wait_ge(bonus_psum.sem, bonus_psum.at(i, hf + 1))
                    tensor_tensor(bv[:, hf, :], pre.bank(("bonus", hf))[:], vT[:, hf, :], ALU.mult, bv_ready)

            def gate(i):
                for hf in range(HF):
                    dve.wait_ge(th_ready.sem, th_ready.at(i, hf + 1))
                    stt(sg[:, hf, :], gate_tanh[:, hf, :], 1.0, sg[:, hf, :], ALU.add, ALU.mult, sg_ready)

            def sum_up(hf, i):
                dve.wait_ge(o_psum.sem, o_psum.at(i, (hf + 1) * DV))
                dve.wait_ge(bv_ready.sem, bv_ready.at(i, hf + 1))
                tensor_tensor(bv[:, hf, :], scan_sum[:], bv[:, hf, :], ALU.add, o_ready)

            def times_rstd(hf, i):
                dve.wait_ge(rstd_ready.sem, rstd_ready.at(i, hf + 1))
                tensor_tensor(oc[:], oc[:], sq[:], ALU.mult, on_ready)

            def times_gate(hf, i):
                dve.wait_ge(on_scaled.sem, on_scaled.at(i, hf + 1))
                dve.wait_ge(sg_ready.sem, sg_ready.at(i, hf + 1))
                stt(sg[:, hf, :], oc[:], 0.5, sg[:, hf, :], ALU.mult, ALU.mult, og_ready)

            def open_row(i, last):
                if last is not None:
                    sum_up(1, last)
                mix(0, i)
                mix(1, i)
                low_rank_lo((4,), i)
                mix(2, i)
                if last is not None:
                    times_rstd(1, last)
                else:
                    quantise_weight()
                mix(3, i)
                v_low(i)
                if last is not None:
                    times_gate(1, last)
                low_b_lo(0, i)
                mix(4, i)
                if last is not None:
                    add_to_x(NA, pre, last, (0,))
                scans(range(0, 4), i)
                bonus(i)
                scans(range(4, 6), i)
                if last is not None:
                    add_to_x(NA, pre, last, (1, 2))
                scans(range(6, 8), i)
                if last is not None:
                    add_to_x(NA, pre, last, (3,))

            def close_row(i, following):
                more = following is not None
                kv_product(8, i)
                if more:
                    layer_norm(NA, following)
                scans(range(8, 12), i)
                bonus_times_v(i)
                scans(range(12, 18), i)
                low_b_lo(1, i)
                sum_up(0, i)
                scans(range(18, 20), i)
                if more:
                    shift(following)
                scans(range(20, 24), i)
                gate(i)
                scans(range(24, 28), i)
                times_rstd(0, i)
                if more:
                    low_rank_lo((0, 1), following)
                scans(range(28, 32), i)
                if more:
                    low_rank_lo((2, 3), following)
                times_gate(0, i)

            layer_norm(NA, 0, arriving=True)
            dve.wait_ge(vecs_loaded, 16)
            shift(0)
            split_wx2()
            sum_weight()
            low_rank_lo((0, 1), 0)
            split_weights()
            low_rank_lo((2, 3), 0)
            open_row(0, None)
            dve.wait_ge(x_loaded, 32)
            with dve.Fori(0, B - 1) as i:
                close_row(i, i + 1)
                open_row(i + 1, i)
            close_row(B - 1, None)
            sum_up(1, B - 1)
            layer_norm(NF1, 0, after=NA)
            times_rstd(1, B - 1)
            times_gate(1, B - 1)
            add_to_x(NA, pre, B - 1)

            def normalise(norm, i):
                dve.wait_ge(norm.scale.sem, norm.scale.at(i, 1))
                dve.wait_ge(norm.xT_psum.sem, norm.xT_psum.before(i, CC))
                for tt in range(TT):
                    nc.vector.tensor_scalar(xh[:, tt, :], x[:, bass.ds(i * TT + tt, 1), :].rearrange("p a h -> p (a h)"),
                                            sc[:, 2, tt:tt + 1], sc[:, 3, tt:tt + 1], ALU.mult, ALU.add).then_inc(norm.xh_ready.sem, 1)

            def ffn(norm, following, beside):
                def add(i, tiles):
                    add_to_x(norm, ffn_banks[norm], i, tiles)

                layer_norm(norm, 1)
                with dve.Fori(0, B - 2) as i:
                    normalise(norm, i + 1)
                    add(i, (0, 1))
                    layer_norm(norm, i + 2)
                    add(i, (2, 3))
                normalise(norm, B - 1)
                add(B - 2, (0, 1))
                if following:
                    layer_norm(following, 0, after=norm)
                beside(0)
                add(B - 2, (2, 3))
                beside(1)
                add(B - 1, (0, 1))
                beside(2)
                add(B - 1, (2, 3))
                beside(3)

            def zero_kz():
                nc.vector.memset(kz[UP, :, 0, :], 0.0).then_inc(kz_zero, 1)
                nc.vector.memset(kz[LO, :, 1, :], 0.0).then_inc(kz_zero, 1)

            def split_b(m):
                n = ("q_b", "k_b", "v_b", "g_b")[m]
                dve.wait_ge(raw_loaded, 16 * (m + 1))
                nc.vector.tensor_copy(WB[n][0][:], raw[n]).then_inc(b_hi, 1)
                dve.wait_ge(b_hi, m + 1)
                nc.vector.tensor_tensor(WB[n][1][:], raw[n], WB[n][0][:].bitcast(F32), ALU.subtract).then_inc(b_lo, 1)

            ffn(NF1, NB, lambda m: split_b(m) if m < 3 else None)

            swap = [k ^ 1 for k in range(32)]

            def rotate(p, i):
                s = p % 2
                for j in range(2):
                    m = 2 * p + j
                    src = rb.bank(("qk", p, j))
                    dve.wait_ge(qk_psum.sem, qk_psum.at(i, m + 1))
                    if p >= 2:
                        dve.wait_ge(sc_psum.sem, sc_psum.at(i, (2 * p - 2) * TT))
                    else:
                        dve.wait_ge(sc_psum.sem, sc_psum.before(i, NHB * TT))
                    if j == 1:
                        tensor_tensor(qT[:, s, :], src[:], CB["cos"][:, 0, :], ALU.mult, rot_cos)
                    else:
                        for e in range(2):
                            rows = (LO, UP)[e]
                            tensor_tensor(kz[rows, s, e, :], src[rows, :], CB["cos"][rows, 1, :], ALU.mult, rot_cos)
                    ready, k = ((k_ready, 2 * p), (q_ready, p))[j]
                    if p >= 1:
                        wait_apart(ready.sem, ready.at(i, k))
                    else:
                        wait_apart(ready.sem, ready.before(i, ready.per))
                    nc.vector.stream_shuffle(tmp[:, j, :], src[:], swap).then_inc(rot_swap.sem, 1)
                dve.wait_ge(rot_swap.sem, rot_swap.at(i, 2 * p + 2))
                tensor_tensor(tmp[:, 1, :], tmp[:, 1, :], CB["sin"][:, 0, :], ALU.mult, q_sin)
                dve.wait_ge(q_sin.sem, q_sin.at(i, p + 1))
                dve.wait_ge(rot_cos.sem, rot_cos.at(i, 3 * p + 3))
                tensor_tensor(qT[:, s, :], qT[:, s, :], tmp[:, 1, :], ALU.add, q_ready)

            def x_lo(i):
                for c in range(CC):
                    dve.wait_ge(n_hi.sem, n_hi.at(i, c + 1))
                    tensor_tensor(loT[:, c, :], rb.bank(("xT", c))[:], hiT[:, c, :].bitcast(F32), ALU.subtract, n_lo)

            def head_sums(p, i):
                dve.wait_ge(gn_psum.sem, gn_psum.at(i, p + 1))
                nc.vector.tensor_copy(gs[:, p, :], rb.bank(("gn", p))[:, 0:2]).then_inc(gn_out.sem, 1)

            def cut_gate(p, i):
                dve.wait_ge(g_ready.sem, g_ready.at(i, p + 1))
                nc.vector.tensor_scalar(retT[:, p, :], mish[:, p, :], 30.0, None, ALU.min).then_inc(g_cut.sem, 1)

            def gate(p, i):
                dve.wait_ge(tanh_ready.sem, tanh_ready.at(i, p + 1))
                tensor_tensor(mish[:, p, :], mish[:, p, :], retT[:, p, :], ALU.mult, gate_ready)

            def gated(p, i):
                dve.wait_ge(gn_coef.sem, gn_coef.at(i, p + 1))
                nc.vector.tensor_scalar(retT[:, p, :], retT[:, p, :], gc[:, 4, p:p + 1], gc[:, 5, p:p + 1], ALU.mult, ALU.add)\
                    .then_inc(y_norm.sem, 1)
                dve.wait_ge(y_norm.sem, y_norm.at(i, p + 1))
                dve.wait_ge(gate_ready.sem, gate_ready.at(i, p + 1))
                tensor_tensor(retT[:, p, :], retT[:, p, :], mish[:, p, :], ALU.mult, y_ready)

            def heads(i, norm, following):
                rotate(0, i)
                for p in range(PAIRS):
                    if p + 1 < PAIRS:
                        rotate(p + 1, i)
                    if p + 1 == PAIRS:
                        cut_gate(p, i)
                    if p:
                        head_sums(p - 1, i)
                    if p + 1 < PAIRS:
                        cut_gate(p, i)
                    if p:
                        gated(p - 1, i)
                    if p == 0:
                        layer_norm(norm, following, after=None if norm is NB else NB)
                    gate(p, i)
                    dve.wait_ge(ret_psum.sem, ret_psum.at(i, p + 1))
                    dve.wait_ge(gate_ready.sem, gate_ready.at(i, p + 1))
                    tensor_tensor(retT[:, p, :], rb.bank(("ret", p))[:], CB["grow"][:, p, :], ALU.mult, ret_ready)
                    dve.wait_ge(ret_ready.sem, ret_ready.at(i, p + 1))
                    nc.vector.bn_stats(gst[:, p, :], retT[:, p, :]).then_inc(gst_step.sem, 1)
                    wait_apart(gst_step.sem, gst_step.at(i, 2 * p + 1))
                    nc.vector.bn_aggr(gmv[:, p, :], gst[:, p, :]).then_inc(gst_step.sem, 1)
                    dve.wait_ge(gst_step.sem, gst_step.at(i, 2 * p + 2))
                    stt(gmv[:, p, 1:2], gmv[:, p, 0:1], gmv[:, p, 0:1], gmv[:, p, 1:2], ALU.mult, ALU.add, gn_in)
                if norm is NB:
                    x_lo(following)
                head_sums(PAIRS - 1, i)
                gated(PAIRS - 1, i)
                add_to_x(NB, rb, i)

            x_lo(0)
            zero_kz()
            split_b(3)
            dve.wait_ge(b_loaded, 16 * (1 + len(CB)))
            dve.wait_ge(kz_zero, 2)
            with dve.Fori(0, B - 1) as i:
                heads(i, NB, i + 1)
            heads(B - 1, NF2, 0)
            ffn(NF2, None, lambda m: None)

        @block.gpsimd
        def _(pool):
            raise_signals(pool, range(1, 8, 2))
            nc.gpsimd.memset(mhalf[:], -0.5).then_inc(mhalf_set, 1)
            nc.gpsimd.memset(eps4[:], EPS).then_inc(mhalf_set, 1)
            nc.gpsimd.memset(minus4[:], -1.0).then_inc(mhalf_set, 1)
            nc.gpsimd.memset(var_scale[:], 1.0 + EPS).then_inc(mhalf_set, 1)
            nc.gpsimd.memset(var_shift[:], EPS * EPS).then_inc(mhalf_set, 1)
            pool.wait_ge(mhalf_set, 5)
            pool.sem_inc(head_start, 1)
            pool.wait_ge(head_start, 3)

            def tensor_tensor(dst, a, b, op, sig):
                nc.gpsimd.tensor_tensor(dst, a, b, op).then_inc(sig.sem, 1)

            def ln_scales(norm, i, after=None):
                k = 0

                def step(*args):
                    nonlocal k
                    k += 1
                    tensor_tensor(*args, norm.step)
                    pool.wait_ge(norm.step.sem, norm.step.at(i, k))

                mean, var = mv[:, :, 0], mv[:, :, 1]
                a, nm, s, shift = (sc[:, n, :] for n in range(4))
                pool.wait_ge(norm.mv_ready.sem, norm.mv_ready.at(i, TT))
                if after:
                    pool.wait_ge(after.xh_ready.sem, after.xh_ready.at(B - 1, TT))
                pool.wait_ge(norm.xh_ready.sem, norm.xh_ready.before(i, TT))
                step(nm, mean, minus4[:], ALU.mult)
                if norm.double:
                    step(a, var, var_scale[:], ALU.mult)
                    step(a, a, var_shift[:], ALU.add)
                else:
                    step(a, var, eps4[:], ALU.add)
                step(s, a, mhalf[:], ALU.pow)
                tensor_tensor(shift, nm, s, ALU.mult, norm.scale)

            def mix(s, i):
                for c in range(CC):
                    pool.wait_ge(dm_ready.sem, dm_ready.at(i, s * CC + c + 1))
                    tensor_tensor(xm[s % 2][:, c, :], xm[s % 2][:, c, :], xnT[:, c, 1:T + 1], ALU.add, xm_ready)

            def times_r(ms, i):
                for m in ms:
                    pool.wait_ge(state_ready.sem, state_ready.at(i, m + 1))
                    if m >= RING:
                        pool.wait_ge(o_psum.sem, o_psum.at(i, m - RING + 1))
                    else:
                        pool.wait_ge(o_psum.sem, o_psum.before(i, HF * DV - RING + m + 1))
                    if m % DV == 0:
                        n = proj_no[MR, m // DV]
                        pool.wait_ge(proj_ready.sem, proj_ready.at(i, n))
                    tensor_tensor(rS[:, m % RING, :], St[:, m % RING, 0:T], rT[:, m // DV, :], ALU.mult, rs_ready)

            def difference(i):
                pool.wait_ge(dm_ready.sem, dm_ready.before(i, 5 * CC))
                for c in range(CC):
                    pool.wait_ge(xn_ready.sem, xn_ready.at(i, c + 1))
                    tensor_tensor(delta[:, c, :], xnT[:, c, 0:T], xnT[:, c, 1:T + 1], ALU.subtract, delta_ready)

            def open_row(i):
                for s in range(5):
                    mix(s, i)
                times_r(range(8), i)

            def close_row(i, following):
                if following is not None:
                    ln_scales(NA, following)
                times_r(range(8, 12), i)
                if following is not None:
                    difference(following)
                times_r(range(12, 32), i)

            pool.wait_ge(consts_set, 6)
            ln_scales(NA, 0)
            difference(0)
            open_row(0)
            with pool.Fori(0, B - 1) as i:
                close_row(i, i + 1)
                open_row(i + 1)
            close_row(B - 1, None)
            ln_scales(NF1, 0, after=NA)

            def unit(norm, u, i):
                half = slice(u * T // 2, (u + 1) * T // 2)
                for k in range(2):
                    cs = slice(2 * k, 2 * k + 2)
                    pool.wait_ge(F_val[norm].sem, F_val[norm].at(i, CC * u + 2 * k + 2))
                    pool.wait_ge(F_hi[norm].sem, F_hi[norm].at(i, CC * u + 2 * k + 2))
                    tensor_tensor(loT[:, cs, half], ffn_val[u][:, cs, :], hiT[:, cs, half].bitcast(F32), ALU.subtract, F_lo[norm])

            def ffn(norm, following=None):
                unit(norm, 0, 0)
                with pool.Fori(0, B - 1) as i:
                    ln_scales(norm, i + 1)
                    unit(norm, 1, i)
                    unit(norm, 0, i + 1)
                if following:
                    ln_scales(following, 0, after=norm)
                unit(norm, 1, B - 1)

            ffn(NF1, NB)
            pool.wait_ge(b_loaded, 16 * (1 + len(CB)))

            def rotate(p, i):
                s = p % 2
                pool.wait_ge(rot_swap.sem, rot_swap.at(i, 2 * p + 1))
                tensor_tensor(tmp[:, 0, :], tmp[:, 0, :], CB["sin"][:, 1, :], ALU.mult, k_sin)
                pool.wait_ge(k_sin.sem, k_sin.at(i, p + 1))
                for e in range(2):
                    rows = (LO, UP)[e]
                    tensor_tensor(kz[rows, s, e, :], kz[rows, s, e, :], tmp[rows, 0, :], ALU.add, k_ready)
                pool.wait_ge(k_ready.sem, k_ready.at(i, 2 * p + 2))

            def head_coefficients(p, i):
                k = 6 * p

                def step(*args):
                    nonlocal k
                    k += 1
                    tensor_tensor(*args, gn_step)
                    pool.wait_ge(gn_step.sem, gn_step.at(i, k))

                at = slice(p, p + 1)
                mean, squares = gs[:, p, 0:1], gs[:, p, 1:2]
                pool.wait_ge(gn_out.sem, gn_out.at(i, p + 1))
                step(gc[:, 0, at], mean, mean, ALU.mult)
                step(gc[:, 1, at], squares, gc[:, 0, at], ALU.subtract)
                step(gc[:, 2, at], gc[:, 1, at], eps4[:, at], ALU.add)
                step(gc[:, 3, at], gc[:, 2, at], mhalf[:, at], ALU.pow)
                step(gc[:, 4, at], gc[:, 3, at], V["gnw"][:, at], ALU.mult)
                step(gc[:, 0, at], mean, gc[:, 4, at], ALU.mult)
                tensor_tensor(gc[:, 5, at], V["gnb"][:, at], gc[:, 0, at], ALU.subtract, gn_coef)

            def heads(i, norm, following):
                rotate(0, i)
                for p in range(PAIRS):
                    for e in range(2):
                        h = 2 * p + e
                        for jt in range(TT):
                            pool.wait_ge(at_copied.sem, at_copied.at(i, h * TT + jt + 1))
                            blk = AT[e][:, AT_AT[jt]:AT_AT[jt] + P]
                            tensor_tensor(blk, blk, CB["causal"][:], ALU.mult, at_masked)
                    if p:
                        head_coefficients(p - 1, i)
                    if p + 1 < PAIRS:
                        rotate(p + 1, i)
                    if p == 0:
                        ln_scales(norm, following, after=None if norm is NB else NB)
                head_coefficients(PAIRS - 1, i)

            with pool.Fori(0, B - 1) as i:
                heads(i, NB, i + 1)
            heads(B - 1, NF2, 0)
            ffn(NF2)


def kernel(**inputs):
    import numpy as np
    import concourse.bacc as bacc
    from concourse import mybir as mb
    from concourse.bass_utils import run_bass_kernel_spmd

    a = {k.replace("L0_", ""): np.asarray(v) for k, v in inputs.items()}

    def rows(w):
        return np.ascontiguousarray(w.reshape(-1, P, w.shape[1]).transpose(1, 0, 2))

    def cols(v):
        return np.ascontiguousarray(v.reshape(-1, P).T)

    def by_dv(w):
        return w.reshape(*w.shape[:-1], HF, HH, DV).swapaxes(-1, -2).reshape(w.shape)

    wx2 = a["attn_a_Wx2"].transpose(1, 2, 0)
    wx2 = np.concatenate([wx2, wx2], axis=1).transpose(1, 0, 2)
    qkv = a["attn_b_wqkv"].reshape(NHB, 3, HD, H)

    weights = {
        "wx1": rows(a["attn_a_Wx1"]), "wx2": np.ascontiguousarray(wx2),
        "wr": rows(a["attn_a_Wr"]), "wk": rows(a["attn_a_Wk"]), "wv": rows(by_dv(a["attn_a_Wv"])),
        "ab_a": rows(np.concatenate([a["attn_a_Ww_a"], a["attn_a_Wg_a"]], axis=1)),
        "ab_b": np.tile(np.stack([a["attn_a_Ww_b"], by_dv(a["attn_a_Wg_b"])], axis=1), (2, 1, 1)),
        "wo_a": rows(by_dv(a["attn_a_Wo"].T).T),
        "wq": rows(a["ffn_weight"].T),
        "q_b": rows(qkv[:, 0].reshape(-1, H).T), "k_b": rows(qkv[:, 1].reshape(-1, H).T), "v_b": rows(qkv[:, 2].reshape(-1, H).T),
        "g_b": rows(a["attn_b_wg"].T), "o_b": rows(a["attn_b_wo"].T),
    }
    vectors = {
        "mu": cols(a["attn_a_mu_x"]), "xb": cols(a["attn_a_x_bias"].reshape(-1)),
        "bw": cols(a["attn_a_bw"]), "bg": cols(by_dv(a["attn_a_bg"])), "bonus": cols(a["attn_a_bonus"].reshape(-1)),
        "lnw": np.repeat(a["attn_a_ln_w"], HH)[:, None].copy(), "lnb": np.repeat(a["attn_a_ln_b"], HH)[:, None].copy(),
        "minus_row1": -(np.arange(P) == 1).astype(np.float32)[:, None],
        "gamma": cols(a["ffn_ln_gamma"]), "beta": cols(a["ffn_ln_beta"]),
        "gnw": cols(np.repeat(a["attn_b_gn_weight"], HD)), "gnb": cols(np.repeat(a["attn_b_gn_bias"], HD)),
    }
    f = np.float32
    p = np.arange(P)
    sel_row = np.zeros((P, 8, P), f)
    sel_col = np.zeros((P, 4, 32), f)
    for h in range(HH):
        for d in range(8):
            sel_row[[8 * d + h, R + 8 * d + h], d, DK * h:DK * h + DK] = 1
        for q in range(4):
            sel_col[DK * h:DK * h + DK, q, 8 * q + h] = 1
    t = np.arange(T, dtype=np.float64)
    inv = 1.0 / 10000.0 ** (np.arange(0, ROT, 2) / ROT)
    fr = np.repeat(t[:, None] * inv[None], 2, axis=1)
    base = (np.arange(0, ROT, 2) + 0.4 * ROT) / (1.4 * ROT)
    scale = base[None] ** ((t - T // 2) / 512.0)[:, None]
    scale = np.concatenate([scale, scale], axis=1)
    sign = np.where(np.arange(ROT) % 2 == 0, -1.0, 1.0)
    cos, sin = np.zeros((P, 2, T)), np.zeros((P, 2, T))
    grow, shrink = np.zeros((P, PAIRS, T)), np.zeros((P, NHB * TT))
    for e in range(2):
        for j in range(2):
            s = scale if j == 0 else 1.0 / scale
            cos[HD * e:HD * e + ROT, j] = (np.cos(fr) * s).T
            sin[HD * e:HD * e + ROT, j] = (np.sin(fr) * s * sign).T
            cos[HD * e + ROT:HD * (e + 1), j] = 1
        for q in range(PAIRS):
            h = 2 * q + e
            gamma = 1.0 - 2.0 ** (-5.0 - h)
            grow[HD * e:HD * (e + 1), q] = gamma ** (t - T // 2)
            shrink[:, h * TT:(h + 1) * TT] = (gamma ** (T // 2 - t)).reshape(TT, P).T
    consts = {
        "ident": np.eye(P, dtype=f), "sel_row": sel_row, "sel_col": sel_col,
        "head_sum": (p[:, None] // DK == p[None] % HH).astype(f),
        "head_mean": (p[:, None] % HH == p[None] % HH).astype(f) / f(DV),
        "head_center": np.eye(P, dtype=f) - (p[:, None] % HH == p[None] % HH).astype(f) / f(DV),
        "pair_mean": (p[:, None] // HD == p[None] // HD).astype(f) / f(HD),
        "causal": (p[None] >= p[:, None]).astype(f),
        "two_rows": np.broadcast_to((p < 2)[:, None], (P, P)).astype(f),
        "cos": cos.astype(f), "sin": sin.astype(f), "grow": grow.astype(f), "shrink": shrink.astype(f),
    }
    ends = np.cumsum([v.shape[1] for v in vectors.values()])
    layout = {"weights": {n: w.shape[1:] for n, w in weights.items()},
              "vectors": {n: (int(e) - v.shape[1], int(e)) for (n, v), e in zip(vectors.items(), ends)},
              "n_vectors": int(ends[-1]),
              "consts": {n: c.shape[1:] for n, c in consts.items()},
              }

    nc = bacc.Bacc("TRN2", target_bir_lowering=False, num_devices=1)
    arrays = {}

    def dram(name, arr):
        arrays[name] = arr
        return nc.dram_tensor(name, arr.shape, mb.dt.from_np(arr.dtype), kind="ExternalInput").ap()

    x_in = dram("x_in", np.ascontiguousarray(a["attn_a_x"]))
    ws = {n: dram("w_in_" + n, w) for n, w in weights.items()}
    vs = dram("v_in", np.concatenate(list(vectors.values()), axis=1))
    bias = dram("bias_in", np.ascontiguousarray(a["ffn_bias"]))
    cs = {n: dram("c_in_" + n, c) for n, c in consts.items()}
    out = nc.dram_tensor("out", (B, T, H), mb.dt.float32, kind="ExternalOutput").ap()
    hybrid_block(nc, x_in, ws, vs, bias, cs, out, layout)
    r = run_bass_kernel_spmd(nc, [arrays], core_ids=[0])
    return r.results[0]["out"]
```
